# Optimizing a Trainium2 kernel written in Bass

```python
import numpy as np
import jax
import jax.numpy as jnp

def _softmax(x, axis=-1):
    return jax.nn.softmax(x, axis=axis)

def _gelu(x):
    return jax.nn.gelu(x, approximate=True)

def _silu(x):
    return jax.nn.silu(x)

def _sigmoid(x):
    return jax.nn.sigmoid(x)

def _layernorm(x, axis=-1, eps=1e-05):
    m = jnp.mean(x, axis=axis, keepdims=True)
    v = jnp.var(x, axis=axis, keepdims=True)
    return (x - m) / jnp.sqrt(v + eps)

def _scatter_add(tgt, idx, src, axis=0):
    return tgt.at[idx].add(src)

def _segment_sum(src, seg, n):
    return jax.ops.segment_sum(src, seg, n)
kernel_name = 'mk_decoder_postln_d1_seqx_r4_18b121'

def setup_inputs(seed: int=0):
    np.random.seed(seed)
    _w = jnp.asarray

    def _rec_inputs():
        import jax
        import jax.numpy as jnp
        _rk = jax.random.key(seed)
        x = -0.0002928 + 1 * jax.random.normal(jax.random.fold_in(_rk, 1), (8, 112, 256), jnp.float32)
        _lenS = 112 - jax.random.randint(jax.random.fold_in(_rk, 7), (8,), 0, max(1, 112 // 4) + 1, jnp.int32)
        _lenS2 = 375 - jax.random.randint(jax.random.fold_in(_rk, 8), (8,), 0, max(1, 375 // 4) + 1, jnp.int32)
        _ctx_1024P = jax.random.normal(jax.random.fold_in(_rk, 11), (8, 16, 256), jnp.float32)
        _ctx_1024c = jax.random.dirichlet(jax.random.fold_in(_rk, 511), 0.3 * jnp.ones((16,), jnp.float32), (8, 375))
        _ctx_1024t = jnp.einsum('bsk,bkd->bsd', _ctx_1024c, _ctx_1024P)
        _ctx_1024t = _ctx_1024t * jax.lax.rsqrt(jnp.mean(jnp.square(_ctx_1024t)) + 1e-12) * 0.953939
        ctx_1024 = 4.13588e-05 + 0.999923 * (_ctx_1024t + 0.3 * jax.random.normal(jax.random.fold_in(_rk, 611), (8, 375, 256), jnp.float32))
        _validS = jnp.arange(112)[None, :] < _lenS[:, None]
        _validS2 = jnp.arange(375)[None, :] < _lenS2[:, None]
        _causal = jnp.tril(jnp.ones((112, 112), dtype=bool))
        mask_Bx1x1xS2_ff0 = jnp.where(jnp.ones((8, 1, 1, 375), dtype=bool), 0.0, -1000000000.0).astype(jnp.float32)
        return (x, ctx_1024, mask_Bx1x1xS2_ff0)
    x, ctx_1024, mask_Bx1x1xS2_ff0 = _rec_inputs()

    def _L0_attn_setup():
        import jax, jax.numpy as jnp
        import numpy as np
        import math
        D_MODEL = 256
        EMB = 256
        key = jax.random.key(seed)
        ks = jax.random.split(key, 9)
        s = 1.0 / math.sqrt(EMB)
        x = jax.random.normal(ks[0], (4, 512, EMB), dtype=jnp.float32)
        W1 = jax.random.uniform(ks[1], (EMB, EMB), minval=-s, maxval=s)
        b1 = jax.random.uniform(ks[2], (EMB,), minval=-s, maxval=s)
        W2 = jax.random.uniform(ks[3], (EMB, EMB), minval=-s, maxval=s)
        b2 = jax.random.uniform(ks[4], (EMB,), minval=-s, maxval=s)
        W3 = jax.random.uniform(ks[5], (EMB, EMB), minval=-s, maxval=s)
        b3 = jax.random.uniform(ks[6], (EMB,), minval=-s, maxval=s)
        W4 = jax.random.uniform(ks[7], (EMB, EMB), minval=-s, maxval=s)
        b4 = jax.random.uniform(ks[8], (EMB,), minval=-s, maxval=s)
        return {'x': x, 'W1': W1, 'b1': b1, 'W2': W2, 'b2': b2, 'W3': W3, 'b3': b3, 'W4': W4, 'b4': b4}
    _L0_attn_all = _L0_attn_setup()
    _L0_attn_in = {k: v for k, v in _L0_attn_all.items() if k in ('W1', 'b1', 'W2', 'b2', 'W3', 'b3', 'W4', 'b4')}
    del _L0_attn_all

    def _L0_xattn_setup():
        import jax, jax.numpy as jnp
        import numpy as np
        H = 16
        D = 256
        F = 1024
        LN_EPS = 1e-05

        def _glorot(key, shape):
            fan_in, fan_out = (shape[0], shape[1])
            lim = np.sqrt(6.0 / (fan_in + fan_out))
            return jax.random.uniform(key, shape, jnp.float32, -lim, lim)

        def _split_heads(x):
            b, l, _ = x.shape
            return x.reshape(b, l, H, D // H)

        def _mha(x, ctx, mask, qw, qb, kw, kb, vw, vb):
            q = _split_heads(x @ qw + qb)
            k = _split_heads(ctx @ kw + kb)
            v = _split_heads(ctx @ vw + vb)
            scores = jnp.einsum('bqhd,bkhd->bhqk', q, k) / np.sqrt(D // H).astype(np.float32)
            if mask is not None:
                scores = scores + mask
            probs = jax.nn.softmax(scores, axis=-1)
            out = jnp.einsum('bhqk,bkhd->bqhd', probs, v)
            return out.reshape(x.shape[0], x.shape[1], D)

        def _self_output(h, residual, w, b, g, be):
            h = h @ w + b
            h = h + residual
            mu = jnp.mean(h, axis=-1, keepdims=True)
            var = jnp.mean(jnp.square(h - mu), axis=-1, keepdims=True)
            return (h - mu) * jax.lax.rsqrt(var + LN_EPS) * g + be
        key = jax.random.key(seed)
        ks = jax.random.split(key, 16)
        inp = {'input_tensor': jax.random.normal(ks[0], (4, 256, D), jnp.float32), 'ctx_tensor': jax.random.normal(ks[1], (4, 512, D), jnp.float32), 'ctx_attn_mask': jnp.zeros((4, 1, 1, 512), jnp.float32), 'cq_w': _glorot(ks[2], (D, D)), 'cq_b': jnp.zeros((D,)), 'ck_w': _glorot(ks[3], (D, D)), 'ck_b': jnp.zeros((D,)), 'cv_w': _glorot(ks[4], (D, D)), 'cv_b': jnp.zeros((D,)), 'co_w': _glorot(ks[5], (D, D)), 'co_b': jnp.zeros((D,)), 'co_g': jnp.ones((D,)), 'co_be': jnp.zeros((D,)), 'sq_w': _glorot(ks[6], (D, D)), 'sq_b': jnp.zeros((D,)), 'sk_w': _glorot(ks[7], (D, D)), 'sk_b': jnp.zeros((D,)), 'sv_w': _glorot(ks[8], (D, D)), 'sv_b': jnp.zeros((D,)), 'so_w': _glorot(ks[9], (D, D)), 'so_b': jnp.zeros((D,)), 'so_g': jnp.ones((D,)), 'so_be': jnp.zeros((D,)), 'fi_w': _glorot(ks[10], (D, F)), 'fi_b': jnp.zeros((F,)), 'fo_w': _glorot(ks[11], (F, D)), 'fo_b': jnp.zeros((D,)), 'fo_g': jnp.ones((D,)), 'fo_be': jnp.zeros((D,))}
        return inp
    _L0_xattn_all = _L0_xattn_setup()
    _L0_xattn_in = {k: v for k, v in _L0_xattn_all.items() if k in ('cq_w', 'cq_b', 'ck_w', 'ck_b', 'cv_w', 'cv_b', 'co_w', 'co_b', 'co_g', 'co_be', 'sq_w', 'sq_b', 'sk_w', 'sk_b', 'sv_w', 'sv_b', 'so_w', 'so_b', 'so_g', 'so_be', 'fi_w', 'fi_b', 'fo_w', 'fo_b', 'fo_g', 'fo_be')}
    del _L0_xattn_all

    def _L0_ffn_setup():
        import jax, jax.numpy as jnp
        import numpy as np
        B, S, D, F, E = (1, 256, 256, 1024, 8)
        EPS = 1e-05

        def _sublayer(xs, g, b, W1e, b1e, W2e, b2e):
            mu = jnp.mean(xs, axis=-1, keepdims=True)
            var = jnp.mean(jnp.square(xs - mu), axis=-1, keepdims=True)
            h = (xs - mu) * jax.lax.rsqrt(var + EPS) * g + b
            return xs + jax.nn.relu(h @ W1e.T + b1e) @ W2e.T + b2e
        key = jax.random.key(seed)
        ks = jax.random.split(key, 4)
        x = jax.random.normal(ks[0], (B, S, D), jnp.float32)
        centroids = jax.random.normal(ks[1], (E, D), jnp.float32) * 0.1
        gamma = jnp.ones((E, D), jnp.float32)
        beta = jnp.zeros((E, D), jnp.float32)
        W1 = jax.random.normal(ks[2], (E, F, D), jnp.float32) * 0.02
        b1 = jnp.zeros((E, F), jnp.float32)
        W2 = jax.random.normal(ks[3], (E, D, F), jnp.float32) * 0.02
        b2 = jnp.zeros((E, D), jnp.float32)
        return {'x': x, 'centroids': centroids, 'gamma': gamma, 'beta': beta, 'W1': W1, 'b1': b1, 'W2': W2, 'b2': b2}
    _L0_ffn_all = _L0_ffn_setup()
    _L0_ffn_in = {k: v for k, v in _L0_ffn_all.items() if k in ('centroids', 'gamma', 'beta', 'W1', 'b1', 'W2', 'b2')}
    del _L0_ffn_all
    return {'x': x, 'ctx_1024': ctx_1024, 'mask_Bx1x1xS2_ff0': mask_Bx1x1xS2_ff0, 'L0_attn_W1': _L0_attn_in['W1'], 'L0_attn_b1': _L0_attn_in['b1'], 'L0_attn_W2': _L0_attn_in['W2'], 'L0_attn_b2': _L0_attn_in['b2'], 'L0_attn_W3': _L0_attn_in['W3'], 'L0_attn_b3': _L0_attn_in['b3'], 'L0_attn_W4': _L0_attn_in['W4'], 'L0_attn_b4': _L0_attn_in['b4'], 'L0_xattn_cq_w': _L0_xattn_in['cq_w'], 'L0_xattn_cq_b': _L0_xattn_in['cq_b'], 'L0_xattn_ck_w': _L0_xattn_in['ck_w'], 'L0_xattn_ck_b': _L0_xattn_in['ck_b'], 'L0_xattn_cv_w': _L0_xattn_in['cv_w'], 'L0_xattn_cv_b': _L0_xattn_in['cv_b'], 'L0_xattn_co_w': _L0_xattn_in['co_w'], 'L0_xattn_co_b': _L0_xattn_in['co_b'], 'L0_xattn_co_g': _L0_xattn_in['co_g'], 'L0_xattn_co_be': _L0_xattn_in['co_be'], 'L0_xattn_sq_w': _L0_xattn_in['sq_w'], 'L0_xattn_sq_b': _L0_xattn_in['sq_b'], 'L0_xattn_sk_w': _L0_xattn_in['sk_w'], 'L0_xattn_sk_b': _L0_xattn_in['sk_b'], 'L0_xattn_sv_w': _L0_xattn_in['sv_w'], 'L0_xattn_sv_b': _L0_xattn_in['sv_b'], 'L0_xattn_so_w': _L0_xattn_in['so_w'], 'L0_xattn_so_b': _L0_xattn_in['so_b'], 'L0_xattn_so_g': _L0_xattn_in['so_g'], 'L0_xattn_so_be': _L0_xattn_in['so_be'], 'L0_xattn_fi_w': _L0_xattn_in['fi_w'], 'L0_xattn_fi_b': _L0_xattn_in['fi_b'], 'L0_xattn_fo_w': _L0_xattn_in['fo_w'], 'L0_xattn_fo_b': _L0_xattn_in['fo_b'], 'L0_xattn_fo_g': _L0_xattn_in['fo_g'], 'L0_xattn_fo_be': _L0_xattn_in['fo_be'], 'L0_ffn_centroids': _L0_ffn_in['centroids'], 'L0_ffn_gamma': _L0_ffn_in['gamma'], 'L0_ffn_beta': _L0_ffn_in['beta'], 'L0_ffn_W1': _L0_ffn_in['W1'], 'L0_ffn_b1': _L0_ffn_in['b1'], 'L0_ffn_W2': _L0_ffn_in['W2'], 'L0_ffn_b2': _L0_ffn_in['b2']}

def reference(x, ctx_1024, mask_Bx1x1xS2_ff0, L0_attn_W1, L0_attn_b1, L0_attn_W2, L0_attn_b2, L0_attn_W3, L0_attn_b3, L0_attn_W4, L0_attn_b4, L0_xattn_cq_w, L0_xattn_cq_b, L0_xattn_ck_w, L0_xattn_ck_b, L0_xattn_cv_w, L0_xattn_cv_b, L0_xattn_co_w, L0_xattn_co_b, L0_xattn_co_g, L0_xattn_co_be, L0_xattn_sq_w, L0_xattn_sq_b, L0_xattn_sk_w, L0_xattn_sk_b, L0_xattn_sv_w, L0_xattn_sv_b, L0_xattn_so_w, L0_xattn_so_b, L0_xattn_so_g, L0_xattn_so_be, L0_xattn_fi_w, L0_xattn_fi_b, L0_xattn_fo_w, L0_xattn_fo_b, L0_xattn_fo_g, L0_xattn_fo_be, L0_ffn_centroids, L0_ffn_gamma, L0_ffn_beta, L0_ffn_W1, L0_ffn_b1, L0_ffn_W2, L0_ffn_b2):
    import jax
    import jax.numpy as jnp

    def _L0_attn_ref(x, W1, b1, W2, b2, W3, b3, W4, b4):
        import jax, jax.numpy as jnp
        import numpy as np
        import math
        D_MODEL = 256
        EMB = 256
        Q = x @ W1 + b1
        K = x @ W2 + b2
        V = x @ W3 + b3
        scale = 1.0 / math.sqrt(D_MODEL)
        scores = jnp.einsum('bse,bte->bst', Q, K) * scale
        attn = jax.nn.softmax(scores, axis=-1)
        out = jnp.einsum('bst,bte->bse', attn, V)
        return out @ W4 + b4

    def _L0_xattn_ref(input_tensor, ctx_tensor, ctx_attn_mask, cq_w, cq_b, ck_w, ck_b, cv_w, cv_b, co_w, co_b, co_g, co_be, sq_w, sq_b, sk_w, sk_b, sv_w, sv_b, so_w, so_b, so_g, so_be, fi_w, fi_b, fo_w, fo_b, fo_g, fo_be):
        import jax, jax.numpy as jnp
        import numpy as np
        H = 16
        D = 256
        F = 1024
        LN_EPS = 1e-05

        def _glorot(key, shape):
            fan_in, fan_out = (shape[0], shape[1])
            lim = np.sqrt(6.0 / (fan_in + fan_out))
            return jax.random.uniform(key, shape, jnp.float32, -lim, lim)

        def _split_heads(x):
            b, l, _ = x.shape
            return x.reshape(b, l, H, D // H)

        def _mha(x, ctx, mask, qw, qb, kw, kb, vw, vb):
            q = _split_heads(x @ qw + qb)
            k = _split_heads(ctx @ kw + kb)
            v = _split_heads(ctx @ vw + vb)
            scores = jnp.einsum('bqhd,bkhd->bhqk', q, k) / np.sqrt(D // H).astype(np.float32)
            if mask is not None:
                scores = scores + mask
            probs = jax.nn.softmax(scores, axis=-1)
            out = jnp.einsum('bhqk,bkhd->bqhd', probs, v)
            return out.reshape(x.shape[0], x.shape[1], D)

        def _self_output(h, residual, w, b, g, be):
            h = h @ w + b
            h = h + residual
            mu = jnp.mean(h, axis=-1, keepdims=True)
            var = jnp.mean(jnp.square(h - mu), axis=-1, keepdims=True)
            return (h - mu) * jax.lax.rsqrt(var + LN_EPS) * g + be
        ca = _mha(input_tensor, ctx_tensor, ctx_attn_mask, cq_w, cq_b, ck_w, ck_b, cv_w, cv_b)
        x = _self_output(ca, input_tensor, co_w, co_b, co_g, co_be)
        sa = _mha(x, x, None, sq_w, sq_b, sk_w, sk_b, sv_w, sv_b)
        x = _self_output(sa, x, so_w, so_b, so_g, so_be)
        inter = jax.nn.gelu(x @ fi_w + fi_b, approximate=False)
        x = _self_output(inter, x, fo_w, fo_b, fo_g, fo_be)
        return x

    def _L0_ffn_ref(x, centroids, gamma, beta, W1, b1, W2, b2):
        import jax, jax.numpy as jnp
        import numpy as np
        B, S, D, F, E = (1, 256, 256, 1024, 8)
        EPS = 1e-05

        def _sublayer(xs, g, b, W1e, b1e, W2e, b2e):
            mu = jnp.mean(xs, axis=-1, keepdims=True)
            var = jnp.mean(jnp.square(xs - mu), axis=-1, keepdims=True)
            h = (xs - mu) * jax.lax.rsqrt(var + EPS) * g + b
            return xs + jax.nn.relu(h @ W1e.T + b1e) @ W2e.T + b2e
        feats = x.reshape(-1, x.shape[-1])
        scores = jax.lax.stop_gradient(feats @ centroids.T)
        expert = jnp.argmax(scores, axis=1)
        onehot = jax.nn.one_hot(expert, E, dtype=feats.dtype)
        alpha = jax.nn.sigmoid(jnp.sum(feats * centroids[expert], axis=-1, keepdims=True))
        ys = jax.vmap(_sublayer, in_axes=(None, 0, 0, 0, 0, 0, 0))(feats, gamma, beta, W1, b1, W2, b2)
        y = jnp.einsum('te,etd->td', onehot, ys)
        out = alpha * y + (1.0 - alpha) * feats
        return out.reshape(x.shape)
    x = _layernorm(x + _L0_attn_ref(x, L0_attn_W1, L0_attn_b1, L0_attn_W2, L0_attn_b2, L0_attn_W3, L0_attn_b3, L0_attn_W4, L0_attn_b4), axis=-1)
    x = _layernorm(x + _L0_xattn_ref(x, ctx_1024, mask_Bx1x1xS2_ff0, L0_xattn_cq_w, L0_xattn_cq_b, L0_xattn_ck_w, L0_xattn_ck_b, L0_xattn_cv_w, L0_xattn_cv_b, L0_xattn_co_w, L0_xattn_co_b, L0_xattn_co_g, L0_xattn_co_be, L0_xattn_sq_w, L0_xattn_sq_b, L0_xattn_sk_w, L0_xattn_sk_b, L0_xattn_sv_w, L0_xattn_sv_b, L0_xattn_so_w, L0_xattn_so_b, L0_xattn_so_g, L0_xattn_so_be, L0_xattn_fi_w, L0_xattn_fi_b, L0_xattn_fo_w, L0_xattn_fo_b, L0_xattn_fo_g, L0_xattn_fo_be), axis=-1)
    x = _layernorm(x + _L0_ffn_ref(x, L0_ffn_centroids, L0_ffn_gamma, L0_ffn_beta, L0_ffn_W1, L0_ffn_b1, L0_ffn_W2, L0_ffn_b2), axis=-1)
    return x

_drawn_inputs = setup_inputs


def setup_inputs(seed=0):
    import zlib

    import numpy as np

    out = dict(_drawn_inputs(seed))
    spreads = {'L0_xattn_cq_b': (0.0, 0.423),
     'L0_xattn_ck_b': (0.0, 0.8),
     'L0_xattn_cv_b': (0.0, 0.1),
     'L0_xattn_co_b': (0.0, 0.1),
     'L0_xattn_co_g': (1.0, 0.2),
     'L0_xattn_co_be': (0.0, 0.1),
     'L0_xattn_sq_b': (0.0, 0.769),
     'L0_xattn_sk_b': (0.0, 0.8),
     'L0_xattn_sv_b': (0.0, 0.1),
     'L0_xattn_so_b': (0.0, 0.1),
     'L0_xattn_so_g': (1.0, 0.2),
     'L0_xattn_so_be': (0.0, 0.1),
     'L0_xattn_fi_b': (0.0, 0.1),
     'L0_xattn_fo_b': (0.0, 0.1),
     'L0_xattn_fo_g': (1.0, 0.2),
     'L0_xattn_fo_be': (0.0, 0.1),
     'L0_ffn_gamma': (1.0, 0.6),
     'L0_ffn_beta': (0.0, 0.8),
     'L0_ffn_b1': (0.0, 0.401),
     'L0_ffn_b2': (0.0, 0.1)}
    factors = {'L0_attn_W1': 3.411, 'L0_attn_b1': 8.0, 'L0_attn_W2': 3.517, 'L0_attn_b2': 8.0}
    for name, (base, spread) in spreads.items():
        noise = np.random.default_rng([zlib.crc32(name.encode()), seed]).standard_normal(out[name].shape)
        drawn = base * np.exp(spread * noise) if base else spread * noise
        out[name] = jnp.asarray(drawn.astype(out[name].dtype))
    for name, factor in factors.items():
        out[name] = (out[name] * factor).astype(out[name].dtype)
    return out
```

```python
import numpy as np
import concourse.bass as bass
from concourse import mybir
from contextlib import ExitStack

F32 = mybir.dt.float32
I32 = mybir.dt.int32
U32 = mybir.dt.uint32
ALU = mybir.AluOpType
ACT = mybir.ActivationFunctionType
AX = mybir.AxisListType

B, S, D, KX = 8, 112, 256, 375
H, HD = 16, 16
F, E = 1024, 8
U = 4
TURNS = B // U
N = U * S
C = D // 128
FC = F // 128
KP, KC = 125, 3
HG = 4
NG = H // HG
HB = 128 // HD
VW = D + HD
TILES = (B * S) // 128 + E - 1
EPS = 1e-5

COLS = dict(b1=0, b2=2, b3=4, cqb=6, ckb=8, cvb=10, sqb=12, skb=14, svb=16, fib=18, cog=26, cobe=28,
            sog=30, sobe=32, gamma=34, beta=50, moeb1=66, cent=130)
NCOLS = 146
ROWS = ["b4", "cob", "cog", "cobe", "sob", "sog", "sobe", "fob", "fog", "fobe"]
WEIGHTS = ["W1", "W2", "W3", "W4", "cq", "ck", "cv", "co", "sq", "sk", "sv", "so"]


def steps():
    s = [("aqk", 0)] + [("av", u) for u in range(U)] + [("as", u) for u in range(U)] + [("ckv", 0)]
    s += [("at", u) for u in range(U)] + [("apv", u) for u in range(U)]
    for t in range(U + 2):
        s += [(k, t - lag) for k, lag in (("ay", 0), ("ab", 1), ("ax", 2)) if 0 <= t - lag < U]
        if t == U - 1:
            s += [("ckv", 1)]
    for kind in "cs":
        s += [("cq", 0)] if kind == "c" else [("sqk", 0)] + [("sv", u) for u in range(U)]
        s += [(kind + "qb", 0), (kind + "qb", 1)]
        for t in range(NG * U + 8):
            if t < NG * U:
                s += [(kind + "s", t)]
            if 0 <= t - 1 < NG * U:
                s += [(kind + "t", t - 1)]
            if 0 <= t - 2 < NG * U:
                s += [(kind + "pv", t - 2)]
            if t % NG in (1, 2) and 0 <= t < NG * (U - 1):
                s += [(kind + "qb", 2 * (t // NG + 1) + t % NG - 1)]
            for stage, lag in (("ob", 5), ("ot", 6), ("y", 7), ("b", 8), ("x", 9)):
                if t >= lag and (t - lag) % NG == 0 and (t - lag) // NG < U:
                    s += [(kind + stage, (t - lag) // NG)]
                    if kind == "c" and stage == "ot" and (t - lag) // NG + 2 < U:
                        s += [("ckv", (t - lag) // NG + 2)]
    s += [("f1", f) for f in range(FC)]
    for t in range(U + 4):
        s += [(k, t - lag) for k, lag in (("f2", 0), ("zf", 1), ("zb", 2), ("zx", 3), ("sc", 4)) if 0 <= t - lag < U]
    return s


STEPS = steps()
OUT_SLOTS = dict(aqk=2 * C, av=1, apv=1, ay=1, ax=1, ckv=C + KC, cq=C, cpv=1, cob=1, cot=1, cy=1, cx=1,
                 sqk=2 * C, sv=1, spv=1, sob=1, sot=1, sy=1, sx=1, f2=1, zx=1, sc=1)
SCORE_SLOTS = {"as": 1, "cs": HG, "ss": 1, "f1": 1}
PT_SLOTS = {"at": 1, "ct": KC, "st": 1}
RESID = dict(ay=0, cy=1, sy=2, f2=3)
NORMS = ("ay", "cy", "sy", "f2", "zf")


def number(slots):
    at, first = 0, {}
    for stage in STEPS:
        if stage[0] in slots:
            first[stage] = at
            at += slots[stage[0]]
    return first, at


OUT, N_OUT = number(OUT_SLOTS)
SCORE, N_SCORE = number(SCORE_SLOTS)
PT, N_PT = number(PT_SLOTS)
NORM, N_NORM = number(dict.fromkeys(NORMS, 1))


def decoder_layer(nc, xT, xrow, ctxT, mask, weights, fi, fo, cols, rows, b2rows, moe, x_slots, y_slots, out):
    ctx = ExitStack()
    with ctx:
        def sb(name, shape, dt=F32):
            return ctx.enter_context(nc.sbuf_tensor(name, shape, dt))

        def sem(name):
            return ctx.enter_context(nc.semaphore(name))

        MOE_WORDS = E * 2 * C * F
        arena = sb("arena", [128, 45760])
        top = [0]

        def take(words):
            top[0] += words
            assert top[0] <= 45760, top
            return arena[:, top[0] - words:top[0]]

        w_all = take(len(WEIGHTS) * C * D).rearrange("p (w c n) -> p w c n", w=len(WEIGHTS), c=C)
        W = {name: w_all[:, i] for i, name in enumerate(WEIGHTS)}
        keysT = take(2 * C * KX).rearrange("p (r c k) -> p r c k", r=2, c=C)
        context = take(2 * C * KX).rearrange("p (r c k) -> p r c k", r=2, c=C)
        values = take(2 * KC * VW).rearrange("p (r k v) -> p r k v", r=2, k=KC)
        masks = take(2 * KX).rearrange("p (r k) -> p r k", r=2)
        qheads = take(2 * C * HB * S).rearrange("p (r c h s) -> p r c h s", r=2, c=C, h=HB)
        probs = take(2 * HG * KX).rearrange("p (r k) -> p r k", r=2 * HG)
        probsT = take(2 * KC * HG * S).rearrange("p (r k n) -> p r k n", r=2, k=KC)
        headsT = take(2 * NG * S).rearrange("p (r g s) -> p r g s", r=2, g=NG)
        heads = take(2 * D).rearrange("p (r d) -> p r d", r=2)
        vrows = take(U * VW).rearrange("p (u v) -> p u v", u=U)
        QT = take(C * N).rearrange("p (c n) -> p c n", c=C)
        KT = take(C * N).rearrange("p (c n) -> p c n", c=C)
        OT = take(C * N).rearrange("p (c n) -> p c n", c=C)
        T = [take(C * N).rearrange("p (c n) -> p c n", c=C) for _ in range(2)]
        resid = take(U * D).rearrange("p (u d) -> p u d", u=U)
        x1 = take(U * D).rearrange("p (u d) -> p u d", u=U)
        ybuf = take(4 * D).rearrange("p (r d) -> p r d", r=4)
        hiddenT = take(FC * N).rearrange("p (f n) -> p f n", f=FC)
        fi_sb = take(C * F).rearrange("p (c f) -> p c f", c=C)
        fo_sb = take(FC * D).rearrange("p (f d) -> p f d", f=FC)
        spread = take(len(ROWS) * D).rearrange("p (r d) -> p r d", r=len(ROWS))
        R = {name: spread[0:S, i] for i, name in enumerate(ROWS)}

        moe_w = arena[:, 0:MOE_WORDS].rearrange("p (e w) -> p e w", e=E)
        late = [MOE_WORDS]

        def take_late(words):
            late[0] += words
            assert late[0] <= 45760
            return arena[:, late[0] - words:late[0]]

        b2_sb = take_late(E * D).rearrange("p (e d) -> p e d", e=E)
        xs = take_late(2 * D).rearrange("p (r d) -> p r d", r=2)
        xsn = take_late(2 * D).rearrange("p (r d) -> p r d", r=2)
        xsT = take_late(2 * C * 128).rearrange("p (r c s) -> p r c s", r=2, c=C)
        hid = take_late(2 * F).rearrange("p (r f) -> p r f", r=2)
        hidT = take_late(2 * F).rearrange("p (r f s) -> p r f s", r=2, f=FC)
        ys = take_late(2 * D).rearrange("p (r d) -> p r d", r=2)
        yg = take_late(B * D).rearrange("p (b d) -> p b d", b=B)

        x5 = sb("x5", [128, B, D])
        scores = sb("scores", [128, B, E])
        consts = sb("consts", [128, NCOLS])
        ident = sb("ident", [128, 128])
        qmask = sb("qmask", [128, HB])
        negmax = sb("negmax", [128, 2, H])
        sums = sb("sums", [128, 2, H])
        recips = sb("recips", [128, 2, H])
        stats = sb("stats", [128, 4, 6])
        meanvar = sb("meanvar", [128, 4, 2])
        vareps = sb("vareps", [128, 4, 1])
        rstd = sb("rstd", [128, 4, 1])
        scal = sb("scal", [128, 2])
        lower = sb("lower", [S, S])
        ones = sb("ones", [S, 128])
        rev = sb("rev", [128, B, E])
        thr = sb("thr", [128, E, 6])
        tidx = sb("tidx", [128, TILES, E - 1])
        best = sb("best", [128, B])
        onehot = sb("onehot", [128, B, E])
        rt = sb("rt", [128, B, E])
        before = sb("before", [128, B, E])
        cnt = sb("cnt", [128, E])
        over = sb("over", [128, E, 6])
        ntile = sb("ntile", [128, E])
        ends = sb("ends", [128, E])
        base = sb("base", [128, E])
        slotf = sb("slotf", [128, B])
        token_slot = sb("token_slot", [128, B], U32)
        tge = sb("tge", [128, TILES, E - 1])
        tilef = sb("tilef", [128, TILES])
        tile_expert = sb("tile_expert", [128, TILES], I32)
        zero = sb("zero", [128, D])
        alpha = sb("alpha", [128, B])
        ex = sb("ex", [128, B])

        bank = [ctx.enter_context(nc.psum_tensor(f"bank{i}", [128, 512], F32)) for i in range(8)]
        score_bank, pt_bank, out_bank = bank[0:3], bank[3:6], bank[6:8]

        def col(name, i=0, p=128):
            return consts[0:p, COLS[name] + i:COLS[name] + i + 1]

        w_first, w_rest, w_ffn = sem("w_first"), sem("w_rest"), sem("w_ffn")
        consts_in, rows_in = sem("consts_in"), sem("rows_in")
        setup, setup_dve, pool_setup, setup_pool = sem("setup"), sem("setup_dve"), sem("pool_setup"), sem("setup_pool")
        turn_over, turn_go = sem("turn_over"), sem("turn_go")
        turn_sems = {n: sem(n) for n in (
            "x_in", "ctx_in0", "ctx_in1", "mask_in0", "mask_in1",
            "out_full", "out_free", "score_full", "hidden_ready", "scores_masked", "pt_full", "pt_free",
            "negmax_ready", "probs_ready", "probs_normed", "qheads_ready", "stats_ready", "rstd_ready",
            "norm_done", "resid_ready", "x1_biased", "dve_chain", "pool_chain", "x5_kept", "vareps_ready")}
        (x_in, ctx_in0, ctx_in1, mask_in0, mask_in1, out_full, out_free, score_full, hidden_ready,
         scores_masked, pt_full, pt_free, negmax_ready, probs_ready, probs_normed, qheads_ready, stats_ready,
         rstd_ready, norm_done, resid_ready, x1_biased, dve_chain, pool_chain, x5_kept, vareps_ready) = turn_sems.values()
        ctx_in, mask_in = (ctx_in0, ctx_in1), (mask_in0, mask_in1)
        (zero_in, e_chain, picked, exped, alphaed, ranked, routed, scattered, moe_in0, moe_b2_in, tile_in0, tile_in1,
         t_stats, t_rstd, t_normed, t_xT_full, t_xT_ready, t_hid_full, t_hid_copied, t_hidT_full, t_hidT_ready,
         t_y_full, t_y_ready, y_out0, y_out1, gathered, f_stats, f_rstd, f_done, out_sent, x5_doubled) = [sem(n) for n in (
            "zero_in e_chain picked exped alphaed ranked routed scattered moe_in0 moe_b2_in tile_in0 tile_in1 "
            "t_stats t_rstd t_normed t_xT_full t_xT_ready t_hid_full t_hid_copied t_hidT_full t_hidT_ready "
            "t_y_full t_y_ready y_out0 y_out1 gathered f_stats f_rstd f_done out_sent x5_doubled").split()]
        moe_in = [moe_in0] + [sem(f"moe_in{e}") for e in range(1, E)]
        tile_in, y_out = (tile_in0, tile_in1), (y_out0, y_out1)

        block = ctx.enter_context(nc.Block())

        score_release = []
        for stage, i in STEPS:
            for j in range(SCORE_SLOTS.get(stage, 0)):
                score_release.append({"as": (probs_ready, i + 1), "cs": (scores_masked, HG * i + j + 1),
                                      "ss": (probs_ready, U + H * U + HG * (i + 1)), "f1": (hidden_ready, i + 1)}[stage])

        def tokens(u):
            return slice(u * S, (u + 1) * S)

        def group(n):
            u, g = divmod(n, NG)
            return u, g, g * HG // HB, (g * HG) % HB

        @block.sync
        def _(sp):
            sp.dma_start(w_all[:, 0:3], weights[:, 0:3]).then_inc(w_first, 16)
            sp.dma_start(consts[:, :], cols).then_inc(consts_in, 16)
            with sp.Fori(0, TURNS) as turn:
                sp.dma_start(T[0], xT[bass.ds(turn, 1)].rearrange("t p c n -> (t p) c n")).then_inc(x_in, 16)
                sp.dma_start(resid[0:S], xrow[bass.ds(turn, 1)].rearrange("t s u d -> (t s) u d")).then_inc(x_in, 16)
                for u in range(U):
                    if u >= 2:
                        sp.wait_ge(out_full, OUT["ckv", u - 2] + OUT_SLOTS["ckv"])
                    sp.dma_start(context[:, u % 2], ctxT[bass.ds(turn * U + u, 1)].rearrange("b p c k -> (b p) c k"))\
                      .then_inc(ctx_in[u % 2], 16)
                    if u >= 2:
                        sp.wait_ge(scores_masked, H * (u - 1))
                    sp.dma_start(masks[0:S, u % 2], mask[bass.ds(turn * U + u, 1), :].to_broadcast([S, KX])).then_inc(mask_in[u % 2], 16)
                sp.wait_ge(turn_over, 4)
                sp.sem_clear(turn_over)
                for s in turn_sems.values():
                    sp.sem_clear(s)
                sp.sem_inc(turn_go, 1)
            sp.dma_start(b2_sb.rearrange("p e d -> p (e d)"), b2rows.to_broadcast([128, E * D])).then_inc(moe_b2_in, 16)
            for e in range(E):
                sp.dma_start(moe_w[:, e], moe[e]).then_inc(moe_in[e], 16)
            sp.wait_ge(scattered, 16 * B)
            for t in range(TILES + 4):
                if t < TILES:
                    if t >= 2:
                        sp.wait_ge(t_normed, t - 1)
                    sp.dma_start(xs[:, t % 2], x_slots[t * 128:(t + 1) * 128, :]).then_inc(tile_in[t % 2], 16)
                j = t - 4
                if j >= 0:
                    sp.wait_ge(t_y_ready, j + 1)
                    sp.dma_start(y_slots[j * 128:(j + 1) * 128, :], ys[:, j % 2]).then_inc(y_out[j % 2], 16)
            for b in range(B):
                sp.wait_ge(f_done, b + 1)
                sp.dma_start(out[b], yg[0:S, b]).then_inc(out_sent, 16)
            sp.wait_ge(out_sent, 16 * B)

        def end_turn(eng, turn):
            eng.sem_inc(turn_over, 1)
            eng.wait_ge(turn_go, turn + 1)

        @block.tensor
        def _(pe):
            mm = nc.tensor.matmul

            def out_slot(n):
                if n >= 2:
                    pe.wait_ge(out_free, n - 1)
                return out_bank[n % 2]

            def score_slot(n):
                if n >= 3:
                    pe.wait_ge(*score_release[n - 3])
                return score_bank[n % 3]

            def pt_slot(n):
                if n >= 3:
                    pe.wait_ge(pt_free, n - 2)
                return pt_bank[n % 3]

            def project_T(slot, w, m, src, n=N):
                dst = out_slot(slot)
                for k in range(C):
                    last = mm(dst[:, 0:n], w[:, k, m * 128:(m + 1) * 128], src[:, k], start=k == 0, stop=k == C - 1)
                last.then_inc(out_full, 1)

            def project_rows(slot, src, w, rows=S):
                dst = out_slot(slot)
                for k in range(C):
                    last = mm(dst[0:rows, 0:D], src(k), w[:, k], start=k == 0, stop=k == C - 1)
                last.then_inc(out_full, 1)

            pe.wait_ge(setup, 1)
            with pe.Fori(0, TURNS) as turn:
                for stage, i in STEPS:
                    slot = OUT.get((stage, i))
                    if stage == "aqk":
                        pe.wait_ge(w_first, 16)
                        pe.wait_ge(x_in, 32)
                        for q, w in enumerate(("W1", "W2")):
                            for m in range(C):
                                project_T(slot + q * C + m, W[w], m, T[0])
                    elif stage == "av":
                        project_rows(slot, lambda k: T[0][:, k, tokens(i)], W["W3"])
                    elif stage == "as":
                        if i == 0:
                            pe.wait_ge(out_free, OUT["aqk", 0] + 2 * C)
                        dst = score_slot(SCORE[stage, i])
                        for k in range(C):
                            last = mm(dst[0:S, 0:S], QT[:, k, tokens(i)], KT[:, k, tokens(i)], start=k == 0, stop=k == C - 1)
                        last.then_inc(score_full, 1)
                    elif stage == "at":
                        dst = pt_slot(PT[stage, i])
                        pe.wait_ge(probs_normed, i + 1)
                        nc.tensor.transpose(dst[0:S, 0:S], probs[0:S, i, 0:S], ident[0:S, 0:S]).then_inc(pt_full, 1)
                    elif stage == "apv":
                        dst = out_slot(slot)
                        pe.wait_ge(pt_free, PT["at", i] + 1)
                        pe.wait_ge(out_free, OUT["av", i] + 1)
                        for m in range(C):
                            last = mm(dst[:, m * S:(m + 1) * S], vrows[0:S, i, m * 128:(m + 1) * 128],
                                      probsT[0:S, i % 2, i // 2, 0:S], start=True, stop=True)
                        last.then_inc(out_full, 1)
                    elif stage in ("ay", "cy", "sy"):
                        if stage == "ay" and i == 0:
                            pe.wait_ge(w_rest, 16)
                        of = {"ay": "apv", "cy": "cot", "sy": "sot"}[stage]
                        pe.wait_ge(out_free, OUT[of, i] + 1)
                        project_rows(slot, lambda k: OT[:, k, tokens(i)], W[{"ay": "W4", "cy": "co", "sy": "so"}[stage]])
                    elif stage in ("ax", "cx", "sx", "zx"):
                        k = NORM[{"ax": "ay", "cx": "cy", "sx": "sy", "zx": "zf"}[stage], i]
                        pe.wait_ge(norm_done, k + 1)
                        src = x1[0:S, i] if stage in ("ax", "zx") else ybuf[0:S, k % 4]
                        dst = out_slot(slot)
                        for m in range(C):
                            last = nc.tensor.transpose(dst[:, m * S:(m + 1) * S], src[:, m * 128:(m + 1) * 128], ident[0:S, 0:S])
                        last.then_inc(out_full, 1)
                    elif stage == "ckv":
                        if i == 0:
                            pe.wait_ge(w_rest, 16)
                        pe.wait_ge(ctx_in[i % 2], 16 * (i // 2 + 1))
                        for m in range(C):
                            project_T(slot + m, W["ck"], m, context[:, i % 2], KX)
                        for c in range(KC):
                            project_rows(slot + C + c, lambda k: context[:, i % 2, k, c * KP:(c + 1) * KP], W["cv"], KP)
                    elif stage == "cq":
                        pe.wait_ge(out_free, OUT["ax", U - 1] + 1)
                        for m in range(C):
                            project_T(slot + m, W["cq"], m, T[1])
                    elif stage == "sqk":
                        pe.wait_ge(out_free, OUT["cx", U - 1] + 1)
                        for q, w in enumerate(("sq", "sk")):
                            for m in range(C):
                                project_T(slot + q * C + m, W[w], m, T[0])
                    elif stage == "sv":
                        project_rows(slot, lambda k: T[0][:, k, tokens(i)], W["sv"])
                    elif stage == "cs":
                        u, g, m, h = group(i)
                        pe.wait_ge(qheads_ready, 2 * u + m + 1)
                        pe.wait_ge(out_free, OUT["ckv", u] + C)
                        for j in range(HG):
                            dst = score_slot(SCORE[stage, i] + j)
                            mm(dst[0:S, 0:KX], qheads[:, u % 2, m, h + j], keysT[:, u % 2, m], start=True, stop=True)\
                                .then_inc(score_full, 1)
                    elif stage == "ss":
                        u, g, m, h = group(i)
                        pe.wait_ge(qheads_ready, 2 * U + 2 * u + m + 1)
                        dst = score_slot(SCORE[stage, i])
                        for j in range(HG):
                            last = mm(dst[0:S, j * S:(j + 1) * S], qheads[:, u % 2, m, h + j], KT[:, m, tokens(u)],
                                      start=True, stop=True)
                        last.then_inc(score_full, 1)
                    elif stage in ("ct", "st"):
                        n = i + (NG * U if stage == "st" else 0)
                        kc, kp = (KC, KP) if stage == "ct" else (1, S)
                        for c in range(kc):
                            dst = pt_slot(PT[stage, i] + c)
                            if c == 0:
                                pe.wait_ge(probs_ready, U + HG * (n + 1))
                            for j in range(HG):
                                last = nc.tensor.transpose(dst[0:kp, j * S:(j + 1) * S],
                                                           probs[0:S, (n % 2) * HG + j, c * kp:(c + 1) * kp], ident[0:S, 0:S])
                            last.then_inc(pt_full, 1)
                    elif stage in ("cpv", "spv"):
                        n = i + (NG * U if stage == "spv" else 0)
                        u, g = divmod(i, NG)
                        kc, kp = (KC, KP) if stage == "cpv" else (1, S)
                        dst = out_slot(slot)
                        pe.wait_ge(pt_free, PT["ct" if stage == "cpv" else "st", i] + kc)
                        pe.wait_ge(out_free, OUT["ckv", u] + C + KC if stage == "cpv" else OUT["sv", u] + 1)
                        for c in range(kc):
                            for j in range(HG):
                                v = values[0:kp, u % 2, c] if stage == "cpv" else vrows[0:kp, u]
                                at = (g * HG + j) * HD
                                last = mm(dst[32 * j:32 * j + 32, 0:S], v[:, at:at + 32],
                                          probsT[0:kp, n % 2, c, j * S:(j + 1) * S], start=c == 0, stop=c == kc - 1)
                        last.then_inc(out_full, 1)
                    elif stage in ("cob", "sob"):
                        pe.wait_ge(out_free, OUT[stage[0] + "pv", NG * i + NG - 1] + 1)
                        dst = out_slot(slot)
                        for g in range(NG):
                            last = nc.tensor.transpose(dst[0:S, g * 128:(g + 1) * 128], headsT[:, i % 2, g], ident[:, :])
                        last.then_inc(out_full, 1)
                    elif stage in ("cot", "sot"):
                        pe.wait_ge(out_free, OUT[stage[0] + "ob", i] + 1)
                        dst = out_slot(slot)
                        for m in range(C):
                            last = nc.tensor.transpose(dst[:, m * S:(m + 1) * S], heads[0:S, i % 2, m * 128:(m + 1) * 128], ident[0:S, 0:S])
                        last.then_inc(out_full, 1)
                    elif stage == "f1":
                        if i == 0:
                            pe.wait_ge(w_ffn, 32)
                            pe.wait_ge(out_free, OUT["sx", U - 1] + 1)
                        dst = score_slot(SCORE[stage, i])
                        for k in range(C):
                            last = mm(dst[:, 0:N], fi_sb[:, k, i * 128:(i + 1) * 128], T[1][:, k], start=k == 0, stop=k == C - 1)
                        last.then_inc(score_full, 1)
                    elif stage == "f2":
                        if i == 0:
                            pe.wait_ge(hidden_ready, FC)
                        dst = out_slot(slot)
                        for f in range(FC):
                            last = mm(dst[0:S, 0:D], hiddenT[:, f, tokens(i)], fo_sb[:, f], start=f == 0, stop=f == FC - 1)
                        last.then_inc(out_full, 1)
                    elif stage == "sc":
                        pe.wait_ge(out_free, OUT["zx", i] + 1)
                        dst = out_slot(slot)
                        for k in range(C):
                            last = mm(dst[0:S, 0:E], T[0][:, k, tokens(i)], consts[:, COLS["cent"] + k * E:COLS["cent"] + (k + 1) * E],
                                      start=k == 0, stop=k == C - 1)
                        last.then_inc(out_full, 1)
                end_turn(pe, turn)

            pe.wait_ge(picked, 1)
            mm(bank[4][0:S, 0:B * E], lower[:, :], onehot[0:S].rearrange("p b e -> p (b e)"), start=True, stop=True)
            mm(bank[5][:, 0:B * E], ones[:, :], onehot[0:S].rearrange("p b e -> p (b e)"), start=True, stop=True).then_inc(ranked, 1)
            pe.wait_ge(routed, 1)
            expert = {}

            for t in range(-1, TILES + 2):
                j = t + 1
                if j < TILES:
                    pe.wait_ge(t_normed, j + 1)
                    if j >= 1:
                        pe.wait_ge(t_xT_ready, j)
                    for c in range(C):
                        last = nc.tensor.transpose(bank[6][:, c * 128:(c + 1) * 128], xsn[:, j % 2, c * 128:(c + 1) * 128], ident[:, :])
                    last.then_inc(t_xT_full, 1)
                j = t
                if 0 <= j < TILES:
                    expert[j] = pe.value_load(tile_expert[0:1, j:j + 1], min_val=0, max_val=E - 1)
                    pe.wait_ge(moe_in[min(j, E - 1)], 16)
                    pe.wait_ge(t_xT_ready, j + 1)
                    if j >= 2:
                        pe.wait_ge(t_hid_copied, 2 * (j - 1))
                    w1 = moe_w[:, bass.ds(expert[j], 1), 0:C * F].rearrange("p e (c f) -> p (e c) f", c=C)
                    for half in range(2):
                        for c in range(C):
                            last = mm(bank[2 * (j % 2) + half][:, :], xsT[:, j % 2, c], w1[:, c, half * 512:(half + 1) * 512],
                                      start=c == 0, stop=c == C - 1)
                        last.then_inc(t_hid_full, 1)
                j = t - 1
                if 0 <= j < TILES:
                    pe.wait_ge(t_hid_copied, 2 * (j + 1))
                    for half in range(2):
                        if j >= 1:
                            pe.wait_ge(t_hidT_ready, 2 * (j - 1) + half + 1)
                        for f in range(4):
                            last = nc.tensor.transpose(bank[4 + half][:, f * 128:(f + 1) * 128],
                                                       hid[:, j % 2, (half * 4 + f) * 128:(half * 4 + f + 1) * 128], ident[:, :])
                        last.then_inc(t_hidT_full, 1)
                j = t - 2
                if 0 <= j < TILES:
                    pe.wait_ge(t_hidT_ready, 2 * (j + 1))
                    if j >= 1:
                        pe.wait_ge(t_y_ready, j)
                    w2 = moe_w[:, bass.ds(expert[j], 1), C * F:].rearrange("p e (f d) -> p (e f) d", f=FC)
                    for f in range(FC):
                        last = mm(bank[7][:, 0:D], hidT[:, j % 2, f], w2[:, f], start=f == 0, stop=f == FC - 1)
                    last.then_inc(t_y_full, 1)

        @block.vector
        def _(dve):
            v = nc.vector
            chain = [0]

            def link(ins):
                chain[0] += 1
                ins.then_inc(dve_chain, 1)

            def linked():
                dve.wait_ge(dve_chain, chain[0])

            dve.wait_ge(setup, 1)
            v.reduce_sum(qmask[:, :], ident[:, :].rearrange("p (h d) -> p h d", d=HD), axis=AX.X).then_inc(setup_dve, 1)
            dve.wait_ge(setup_dve, 1)
            v.tensor_scalar(qmask[:, :], qmask[:, :], 1.0 / HD ** 0.5, None, ALU.mult).then_inc(setup_dve, 1)
            dve.wait_ge(setup, 6)
            dve.wait_ge(consts_in, 16)

            def full(n):
                dve.wait_ge(out_full, n + 1)
                return out_bank[n % 2]

            def norm_front(k):
                linked()
                link(v.bn_stats(stats[0:S, k % 4], ybuf[0:S, k % 4]))
                linked()
                v.bn_aggr(meanvar[0:S, k % 4], stats[0:S, k % 4]).then_inc(stats_ready, 1)

            def open_norm(k):
                if k >= 4:
                    dve.wait_ge(norm_done, k - 3)
                    was = next(s for s, n in NORM.items() if n == k - 4)
                    if was[0] in ("cy", "sy"):
                        dve.wait_ge(out_full, OUT[was[0][0] + "x", was[1]] + 1)
                        dve.wait_ge(resid_ready, (RESID[was[0]] + 1) * U + was[1] + 1)

            with dve.Fori(0, TURNS) as turn:
                chain[0] = 0
                for stage, i in STEPS:
                    slot = OUT.get((stage, i))
                    if stage in ("aqk", "sqk"):
                        for n, (dst, bias, scale) in enumerate(((QT, {"a": "b1", "s": "sqb"}, 1.0 / D ** 0.5),
                                                                (KT, {"a": "b2", "s": "skb"}, 1.0))):
                            for m in range(C):
                                src = full(slot + n * C + m)
                                b = col(bias[stage[0]], m)
                                if stage == "aqk" and n == 0:
                                    v.tensor_scalar(dst[:, m], src[:, 0:N], b, scale, ALU.add, ALU.mult).then_inc(out_free, 1)
                                else:
                                    v.tensor_scalar(dst[:, m], src[:, 0:N], b, None, ALU.add).then_inc(out_free, 1)
                    elif stage in ("av", "sv"):
                        src = full(slot)
                        v.tensor_copy(vrows[0:S, i, 0:D], src[0:S, 0:D]).then_inc(out_free, 1)
                    elif stage == "as":
                        dve.wait_ge(score_full, SCORE[stage, i] + 1)
                        v.tensor_reduce(negmax[0:S, 0, i:i + 1], score_bank[SCORE[stage, i] % 3][0:S, 0:S], AX.X, ALU.max,
                                        negate=True).then_inc(negmax_ready, 1)
                    elif stage == "at":
                        dve.wait_ge(probs_ready, i + 1)
                        link(v.reciprocal(recips[0:S, 0, i:i + 1], sums[0:S, 0, i:i + 1]))
                        linked()
                        v.tensor_scalar(probs[0:S, i, 0:S], probs[0:S, i, 0:S], recips[0:S, 0, i:i + 1], None, ALU.mult)\
                            .then_inc(probs_normed, 1)
                    elif stage in ("apv", "cot", "sot"):
                        src = full(slot)
                        bias = {"apv": "b3", "cot": "cvb", "sot": "svb"}[stage]
                        v.tensor_scalar(OT[:, 0, tokens(i)], src[:, 0:S], col(bias, 0), None, ALU.add)
                        v.tensor_scalar(OT[:, 1, tokens(i)], src[:, S:2 * S], col(bias, 1), None, ALU.add).then_inc(out_free, 1)
                    elif stage in ("ay", "cy", "sy", "f2"):
                        k = NORM[stage, i]
                        open_norm(k)
                        src = full(slot)
                        dve.wait_ge(resid_ready, RESID[stage] * U + i + 1)
                        v.tensor_tensor(ybuf[0:S, k % 4], src[0:S, 0:D], resid[0:S, i], ALU.add).then_inc(out_free, 1)
                        dve.wait_ge(out_free, slot + 1)
                        norm_front(k)
                    elif stage in ("ab", "cb", "sb", "zb"):
                        k = NORM[{"ab": "ay", "cb": "cy", "sb": "sy", "zb": "zf"}[stage], i]
                        dve.wait_ge(rstd_ready, k + 1)
                        dst = x1[0:S, i] if stage in ("ab", "zb") else ybuf[0:S, k % 4]
                        v.tensor_scalar(dst, ybuf[0:S, k % 4], meanvar[0:S, k % 4, 0:1], rstd[0:S, k % 4], ALU.subtract, ALU.mult)\
                            .then_inc(norm_done, 1)
                    elif stage in ("ax", "zx"):
                        src = full(slot)
                        dst = T[1] if stage == "ax" else T[0]
                        v.tensor_copy(dst[:, :, tokens(i)], src[:, 0:2 * S].rearrange("p (c s) -> p c s", c=C)).then_inc(out_free, 1)
                    elif stage in ("cx", "sx"):
                        src = full(slot)
                        dst, gain, shift = (T[0], "cog", "cobe") if stage == "cx" else (T[1], "sog", "sobe")
                        v.tensor_scalar(dst[:, 0, tokens(i)], src[:, 0:S], col(gain, 0), col(shift, 0), ALU.mult, ALU.add)
                        v.tensor_scalar(dst[:, 1, tokens(i)], src[:, S:2 * S], col(gain, 1), col(shift, 1), ALU.mult, ALU.add)\
                            .then_inc(out_free, 1)
                    elif stage == "ckv":
                        for m in range(C):
                            src = full(slot + m)
                            v.tensor_scalar(keysT[:, i % 2, m], src[:, 0:KX], col("ckb", m), None, ALU.add).then_inc(out_free, 1)
                        for c in range(KC):
                            src = full(slot + C + c)
                            v.tensor_copy(values[0:KP, i % 2, c, 0:D], src[0:KP, 0:D]).then_inc(out_free, 1)
                    elif stage == "cq":
                        for m in range(C):
                            src = full(slot + m)
                            v.tensor_scalar(QT[:, m], src[:, 0:N], col("cqb", m), None, ALU.add).then_inc(out_free, 1)
                    elif stage in ("cqb", "sqb"):
                        u, m = divmod(i, C)
                        if i == 0:
                            dve.wait_ge(out_free, OUT["cq" if stage == "cqb" else "sqk", 0] + C)
                        n = i + (0 if stage == "cqb" else C * U)
                        if n >= 2 * C:
                            ub = (u - 2) if u >= 2 else U + u - 2
                            cross = stage == "cqb" or u < 2
                            last_group = NG * ub + (NG - 1 if m else NG // 2 - 1)
                            dve.wait_ge(score_full, SCORE["cs" if cross else "ss", last_group] + (HG if cross else 1))
                        v.tensor_tensor(qheads[:, u % 2, m], QT[:, m:m + 1, tokens(u)].to_broadcast([128, HB, S]),
                                        qmask[:, :].unsqueeze(2).to_broadcast([128, HB, S]), ALU.mult).then_inc(qheads_ready, 1)
                    elif stage == "cs":
                        u, g, m, h = group(i)
                        if g == 0:
                            dve.wait_ge(mask_in[u % 2], 16 * (u // 2 + 1))
                            dve.wait_ge(probs_ready, U + H * (u - 1) if u >= 2 else U)
                        if i >= 2:
                            dve.wait_ge(pt_full, PT["ct", i - 2] + KC)
                        else:
                            dve.wait_ge(pt_full, PT["at", U - 1] + 1)
                        for j in range(HG):
                            s = SCORE[stage, i] + j
                            dve.wait_ge(score_full, s + 1)
                            v.tensor_tensor_reduce(out=probs[0:S, (i % 2) * HG + j], in0=score_bank[s % 3][0:S, 0:KX], in1=masks[0:S, u % 2],
                                                   scale=-1.0, scalar=3.0e38, op0=ALU.add, op1=ALU.min,
                                                   accum_out=negmax[0:S, u % 2, g * HG + j:g * HG + j + 1]).then_inc(scores_masked, 1)
                    elif stage == "ss":
                        u, g, m, h = group(i)
                        if g == 0:
                            dve.wait_ge(probs_ready, U + H * (U + u - 1))
                        s = SCORE[stage, i]
                        dve.wait_ge(score_full, s + 1)
                        v.tensor_reduce(negmax[0:S, u % 2, g * HG:(g + 1) * HG],
                                        score_bank[s % 3][0:S, 0:HG * S].rearrange("p (j s) -> p j s", j=HG), AX.X, ALU.max,
                                        negate=True).then_inc(negmax_ready, 1)
                    elif stage in ("cpv", "spv"):
                        u, g = divmod(i, NG)
                        src = full(slot)
                        v.tensor_copy(headsT[:, u % 2, g], src[:, 0:S]).then_inc(out_free, 1)
                    elif stage in ("cob", "sob"):
                        src = full(slot)
                        dve.wait_ge(probs_ready, U + H * (i + 1) + (H * U if stage == "sob" else 0))
                        link(v.reciprocal(recips[0:S, i % 2], sums[0:S, i % 2]))
                        linked()
                        v.tensor_tensor(heads[0:S, i % 2].rearrange("p (h d) -> p h d", d=HD),
                                        src[0:S, :].rearrange("p (h d) -> p h d", d=2 * HD)[:, :, 0:HD],
                                        recips[0:S, i % 2].unsqueeze(2).to_broadcast([S, H, HD]), ALU.mult).then_inc(out_free, 1)
                    elif stage == "zf":
                        kf, k = NORM["f2", i], NORM["zf", i]
                        dve.wait_ge(rstd_ready, kf + 1)
                        open_norm(k)
                        link(v.scalar_tensor_tensor(ybuf[0:S, kf % 4], ybuf[0:S, kf % 4], meanvar[0:S, kf % 4, 0:1], R["fog"],
                                                    ALU.subtract, ALU.mult))
                        linked()
                        dve.wait_ge(x1_biased, i + 1)
                        v.scalar_tensor_tensor(ybuf[0:S, k % 4], ybuf[0:S, kf % 4], rstd[0:S, kf % 4], x1[0:S, i],
                                               ALU.mult, ALU.add).then_inc(norm_done, 1)
                        dve.wait_ge(norm_done, kf + 1)
                        norm_front(k)
                    elif stage == "sc":
                        src = full(slot)
                        v.tensor_copy(scores[0:S, bass.ds(turn * U + i, 1), :].rearrange("p b e -> p (b e)"), src[0:S, 0:E]).then_inc(out_free, 1)
                dve.wait_ge(out_free, N_OUT)
                end_turn(dve, turn)

            ec = [0]

            def elink(ins):
                ec[0] += 1
                ins.then_inc(e_chain, 1)
                dve.wait_ge(e_chain, ec[0])

            def bc(ap, shape):
                return ap.to_broadcast(shape)

            dve.wait_ge(setup, 12)
            elink(v.tensor_reduce(best[0:S], scores[0:S], AX.X, ALU.max))
            elink(v.tensor_tensor(rt[0:S], scores[0:S], best[0:S].unsqueeze(2).to_broadcast([S, B, E]), ALU.is_equal))
            elink(v.tensor_tensor(rt[0:S], rt[0:S], rev[0:S], ALU.mult))
            elink(v.tensor_reduce(slotf[0:S], rt[0:S], AX.X, ALU.max))
            v.tensor_tensor(onehot[0:S], rt[0:S], slotf[0:S].unsqueeze(2).to_broadcast([S, B, E]), ALU.is_equal).then_inc(picked, 1)
            dve.wait_ge(ranked, 1)
            elink(v.memset(before[:, 0], 0.0))
            tot = bank[5][:, 0:B * E].rearrange("p (b e) -> p b e", b=B)
            for b in range(1, B):
                elink(v.tensor_tensor(before[:, b], before[:, b - 1], tot[:, b - 1], ALU.add))
            elink(v.tensor_tensor(cnt[:, :], before[:, B - 1], tot[:, B - 1], ALU.add))
            elink(v.tensor_tensor(over[:, :, :], cnt[:, :].unsqueeze(2).to_broadcast([128, E, 6]), thr[:, :, :], ALU.is_gt))
            elink(v.reduce_sum(ntile[:, :], over[:, :, :], axis=AX.X))
            elink(v.tensor_scalar(ntile[:, :], ntile[:, :], 1.0, None, ALU.add))
            elink(v.tensor_copy(ends[:, 0:1], ntile[:, 0:1]))
            for e in range(1, E):
                elink(v.tensor_tensor(ends[:, e:e + 1], ends[:, e - 1:e], ntile[:, e:e + 1], ALU.add))
            elink(v.tensor_tensor(base[:, :], ends[:, :], ntile[:, :], ALU.subtract))
            elink(v.tensor_scalar(base[:, :], base[:, :], 128.0, None, ALU.mult))
            elink(v.tensor_tensor(rt[0:S], bank[4][0:S, 0:B * E].rearrange("p (b e) -> p b e", b=B), before[0:S], ALU.add))
            elink(v.tensor_tensor(rt[0:S], rt[0:S], base[0:S].unsqueeze(1).to_broadcast([S, B, E]), ALU.add))
            elink(v.tensor_tensor(rt[0:S], rt[0:S], onehot[0:S], ALU.mult))
            elink(v.reduce_sum(slotf[0:S], rt[0:S], axis=AX.X))
            v.tensor_copy(token_slot[0:S], slotf[0:S]).then_inc(routed, 1)
            dve.wait_ge(routed, 1)
            elink(v.tensor_tensor(tge[:, :, :], tidx[:, :, :], ends[:, 0:E - 1].unsqueeze(1).to_broadcast([128, TILES, E - 1]), ALU.is_ge))
            elink(v.reduce_sum(tilef[:, :], tge[:, :, :], axis=AX.X))
            v.tensor_copy(tile_expert[:, :], tilef[:, :]).then_inc(routed, 1)
            dve.wait_ge(routed, 2)
            dve.wait_ge(exped, 1)
            elink(v.tensor_scalar(ex[0:S], ex[0:S], 1.0, None, ALU.add))
            elink(v.reciprocal(alpha[0:S], ex[0:S]))

            expert = {}

            def load_tile(j):
                dve.wait_ge(tile_in[j % 2], 16 * (j // 2 + 1))
                elink(v.bn_stats(stats[:, j % 4], xs[:, j % 2]))
                v.bn_aggr(meanvar[:, j % 4], stats[:, j % 4]).then_inc(t_stats, 1)
                dve.wait_ge(t_rstd, j + 1)
                v.tensor_scalar(xsn[:, j % 2], xs[:, j % 2], meanvar[:, j % 4, 0:1], rstd[:, j % 4], ALU.subtract, ALU.mult).then_inc(t_normed, 1)

            def gain_tile(j):
                expert[j] = dve.value_load(tile_expert[0:1, j:j + 1], min_val=0, max_val=E - 1)
                dve.wait_ge(t_xT_full, j + 1)
                if j >= 2:
                    dve.wait_ge(t_hid_full, 2 * (j - 1))
                for c in range(C):
                    g = consts[:, bass.ds(expert[j] * C + COLS["gamma"] + c, 1)]
                    b = consts[:, bass.ds(expert[j] * C + COLS["beta"] + c, 1)]
                    last = v.tensor_scalar(xsT[:, j % 2, c], bank[6][:, c * 128:(c + 1) * 128], g, b, ALU.mult, ALU.add)
                last.then_inc(t_xT_ready, 1)

            def relu_tile(j):
                if j >= 2:
                    dve.wait_ge(t_y_full, j - 1)
                for half in range(2):
                    dve.wait_ge(t_hidT_full, 2 * j + half + 1)
                    for f in range(4):
                        b = consts[:, bass.ds(expert[j] * FC + COLS["moeb1"] + half * 4 + f, 1)]
                        last = v.tensor_scalar(hidT[:, j % 2, half * 4 + f], bank[4 + half][:, f * 128:(f + 1) * 128], b, 0.0,
                                               ALU.add, ALU.max)
                    last.then_inc(t_hidT_ready, 1)

            def bias_tile(j):
                if j == 0:
                    dve.wait_ge(moe_b2_in, 16)
                if j >= 2:
                    dve.wait_ge(y_out[j % 2], 16 * (j // 2))
                dve.wait_ge(t_y_full, j + 1)
                v.tensor_tensor(ys[:, j % 2], bank[7][:, 0:D], b2_sb[:, bass.ds(expert[j], 1)].rearrange("p e d -> p (e d)"), ALU.add)\
                    .then_inc(t_y_ready, 1)

            load_tile(0)
            for t in range(-1, TILES + 2):
                if t + 1 < TILES:
                    gain_tile(t + 1)
                if t + 2 < TILES:
                    load_tile(t + 2)
                if 0 <= t - 1 < TILES:
                    relu_tile(t - 1)
                if 0 <= t - 2 < TILES:
                    bias_tile(t - 2)

            dve.wait_ge(x5_doubled, 1)
            dve.wait_ge(gathered, 16 * B)
            for t in range(B + 1):
                if t < B:
                    if t >= 4:
                        dve.wait_ge(f_done, t - 3)
                    elink(v.scalar_tensor_tensor(yg[0:S, t], yg[0:S, t], alpha[0:S, t:t + 1], x5[0:S, t], ALU.mult, ALU.add))
                    elink(v.bn_stats(stats[0:S, t % 4], yg[0:S, t]))
                    v.bn_aggr(meanvar[0:S, t % 4], stats[0:S, t % 4]).then_inc(f_stats, 1)
                if t >= 1:
                    b = t - 1
                    dve.wait_ge(f_rstd, b + 1)
                    v.tensor_scalar(yg[0:S, b], yg[0:S, b], meanvar[0:S, b % 4, 0:1], rstd[0:S, b % 4], ALU.subtract, ALU.mult)\
                        .then_inc(f_done, 1)

        @block.scalar
        def _(act):
            a = nc.scalar
            act.dma_start(w_all[:, 3:], weights[:, 3:]).then_inc(w_rest, 16)
            act.dma_start(spread[0:S].rearrange("p r d -> p (r d)"), rows.to_broadcast([S, len(ROWS) * D])).then_inc(rows_in, 16)
            act.dma_start(fi_sb, fi).then_inc(w_ffn, 16)
            act.dma_start(fo_sb, fo).then_inc(w_ffn, 16)
            act.wait_ge(setup, 1)
            act.wait_ge(consts_in, 16)
            with act.Fori(0, TURNS) as turn:
                for stage, i in STEPS:
                    if stage == "as":
                        act.wait_ge(negmax_ready, i + 1)
                        a.activation(probs[0:S, i, 0:S], score_bank[SCORE[stage, i] % 3][0:S, 0:S], ACT.Exp,
                                     bias=negmax[0:S, 0, i:i + 1], accum_out=sums[0:S, 0, i:i + 1]).then_inc(probs_ready, 1)
                    elif stage == "at":
                        act.wait_ge(pt_full, PT[stage, i] + 1)
                        a.activation(probsT[0:S, i % 2, i // 2, 0:S], pt_bank[PT[stage, i] % 3][0:S, 0:S], ACT.Copy).then_inc(pt_free, 1)
                    elif stage in ("cs", "ss"):
                        u, g, m, h = group(i)
                        if g == 0:
                            if stage == "cs" and u < 2:
                                act.wait_ge(probs_normed, U)
                            else:
                                was = ("cob", u - 2) if stage == "cs" else ("sob", u - 2) if u >= 2 else ("cob", U + u - 2)
                                act.wait_ge(out_free, OUT[was] + 1)
                        if stage == "ss":
                            was = ("st", i - 2) if i >= 2 else ("ct", NG * U + i - 2)
                            act.wait_ge(pt_full, PT[was] + PT_SLOTS[was[0]])
                            act.wait_ge(negmax_ready, U + i + 1)
                        for j in range(HG):
                            p = probs[0:S, (i % 2) * HG + j]
                            if stage == "cs":
                                act.wait_ge(scores_masked, HG * i + j + 1)
                                src, dst, scale = p, p, -1.0
                            else:
                                src, dst, scale = score_bank[SCORE[stage, i] % 3][0:S, j * S:(j + 1) * S], p[:, 0:S], 1.0
                            at = g * HG + j
                            a.activation(dst, src, ACT.Exp, bias=negmax[0:S, u % 2, at:at + 1], scale=scale,
                                         accum_out=sums[0:S, u % 2, at:at + 1]).then_inc(probs_ready, 1)
                    elif stage in ("ct", "st"):
                        kc, kp = (KC, KP) if stage == "ct" else (1, S)
                        n = i + (NG * U if stage == "st" else 0)
                        was = ("apv", U - 1) if n < 2 else (("cpv", n - 2) if n - 2 < NG * U else ("spv", n - 2 - NG * U))
                        act.wait_ge(out_full, OUT[was] + 1)
                        for c in range(kc):
                            act.wait_ge(pt_full, PT[stage, i] + c + 1)
                            a.activation(probsT[0:kp, n % 2, c], pt_bank[(PT[stage, i] + c) % 3][0:kp, 0:HG * S], ACT.Copy)\
                                .then_inc(pt_free, 1)
                    elif stage == "f1":
                        act.wait_ge(score_full, SCORE[stage, i] + 1)
                        a.activation(hiddenT[:, i], score_bank[SCORE[stage, i] % 3][:, 0:N], ACT.Gelu, bias=col("fib", i))\
                            .then_inc(hidden_ready, 1)
                    elif stage == "zb":
                        act.wait_ge(norm_done, NORM["zf", i] + 1)
                        a.activation(x5[0:S, bass.ds(turn * U + i, 1)].rearrange("p b d -> p (b d)"), x1[0:S, i], ACT.Copy)\
                            .then_inc(x5_kept, 1)
                act.wait_ge(x5_kept, U)
                end_turn(act, turn)

            act.wait_ge(picked, 1)
            a.activation(ex[0:S], best[0:S], ACT.Exp, scale=-1.0).then_inc(exped, 1)
            for j in range(TILES):
                if j >= 2:
                    act.wait_ge(t_hidT_full, 2 * (j - 1))
                for half in range(2):
                    act.wait_ge(t_hid_full, 2 * j + half + 1)
                    a.activation(hid[:, j % 2, half * 512:(half + 1) * 512], bank[2 * (j % 2) + half][:, :], ACT.Copy)\
                        .then_inc(t_hid_copied, 1)

        @block.gpsimd
        def _(pool):
            g = nc.gpsimd
            g.memset(ident[:, :], 0.0).then_inc(pool_setup, 1)
            pool.wait_ge(pool_setup, 1)
            g.affine_select(out=ident[:, :], in_=ident[:, :], compare_op=ALU.not_equal, fill=1.0, base=0, pattern=[[-1, 128]],
                            channel_multiplier=1).then_inc(setup, 1)
            g.memset(values[:, 0, :, D:], 0.0).then_inc(setup, 1)
            g.memset(values[:, 1, :, D:], 0.0).then_inc(setup, 1)
            g.memset(vrows[:, :, D:], 0.0).then_inc(setup, 1)
            g.memset(scal[:, 0:1], EPS).then_inc(setup, 1)
            g.memset(scal[:, 1:2], -0.5).then_inc(setup, 1)
            g.memset(zero[:, :], 0.0).then_inc(setup, 1)
            g.memset(lower[:, :], 1.0).then_inc(pool_setup, 1)
            g.memset(ones[:, :], 1.0).then_inc(setup, 1)
            pool.wait_ge(pool_setup, 2)
            g.affine_select(out=lower[:, :], in_=lower[:, :], compare_op=ALU.is_gt, fill=0.0, base=0, pattern=[[1, S]],
                            channel_multiplier=-1).then_inc(setup, 1)
            g.iota(rev[:, :, :], pattern=[[0, B], [-1, E]], base=E, channel_multiplier=0,
                   allow_small_or_imprecise_dtypes=True).then_inc(setup, 1)
            g.iota(thr[:, :, :], pattern=[[0, E], [128, 6]], base=128, channel_multiplier=0,
                   allow_small_or_imprecise_dtypes=True).then_inc(setup, 1)
            g.iota(tidx[:, :, :], pattern=[[1, TILES], [0, E - 1]], base=0, channel_multiplier=0,
                   allow_small_or_imprecise_dtypes=True).then_inc(setup, 1)
            pool.wait_ge(setup, 7)
            for t in range(TILES):
                pool.dma_start(x_slots[t * 128:(t + 1) * 128, :], zero[:, :]).then_inc(zero_in, 16)
            pool.wait_ge(rows_in, 16)
            g.tensor_tensor(R["cobe"], R["cobe"], R["sob"], ALU.add).then_inc(setup_pool, 1)
            g.tensor_tensor(R["sobe"], R["sobe"], R["fob"], ALU.add).then_inc(setup_pool, 1)
            pool.wait_ge(setup_pool, 2)

            def inverse_deviation(k, rows, stats_sem, ready_sem, n):
                pool.wait_ge(stats_sem, n + 1)
                g.tensor_tensor(vareps[0:rows, k % 4], meanvar[0:rows, k % 4, 1:2], scal[0:rows, 0:1], ALU.add).then_inc(vareps_ready, 1)
                vareps_count[0] += 1
                pool.wait_ge(vareps_ready, vareps_count[0])
                g.tensor_tensor(rstd[0:rows, k % 4], vareps[0:rows, k % 4], scal[0:rows, 1:2], ALU.pow).then_inc(ready_sem, 1)

            with pool.Fori(0, TURNS) as turn:
                chain = 0
                vareps_count = [0]
                pool.wait_ge(x_in, 32)
                for u in range(U):
                    g.tensor_tensor(resid[0:S, u], resid[0:S, u], R["b4"], ALU.add).then_inc(resid_ready, 1)
                for stage, i in STEPS:
                    if stage in NORMS:
                        k = NORM[stage, i]
                        if k >= 4:
                            pool.wait_ge(norm_done, k - 3)
                        inverse_deviation(k, S, stats_ready, rstd_ready, k)
                    elif stage == "ab":
                        pool.wait_ge(norm_done, NORM["ay", i] + 1)
                        g.tensor_tensor(resid[0:S, i], x1[0:S, i], R["cob"], ALU.add).then_inc(resid_ready, 1)
                    elif stage == "cqb" and i < U:
                        pool.wait_ge(out_full, OUT["ax", i] + 1)
                        pool.wait_ge(resid_ready, U + i + 1)
                        g.tensor_tensor(x1[0:S, i], x1[0:S, i], R["fobe"], ALU.add).then_inc(x1_biased, 1)
                    elif stage in ("cb", "sb"):
                        k = NORM[stage[0] + "y", i]
                        gain, shift = ("cog", "cobe") if stage == "cb" else ("sog", "sobe")
                        pool.wait_ge(norm_done, k + 1)
                        g.tensor_tensor(resid[0:S, i], ybuf[0:S, k % 4], R[gain], ALU.mult).then_inc(pool_chain, 1)
                        chain += 1
                        pool.wait_ge(pool_chain, chain)
                        g.tensor_tensor(resid[0:S, i], resid[0:S, i], R[shift], ALU.add).then_inc(resid_ready, 1)
                pool.wait_ge(rstd_ready, N_NORM)
                end_turn(pool, turn)

            pool.wait_ge(zero_in, 16 * TILES)
            pool.wait_ge(routed, 1)
            for b in range(B):
                g.indirect_dma_start(out=x_slots, out_offset=bass.IndirectOffsetOnAxis(ap=token_slot[0:S, b:b + 1], axis=0),
                                     in_=x5[0:S, b], in_offset=None, bounds_check=TILES * 128 - 1).then_inc(scattered, 16)
            vareps_count = [0]
            vareps_late = vareps_ready
            for j in range(TILES):
                if j == 4:
                    pool.wait_ge(scattered, 16 * B)
                    g.tensor_tensor(x5[0:S], x5[0:S], x5[0:S], ALU.add).then_inc(x5_doubled, 1)
                inverse_deviation(j, 128, t_stats, t_rstd, j)
            pool.wait_ge(y_out[0], 16 * (TILES // 2))
            pool.wait_ge(y_out[1], 16 * (TILES // 2))
            for b in range(B):
                g.indirect_dma_start(out=yg[0:S, b], out_offset=None, in_=y_slots,
                                     in_offset=bass.IndirectOffsetOnAxis(ap=token_slot[0:S, b:b + 1], axis=0),
                                     bounds_check=TILES * 128 - 1).then_inc(gathered, 16)
            for b in range(B):
                inverse_deviation(b, S, f_stats, f_rstd, b)


def kernel(**inputs):
    import concourse.bacc as bacc
    from concourse.bass_utils import run_bass_kernel_spmd

    a = {n: np.ascontiguousarray(v) for n, v in inputs.items()}
    at, xa, mo = "L0_attn_", "L0_xattn_", "L0_ffn_"

    def chunks(w):
        return w.reshape(-1, 128, w.shape[-1]).transpose(1, 0, 2)

    def columns(v):
        return v.reshape(-1, 128).T

    x = a["x"]
    w = [a[at + n] for n in ("W1", "W2", "W3", "W4")]
    w += [a[xa + n + "_w"] for n in ("cq", "ck", "cv", "co", "sq", "sk", "sv", "so")]
    cols = [a[at + n] for n in ("b1", "b2", "b3")]
    cols += [a[xa + n] for n in ("cq_b", "ck_b", "cv_b", "sq_b", "sk_b", "sv_b", "fi_b", "co_g", "co_be", "so_g", "so_be")]
    cols += [a[mo + n] for n in ("gamma", "beta", "b1")]
    cent = chunks(a[mo + "centroids"].T).reshape(128, -1)
    rows = [a[at + "b4"]] + [a[xa + n] for n in ("co_b", "co_g", "co_be", "so_b", "so_g", "so_be", "fo_b", "fo_g", "fo_be")]
    moe1 = a[mo + "W1"].transpose(0, 2, 1).reshape(E, C, 128, F).transpose(0, 2, 1, 3).reshape(E, 128, C * F)
    moe2 = a[mo + "W2"].transpose(0, 2, 1).reshape(E, FC, 128, D).transpose(0, 2, 1, 3).reshape(E, 128, FC * D)
    arrays = {
        "xT": x.reshape(TURNS, N, C, 128).transpose(0, 3, 2, 1),
        "xrow": x.reshape(TURNS, U, S, D).transpose(0, 2, 1, 3),
        "ctxT": a["ctx_1024"].reshape(B, KX, C, 128).transpose(0, 3, 2, 1),
        "mask": a["mask_Bx1x1xS2_ff0"].reshape(B, KX),
        "weights": np.stack([chunks(m) for m in w], axis=1),
        "fi": chunks(a[xa + "fi_w"]),
        "fo": chunks(a[xa + "fo_w"]),
        "cols": np.concatenate([columns(c) for c in cols] + [cent], axis=1),
        "rows": np.concatenate(rows).reshape(1, -1),
        "b2rows": a[mo + "b2"].reshape(1, E * D),
        "moe": np.concatenate([moe1, moe2], axis=2),
    }
    arrays = {n: np.ascontiguousarray(v) for n, v in arrays.items()}
    nc = bacc.Bacc("TRN2", target_bir_lowering=False, num_devices=1)
    ap = {n: nc.dram_tensor(n, v.shape, mybir.dt.from_np(v.dtype), kind="ExternalInput").ap() for n, v in arrays.items()}
    x_slots = nc.dram_tensor("x_slots", (TILES * 128, D), F32, kind="Internal").ap()
    y_slots = nc.dram_tensor("y_slots", (TILES * 128, D), F32, kind="Internal").ap()
    out = nc.dram_tensor("out", (B, S, D), F32, kind="ExternalOutput").ap()
    decoder_layer(nc, **ap, x_slots=x_slots, y_slots=y_slots, out=out)
    r = run_bass_kernel_spmd(nc, [arrays], core_ids=[0])
    return r.results[0]["out"]
```

```python
import numpy as np
import concourse.bass as bass
from concourse import mybir
from contextlib import ExitStack

F32 = mybir.dt.float32
I32 = mybir.dt.int32
U32 = mybir.dt.uint32
ALU = mybir.AluOpType
ACT = mybir.ActivationFunctionType
AX = mybir.AxisListType

B, S, D, KX = 8, 112, 256, 375
H, HD = 16, 16
F, E = 1024, 8
C = D // 128
FC = F // 128
FU = 4
FN = FU * S
KP, KC = 125, 3
HG = 4
NG = H // HG
GROUPS = B * NG
HB = 128 // HD
VW = D + HD
TILES = (B * S) // 128 + E - 1
NR = 6
EPS = 1e-5

COLS = dict(b1=0, b2=2, b3=4, cqb=6, ckb=8, cvb=10, sqb=12, skb=14, svb=16, fib=18, cog=26, cobe=28,
            sog=30, sobe=32, gamma=34, beta=50, moeb1=66, cent=130)
NCOLS = 146
ROWS = ["b4", "cob", "cog", "cobe", "sob", "sog", "sobe", "fob", "fog", "fobe"]
WEIGHTS = ["W1", "W2", "W3", "W4", "cq", "ck", "cv", "co", "sq", "sk", "sv", "so"]


def steps():
    ticks = {}

    def at(t, stage, i, rank):
        ticks.setdefault(t, []).append((rank, stage, i))

    for u in range(B):
        a = u if u < 4 else 4 * u - 9
        for rank, (stage, lag) in enumerate((("aqk", -9), ("av", -9), ("as", -8), ("at", -7), ("apv", -6), ("ay", -5),
                                             ("ab", -4), ("ax", -3))):
            at(a + lag, stage, u, 10 + rank)
        c = NG * u
        at(-4 if u == 0 else c - 2, "ckv", u, 30)
        for rank, (stage, i, lag) in enumerate((("cq", u, -2), ("cqb", C * u, -1), ("cqb", C * u + 1, 0),
                                                ("cob", u, 6), ("cot", u, 7), ("cy", u, 8), ("cb", u, 9), ("cx", u, 10),
                                                ("sqk", u, 11), ("sv", u, 11), ("sqb", C * u, 12), ("sqb", C * u + 1, 13),
                                                ("sob", u, 19), ("sot", u, 20), ("sy", u, 21), ("sb", u, 22), ("sx", u, 23))):
            at(c + lag, stage, i, 31 + rank)
        for g in range(NG):
            n = c + g
            for rank, (stage, lag) in enumerate((("cs", 0), ("ct", 1), ("ss", 13), ("cpv", 2), ("st", 14), ("spv", 15))):
                at(n + lag, stage, n, rank)
    for half, start in ((0, NG * FU + 21), (1, NG * (B - 1) + 24)):
        for f in range(FC):
            at(start, "f1", half * FC + f, 60 + f)
        for j in range(FU):
            for rank, (stage, lag) in enumerate((("f2", 1), ("zf", 2), ("zb", 3), ("zx", 4), ("sc", 5))):
                at(start + lag + j, stage, half * FU + j, 70 + rank)
    return [(stage, i) for t in sorted(ticks) for _, stage, i in sorted(ticks[t])]


STEPS = steps()
PLACE = {stage: n for n, stage in enumerate(STEPS)}


def number(increments):
    count, before = 0, {}
    for stage in STEPS:
        if stage[0] in increments:
            before[stage] = count
            count += increments[stage[0]]
    return before, count


OUT, N_OUT = number(dict(aqk=2 * C, av=1, apv=1, ay=1, ax=1, ckv=C + KC, cq=C, cpv=1, cob=1, cot=1, cy=1, cx=1,
                         sqk=2 * C, sv=1, spv=1, sob=1, sot=1, sy=1, sx=1, f2=1, zx=1, sc=1))
SCORE, N_SCORE = number({"as": 1, "cs": HG, "ss": 1, "f1": 1})
PT, N_PT = number({"at": 1, "ct": KC, "st": 1})
OPENED, N_NORM = number(dict(ay=1, cy=1, sy=1, f2=1, zf=1))
FINISHED, _ = number(dict(ab=1, cb=1, sb=1, zf=1, zb=1))
FINISHES = dict(ay="ab", cy="cb", sy="sb", f2="zf", zf="zb")
PROBS, _ = number({"as": 1, "cs": HG, "ss": HG})
MASKED, _ = number({"cs": HG})
NEGMAX, _ = number({"as": 1, "ss": 1})
NORMED, _ = number({"at": 1})
SPREAD, _ = number({"cqb": 1, "sqb": 1})
RESID, _ = number(dict(ab=1, cb=1, sb=1))
HIDDEN, _ = number({"f1": 1})
KEPT, _ = number({"cq": 1})


def decoder_layer(nc, xT, xrow, ctxT, mask, weights, fi, fo, cols, rows, b2rows, moe, x_slots, y_slots, out):
    ctx = ExitStack()
    with ctx:
        def sb(name, shape, dt=F32):
            return ctx.enter_context(nc.sbuf_tensor(name, shape, dt))

        def sem(name):
            return ctx.enter_context(nc.semaphore(name))

        MOE_WORDS = E * 2 * C * F
        ARENA = 48800
        arena = sb("arena", [128, ARENA])
        top = [0]

        def take(words):
            top[0] += words
            assert top[0] <= ARENA, top
            return arena[:, top[0] - words:top[0]]

        def ring(words, shape, n=2):
            names, sizes = shape
            return take(n * words).rearrange(f"p (r {' '.join(names)}) -> p r {' '.join(names)}", r=n, **dict(zip(names, sizes)))

        rows_T = (("c", "s"), (C, S))
        wA = take(4 * C * D).rearrange("p (w c n) -> p w c n", w=4, c=C)
        xT_sb = take(B * C * S).rearrange("p (b c s) -> p b c s", b=B, c=C)
        QTa, KTa, OTa = ring(C * S, rows_T), ring(C * S, rows_T), ring(C * S, rows_T)
        va = take(4 * D).rearrange("p (u v) -> p u v", u=4)
        probsA = take(2 * S).rearrange("p (r s) -> p r s", r=2)
        probsTA = take(2 * S).rearrange("p (r s) -> p r s", r=2)
        first_end = top[0]
        wC = take(4 * C * D).rearrange("p (w c n) -> p w c n", w=4, c=C)
        x1T = ring(C * S, rows_T, 4)
        QTc, OTc = ring(C * S, rows_T, 1), ring(C * S, rows_T, 1)
        keysT = take(2 * C * KX).rearrange("p (r c k) -> p r c k", r=2, c=C)
        context = take(2 * C * KX).rearrange("p (r c k) -> p r c k", r=2, c=C)
        values = take(2 * KC * VW).rearrange("p (r k v) -> p r k v", r=2, k=KC)
        masks = take(2 * KX).rearrange("p (r k) -> p r k", r=2)
        qheadsC = take(C * HB * S).rearrange("p (c h s) -> p c h s", c=C, h=HB)
        probsC = take(2 * HG * KX).rearrange("p (r k) -> p r k", r=2 * HG)
        probsTC = take(2 * KC * HG * S).rearrange("p (r k n) -> p r k n", r=2, k=KC)
        headsTC = take(2 * NG * S).rearrange("p (r g s) -> p r g s", r=2, g=NG)
        headsC = take(D)
        cross_end = top[0]
        wS = take(4 * C * D).rearrange("p (w c n) -> p w c n", w=4, c=C)
        x2T = ring(C * S, rows_T)
        QTs, KTs, OTs = ring(C * S, rows_T, 1), ring(C * S, rows_T), ring(C * S, rows_T, 1)
        vrows = take(2 * VW).rearrange("p (u v) -> p u v", u=2)
        qheadsS = take(C * HB * S).rearrange("p (c h s) -> p c h s", c=C, h=HB)
        probsS = take(2 * HG * S).rearrange("p (r k) -> p r k", r=2 * HG)
        probsTS = take(2 * HG * S).rearrange("p (r k n) -> p r k n", r=2, k=1)
        headsTS = take(2 * NG * S).rearrange("p (r g s) -> p r g s", r=2, g=NG)
        headsS = take(D)
        self_end = top[0]
        resid = take(B * D).rearrange("p (u d) -> p u d", u=B)
        ybuf = take(NR * D).rearrange("p (r d) -> p r d", r=NR)
        x3T = take(C * B * S).rearrange("p (c n) -> p c n", c=C)
        x5T = ring(C * S, rows_T)
        hiddenT = take(FC * FN).rearrange("p (f n) -> p f n", f=FC)
        zero = hiddenT[:, 0, 0:D]
        fi_sb = take(C * F).rearrange("p (c f) -> p c f", c=C)
        fo_sb = take(FC * D).rearrange("p (f d) -> p f d", f=FC)
        spread = take(len(ROWS) * D).rearrange("p (r d) -> p r d", r=len(ROWS))
        R = {name: spread[0:S, i] for i, name in enumerate(ROWS)}
        W = {name: (wA, wC, wS)[i // 4][:, i % 4] for i, name in enumerate(WEIGHTS)}

        moe_w = arena[:, 0:MOE_WORDS].rearrange("p (e w) -> p e w", e=E)
        words = MOE_WORDS // E
        assert first_end >= words and cross_end >= 5 * words, (first_end, cross_end, self_end)
        late = [MOE_WORDS]

        def take_late(words):
            late[0] += words
            assert late[0] <= ARENA
            return arena[:, late[0] - words:late[0]]

        b2_sb = take_late(E * D).rearrange("p (e d) -> p e d", e=E)
        xs = take_late(2 * D).rearrange("p (r d) -> p r d", r=2)
        xsn = take_late(2 * D).rearrange("p (r d) -> p r d", r=2)
        xsT = take_late(2 * C * 128).rearrange("p (r c s) -> p r c s", r=2, c=C)
        hid = take_late(2 * F).rearrange("p (r f) -> p r f", r=2)
        hidT = take_late(2 * F).rearrange("p (r f s) -> p r f s", r=2, f=FC)
        ys = take_late(2 * D).rearrange("p (r d) -> p r d", r=2)
        yg = take_late(B * D).rearrange("p (b d) -> p b d", b=B)

        x1 = sb("x1", [128, B, D])
        x5 = x1
        scores = sb("scores", [128, B, E])
        consts = sb("consts", [128, NCOLS])
        ident = sb("ident", [128, 128])
        qmask = sb("qmask", [128, HB])
        negmax = {k: sb("negmax" + k, [128, B, h]) for k, h in (("a", 1), ("c", H), ("s", H))}
        sums = {k: sb("sums" + k, [128, B, h]) for k, h in (("a", 1), ("c", H), ("s", H))}
        recips = {k: sb("recips" + k, [128, B, h]) for k, h in (("a", 1), ("c", H), ("s", H))}
        stats = sb("stats", [128, NR, 6])
        meanvar = sb("meanvar", [128, NR, 2])
        vareps = sb("vareps", [128, NR, 1])
        rstd = sb("rstd", [128, NR, 1])
        scal = sb("scal", [128, 2])
        lower = sb("lower", [S, S])
        ones = sb("ones", [S, 128])
        rev = sb("rev", [128, B, E])
        thr = sb("thr", [128, E, 6])
        tidx = sb("tidx", [128, TILES, E - 1])
        best = sb("best", [128, B])
        onehot = sb("onehot", [128, B, E])
        rt = sb("rt", [128, B, E])
        before = sb("before", [128, B, E])
        cnt = sb("cnt", [128, E])
        over = sb("over", [128, E, 6])
        ntile = sb("ntile", [128, E])
        ends = sb("ends", [128, E])
        base = sb("base", [128, E])
        slotf = sb("slotf", [128, B])
        token_slot = sb("token_slot", [128, B], U32)
        tge = sb("tge", [128, TILES, E - 1])
        tilef = sb("tilef", [128, TILES])
        tile_expert = sb("tile_expert", [128, TILES], I32)
        alpha = sb("alpha", [128, B])
        ex = sb("ex", [128, B])

        bank = [ctx.enter_context(nc.psum_tensor(f"bank{i}", [128, 512], F32)) for i in range(8)]
        score_bank, pt_bank, out_bank = bank[0:3], bank[3:6], bank[6:8]

        def col(name, i=0, p=128):
            return consts[0:p, COLS[name] + i:COLS[name] + i + 1]

        w_first, w_second, w_cross, w_self, w_ffn = sem("w_first"), sem("w_second"), sem("w_cross"), sem("w_self"), sem("w_ffn")
        consts_in, rows_in, x_early_in, x_late_in, xrow_in, zero_in, moe_b2_in = [sem(n) for n in (
            "consts_in", "rows_in", "x_early_in", "x_late_in", "xrow_in", "zero_in", "moe_b2_in")]
        ctx_in, mask_in = (sem("ctx_in0"), sem("ctx_in1")), (sem("mask_in0"), sem("mask_in1"))
        setup, setup_dve, pool_setup, biases_added = sem("setup"), sem("setup_dve"), sem("pool_setup"), sem("biases_added")
        (out_full, out_free, score_full, pt_full, pt_free, scores_masked, negmax_ready, probs_ready, probs_normed,
         qheads_ready, stats_ready, vareps_ready, rstd_ready, norm_done, resid_ready, x1_biased, hidden_ready,
         dve_chain, pool_chain) = [sem(n) for n in (
            "out_full out_free score_full pt_full pt_free scores_masked negmax_ready probs_ready probs_normed "
            "qheads_ready stats_ready vareps_ready rstd_ready norm_done resid_ready x1_biased hidden_ready "
            "dve_chain pool_chain").split()]
        (e_chain, picked, exped, alphaed, ranked, routed, scattered, moe_in0, tile_in0, tile_in1,
         t_stats, t_rstd, t_normed, t_xT_full, t_xT_ready, t_hid_full, t_hid_copied, t_hidT_full, t_hidT_ready,
         t_y_full, t_y_ready, y_out0, y_out1, gathered, f_stats, f_rstd, f_done, out_sent, x5_doubled) = [sem(n) for n in (
            "e_chain picked exped alphaed ranked routed scattered moe_in0 tile_in0 tile_in1 "
            "t_stats t_rstd t_normed t_xT_full t_xT_ready t_hid_full t_hid_copied t_hidT_full t_hidT_ready "
            "t_y_full t_y_ready y_out0 y_out1 gathered f_stats f_rstd f_done out_sent x5_doubled").split()]
        moe_in = [moe_in0] + [sem(f"moe_in{e}") for e in range(1, E)]
        tile_in, y_out = (tile_in0, tile_in1), (y_out0, y_out1)

        block = ctx.enter_context(nc.Block())

        score_release = []
        for stage in STEPS:
            for j in range({"as": 1, "cs": HG, "ss": 1, "f1": 1}.get(stage[0], 0)):
                score_release.append({"as": lambda: (probs_ready, PROBS[stage] + 1), "cs": lambda: (scores_masked, MASKED[stage] + j + 1),
                                      "ss": lambda: (probs_ready, PROBS[stage] + HG), "f1": lambda: (hidden_ready, HIDDEN[stage] + 1)}[stage[0]]())

        def group(n):
            u, g = divmod(n, NG)
            return u, g, g * HG // HB, (g * HG) % HB

        @block.sync
        def _(sp):
            sp.dma_start(xT_sb[:, 0:4], xT[:, 0:4]).then_inc(x_early_in, 16)
            sp.dma_start(wA[:, 0:2], weights[:, 0:2]).then_inc(w_first, 16)
            sp.dma_start(consts[:, :], cols).then_inc(consts_in, 16)
            sp.dma_start(wA[:, 2:4], weights[:, 2:4]).then_inc(w_second, 16)
            sp.dma_start(resid[0:S], xrow).then_inc(xrow_in, 16)
            for u in range(B):
                if u >= 2:
                    sp.wait_ge(out_full, OUT["ckv", u - 2] + C + KC)
                sp.dma_start(context[:, u % 2], ctxT[u]).then_inc(ctx_in[u % 2], 16)
                if u >= 2:
                    sp.wait_ge(scores_masked, MASKED["cs", NG * (u - 2) + NG - 1] + HG)
                sp.dma_start(masks[0:S, u % 2], mask[u:u + 1].to_broadcast([S, KX])).then_inc(mask_in[u % 2], 16)
                if u == 0:
                    sp.dma_start(xT_sb[:, 4:8], xT[:, 4:8]).then_inc(x_late_in, 16)
                if u == B - 2:
                    sp.wait_ge(out_free, OUT["ax", B - 1] + 1)
                    sp.dma_start(moe_w[:, 0], moe[0]).then_inc(moe_in[0], 16)
            sp.wait_ge(out_free, OUT["cy", B - 1] + 1)
            for e in range(1, 5):
                sp.dma_start(moe_w[:, e], moe[e]).then_inc(moe_in[e], 16)
            sp.wait_ge(out_free, OUT["sy", B - 1] + 1)
            for e in range(5, E if self_end >= MOE_WORDS else E - 1):
                sp.dma_start(moe_w[:, e], moe[e]).then_inc(moe_in[e], 16)
            sp.wait_ge(out_free, N_OUT)
            sp.wait_ge(resid_ready, B + 3 * B)
            if self_end < MOE_WORDS:
                sp.dma_start(moe_w[:, E - 1], moe[E - 1]).then_inc(moe_in[E - 1], 16)
            sp.dma_start(b2_sb.rearrange("p e d -> p (e d)"), b2rows.to_broadcast([128, E * D])).then_inc(moe_b2_in, 16)
            sp.wait_ge(scattered, 16 * B)
            for t in range(TILES + 4):
                if t < TILES:
                    if t >= 2:
                        sp.wait_ge(t_normed, t - 1)
                    sp.dma_start(xs[:, t % 2], x_slots[t * 128:(t + 1) * 128, :]).then_inc(tile_in[t % 2], 16)
                j = t - 4
                if j >= 0:
                    sp.wait_ge(t_y_ready, j + 1)
                    sp.dma_start(y_slots[j * 128:(j + 1) * 128, :], ys[:, j % 2]).then_inc(y_out[j % 2], 16)
            for b in range(B):
                sp.wait_ge(f_done, b + 1)
                sp.dma_start(out[b], yg[0:S, b]).then_inc(out_sent, 16)
            sp.wait_ge(out_sent, 16 * B)

        @block.tensor
        def _(pe):
            mm = nc.tensor.matmul

            def out_slot(n):
                if n >= 2:
                    pe.wait_ge(out_free, n - 1)
                return out_bank[n % 2]

            def score_slot(n):
                if n >= 3:
                    pe.wait_ge(*score_release[n - 3])
                return score_bank[n % 3]

            def pt_slot(n):
                if n >= 3:
                    pe.wait_ge(pt_free, n - 2)
                return pt_bank[n % 3]

            def project_T(slot, w, m, src, n=S):
                dst = out_slot(slot)
                for k in range(C):
                    last = mm(dst[:, 0:n], w[:, k, m * 128:(m + 1) * 128], src[:, k], start=k == 0, stop=k == C - 1)
                last.then_inc(out_full, 1)

            def project_rows(slot, src, w, rows=S):
                dst = out_slot(slot)
                for k in range(C):
                    last = mm(dst[0:rows, 0:D], src[:, k], w[:, k], start=k == 0, stop=k == C - 1)
                last.then_inc(out_full, 1)

            def transposed_rows(slot, src):
                dst = out_slot(slot)
                for m in range(C):
                    last = nc.tensor.transpose(dst[:, m * S:(m + 1) * S], src[:, m * 128:(m + 1) * 128], ident[0:S, 0:S])
                last.then_inc(out_full, 1)

            pe.wait_ge(setup, 1)
            for stage, i in STEPS:
                kind, slot = stage[0], OUT.get((stage, i))
                if stage == "aqk":
                    if i == 0:
                        pe.wait_ge(w_first, 16)
                    pe.wait_ge(x_early_in if i < 4 else x_late_in, 16)
                    for q, w in enumerate(("W1", "W2")):
                        for m in range(C):
                            project_T(slot + q * C + m, W[w], m, xT_sb[:, i])
                elif stage == "av":
                    if i == 0:
                        pe.wait_ge(w_second, 16)
                    project_rows(slot, xT_sb[:, i], W["W3"])
                elif stage == "as":
                    pe.wait_ge(out_free, OUT["aqk", i] + 2 * C)
                    dst = score_slot(SCORE[stage, i])
                    for k in range(C):
                        last = mm(dst[0:S, 0:S], QTa[:, i % 2, k], KTa[:, i % 2, k], start=k == 0, stop=k == C - 1)
                    last.then_inc(score_full, 1)
                elif stage == "at":
                    dst = pt_slot(PT[stage, i])
                    pe.wait_ge(probs_normed, NORMED[stage, i] + 1)
                    nc.tensor.transpose(dst[0:S, 0:S], probsA[0:S, i % 2], ident[0:S, 0:S]).then_inc(pt_full, 1)
                elif stage == "apv":
                    dst = out_slot(slot)
                    pe.wait_ge(pt_free, PT["at", i] + 1)
                    pe.wait_ge(out_free, OUT["av", i] + 1)
                    for m in range(C):
                        last = mm(dst[:, m * S:(m + 1) * S], va[0:S, i % 4, m * 128:(m + 1) * 128], probsTA[0:S, i % 2],
                                  start=True, stop=True)
                    last.then_inc(out_full, 1)
                elif stage in ("ay", "cy", "sy"):
                    of, src = {"a": ("apv", OTa), "c": ("cot", OTc), "s": ("sot", OTs)}[kind]
                    pe.wait_ge(out_free, OUT[of, i] + 1)
                    project_rows(slot, src[:, i % 2 if kind == "a" else 0], W[{"a": "W4", "c": "co", "s": "so"}[kind]])
                elif stage in ("ax", "cx", "sx", "zx"):
                    opened = {"a": "ay", "c": "cy", "s": "sy", "z": "zf"}[kind]
                    pe.wait_ge(norm_done, FINISHED[FINISHES[opened], i] + 1)
                    transposed_rows(slot, x1[0:S, i] if kind in "az" else ybuf[0:S, OPENED[opened, i] % NR])
                elif stage == "ckv":
                    if i == 0:
                        pe.wait_ge(w_cross, 16)
                    pe.wait_ge(ctx_in[i % 2], 16 * (i // 2 + 1))
                    for m in range(C):
                        project_T(slot + m, W["ck"], m, context[:, i % 2], KX)
                    for c in range(KC):
                        project_rows(slot + C + c, context[:, i % 2, :, c * KP:(c + 1) * KP], W["cv"], KP)
                elif stage == "cq":
                    pe.wait_ge(out_free, OUT["ax", i] + 1)
                    for m in range(C):
                        project_T(slot + m, W["cq"], m, x1T[:, i % 4])
                elif stage == "sqk":
                    if i == 0:
                        pe.wait_ge(w_self, 16)
                    pe.wait_ge(out_free, OUT["cx", i] + 1)
                    for q, w in enumerate(("sq", "sk")):
                        for m in range(C):
                            project_T(slot + q * C + m, W[w], m, x2T[:, i % 2])
                elif stage == "sv":
                    project_rows(slot, x2T[:, i % 2], W["sv"])
                elif stage == "cs":
                    u, g, m, h = group(i)
                    pe.wait_ge(qheads_ready, SPREAD["cqb", C * u + m] + 1)
                    pe.wait_ge(out_free, OUT["ckv", u] + C)
                    for j in range(HG):
                        dst = score_slot(SCORE[stage, i] + j)
                        mm(dst[0:S, 0:KX], qheadsC[:, m, h + j], keysT[:, u % 2, m], start=True, stop=True).then_inc(score_full, 1)
                elif stage == "ss":
                    u, g, m, h = group(i)
                    pe.wait_ge(qheads_ready, SPREAD["sqb", C * u + m] + 1)
                    dst = score_slot(SCORE[stage, i])
                    for j in range(HG):
                        last = mm(dst[0:S, j * S:(j + 1) * S], qheadsS[:, m, h + j], KTs[:, u % 2, m], start=True, stop=True)
                    last.then_inc(score_full, 1)
                elif stage in ("ct", "st"):
                    kc, kp, probs = (KC, KP, probsC) if kind == "c" else (1, S, probsS)
                    for c in range(kc):
                        dst = pt_slot(PT[stage, i] + c)
                        if c == 0:
                            pe.wait_ge(probs_ready, PROBS[kind + "s", i] + HG)
                        for j in range(HG):
                            last = nc.tensor.transpose(dst[0:kp, j * S:(j + 1) * S],
                                                       probs[0:S, (i % 2) * HG + j, c * kp:(c + 1) * kp], ident[0:S, 0:S])
                        last.then_inc(pt_full, 1)
                elif stage in ("cpv", "spv"):
                    u, g = divmod(i, NG)
                    kc, kp, probsT = (KC, KP, probsTC) if kind == "c" else (1, S, probsTS)
                    dst = out_slot(slot)
                    pe.wait_ge(pt_free, PT[kind + "t", i] + kc)
                    pe.wait_ge(out_free, OUT["ckv", u] + C + KC if kind == "c" else OUT["sv", u] + 1)
                    for c in range(kc):
                        for j in range(HG):
                            v = values[0:kp, u % 2, c] if kind == "c" else vrows[0:kp, u % 2]
                            at = (g * HG + j) * HD
                            last = mm(dst[32 * j:32 * j + 32, 0:S], v[:, at:at + 32], probsT[0:kp, i % 2, c, j * S:(j + 1) * S],
                                      start=c == 0, stop=c == kc - 1)
                    last.then_inc(out_full, 1)
                elif stage in ("cob", "sob"):
                    pe.wait_ge(out_free, OUT[kind + "pv", NG * i + NG - 1] + 1)
                    dst = out_slot(slot)
                    headsT = headsTC if kind == "c" else headsTS
                    for g in range(NG):
                        last = nc.tensor.transpose(dst[0:S, g * 128:(g + 1) * 128], headsT[:, i % 2, g], ident[:, :])
                    last.then_inc(out_full, 1)
                elif stage in ("cot", "sot"):
                    pe.wait_ge(out_free, OUT[kind + "ob", i] + 1)
                    transposed_rows(slot, (headsC if kind == "c" else headsS)[0:S])
                elif stage == "f1":
                    half, f = divmod(i, FC)
                    if f == 0:
                        if half == 0:
                            pe.wait_ge(w_ffn, 32)
                        pe.wait_ge(out_free, OUT["sx", (half + 1) * FU - 1] + 1)
                    dst = score_slot(SCORE[stage, i])
                    for k in range(C):
                        last = mm(dst[:, 0:FN], fi_sb[:, k, f * 128:(f + 1) * 128], x3T[:, k, half * FN:(half + 1) * FN],
                                  start=k == 0, stop=k == C - 1)
                    last.then_inc(score_full, 1)
                elif stage == "f2":
                    half, j = divmod(i, FU)
                    pe.wait_ge(hidden_ready, FC * (half + 1))
                    dst = out_slot(slot)
                    for f in range(FC):
                        last = mm(dst[0:S, 0:D], hiddenT[:, f, j * S:(j + 1) * S], fo_sb[:, f], start=f == 0, stop=f == FC - 1)
                    last.then_inc(out_full, 1)
                elif stage == "sc":
                    pe.wait_ge(out_free, OUT["zx", i] + 1)
                    dst = out_slot(slot)
                    for k in range(C):
                        last = mm(dst[0:S, 0:E], x5T[:, i % 2, k], consts[:, COLS["cent"] + k * E:COLS["cent"] + (k + 1) * E],
                                  start=k == 0, stop=k == C - 1)
                    last.then_inc(out_full, 1)

            pe.wait_ge(picked, 1)
            mm(bank[4][0:S, 0:B * E], lower[:, :], onehot[0:S].rearrange("p b e -> p (b e)"), start=True, stop=True)
            mm(bank[5][:, 0:B * E], ones[:, :], onehot[0:S].rearrange("p b e -> p (b e)"), start=True, stop=True).then_inc(ranked, 1)
            pe.wait_ge(routed, 1)
            expert = {}

            for t in range(-1, TILES + 2):
                j = t + 1
                if j < TILES:
                    pe.wait_ge(t_normed, j + 1)
                    if j >= 1:
                        pe.wait_ge(t_xT_ready, j)
                    for c in range(C):
                        last = nc.tensor.transpose(bank[6][:, c * 128:(c + 1) * 128], xsn[:, j % 2, c * 128:(c + 1) * 128], ident[:, :])
                    last.then_inc(t_xT_full, 1)
                j = t
                if 0 <= j < TILES:
                    expert[j] = pe.value_load(tile_expert[0:1, j:j + 1], min_val=0, max_val=E - 1)
                    pe.wait_ge(moe_in[min(j, E - 1)], 16)
                    pe.wait_ge(t_xT_ready, j + 1)
                    if j >= 2:
                        pe.wait_ge(t_hid_copied, 2 * (j - 1))
                    w1 = moe_w[:, bass.ds(expert[j], 1), 0:C * F].rearrange("p e (c f) -> p (e c) f", c=C)
                    for half in range(2):
                        for c in range(C):
                            last = mm(bank[2 * (j % 2) + half][:, :], xsT[:, j % 2, c], w1[:, c, half * 512:(half + 1) * 512],
                                      start=c == 0, stop=c == C - 1)
                        last.then_inc(t_hid_full, 1)
                j = t - 1
                if 0 <= j < TILES:
                    pe.wait_ge(t_hid_copied, 2 * (j + 1))
                    for half in range(2):
                        if j >= 1:
                            pe.wait_ge(t_hidT_ready, 2 * (j - 1) + half + 1)
                        for f in range(4):
                            last = nc.tensor.transpose(bank[4 + half][:, f * 128:(f + 1) * 128],
                                                       hid[:, j % 2, (half * 4 + f) * 128:(half * 4 + f + 1) * 128], ident[:, :])
                        last.then_inc(t_hidT_full, 1)
                j = t - 2
                if 0 <= j < TILES:
                    pe.wait_ge(t_hidT_ready, 2 * (j + 1))
                    if j >= 1:
                        pe.wait_ge(t_y_ready, j)
                    w2 = moe_w[:, bass.ds(expert[j], 1), C * F:].rearrange("p e (f d) -> p (e f) d", f=FC)
                    for f in range(FC):
                        last = mm(bank[7][:, 0:D], hidT[:, j % 2, f], w2[:, f], start=f == 0, stop=f == FC - 1)
                    last.then_inc(t_y_full, 1)

        @block.vector
        def _(dve):
            v = nc.vector
            chain = [0]

            def link(ins):
                chain[0] += 1
                ins.then_inc(dve_chain, 1)

            def linked():
                dve.wait_ge(dve_chain, chain[0])

            dve.wait_ge(setup, 1)
            v.reduce_sum(qmask[:, :], ident[:, :].rearrange("p (h d) -> p h d", d=HD), axis=AX.X).then_inc(setup_dve, 1)
            dve.wait_ge(setup_dve, 1)
            v.tensor_scalar(qmask[:, :], qmask[:, :], 1.0 / HD ** 0.5, None, ALU.mult).then_inc(setup_dve, 1)
            dve.wait_ge(setup, 6)
            dve.wait_ge(consts_in, 16)

            def full(n):
                dve.wait_ge(out_full, n + 1)
                return out_bank[n % 2]

            def open_norm(stage, i):
                k = OPENED[stage, i]
                if k >= NR:
                    was, wi = next(s for s, n in OPENED.items() if n == k - NR)
                    dve.wait_ge(norm_done, FINISHED[FINISHES[was], wi] + 1)
                    if was in ("cy", "sy"):
                        dve.wait_ge(out_full, OUT[was[0] + "x", wi] + 1)
                        dve.wait_ge(resid_ready, B + RESID[was[0] + "b", wi] + 1)
                return k

            def take_stats(k):
                v.bn_stats(stats[0:S, k % NR], ybuf[0:S, k % NR]).then_inc(dve_chain, 1)
                chain[0] += 1
                linked()
                v.bn_aggr(meanvar[0:S, k % NR], stats[0:S, k % NR]).then_inc(stats_ready, 1)

            for stage, i in STEPS:
                kind, slot = stage[0], OUT.get((stage, i))
                if stage in ("aqk", "sqk"):
                    q, kk, bq, bk = (QTa, KTa, "b1", "b2") if kind == "a" else (QTs, KTs, "sqb", "skb")
                    for n, (dst, bias) in enumerate(((q, bq), (kk, bk))):
                        for m in range(C):
                            src = full(slot + n * C + m)
                            if kind == "a" and n == 0:
                                v.tensor_scalar(dst[:, i % 2, m], src[:, 0:S], col(bias, m), 1.0 / D ** 0.5, ALU.add, ALU.mult)\
                                    .then_inc(out_free, 1)
                            else:
                                v.tensor_scalar(dst[:, i % 2 if dst is not QTs else 0, m], src[:, 0:S], col(bias, m), None, ALU.add).then_inc(out_free, 1)
                elif stage in ("av", "sv"):
                    src = full(slot)
                    dst = va[0:S, i % 4] if kind == "a" else vrows[0:S, i % 2, 0:D]
                    v.tensor_copy(dst, src[0:S, 0:D]).then_inc(out_free, 1)
                elif stage == "as":
                    s = SCORE[stage, i]
                    dve.wait_ge(score_full, s + 1)
                    v.tensor_reduce(negmax["a"][0:S, i], score_bank[s % 3][0:S, 0:S], AX.X, ALU.max, negate=True)\
                        .then_inc(negmax_ready, 1)
                elif stage == "at":
                    dve.wait_ge(probs_ready, PROBS["as", i] + 1)
                    link(v.reciprocal(recips["a"][0:S, i], sums["a"][0:S, i]))
                    linked()
                    v.tensor_scalar(probsA[0:S, i % 2], probsA[0:S, i % 2], recips["a"][0:S, i], None, ALU.mult)\
                        .then_inc(probs_normed, 1)
                elif stage in ("apv", "cot", "sot"):
                    src = full(slot)
                    dst, bias = {"a": (OTa, "b3"), "c": (OTc, "cvb"), "s": (OTs, "svb")}[kind]
                    r = i % 2 if kind == "a" else 0
                    v.tensor_scalar(dst[:, r, 0], src[:, 0:S], col(bias, 0), None, ALU.add)
                    v.tensor_scalar(dst[:, r, 1], src[:, S:2 * S], col(bias, 1), None, ALU.add).then_inc(out_free, 1)
                elif stage in ("ay", "cy", "sy", "f2"):
                    k = open_norm(stage, i)
                    src = full(slot)
                    made = {"ay": lambda: i, "cy": lambda: B + RESID["ab", i], "sy": lambda: B + RESID["cb", i],
                            "f2": lambda: B + RESID["sb", i]}[stage]()
                    dve.wait_ge(resid_ready, made + 1)
                    v.tensor_tensor(ybuf[0:S, k % NR], src[0:S, 0:D], resid[0:S, i], ALU.add).then_inc(out_free, 1)
                    dve.wait_ge(out_free, slot + 1)
                    take_stats(k)
                elif stage in ("ab", "cb", "sb", "zb"):
                    k = OPENED[{"a": "ay", "c": "cy", "s": "sy", "z": "zf"}[kind], i]
                    dve.wait_ge(rstd_ready, k + 1)
                    dst = x1[0:S, i] if kind in "az" else ybuf[0:S, k % NR]
                    v.tensor_scalar(dst, ybuf[0:S, k % NR], meanvar[0:S, k % NR, 0:1], rstd[0:S, k % NR], ALU.subtract, ALU.mult)\
                        .then_inc(norm_done, 1)
                elif stage in ("ax", "zx"):
                    src = full(slot)
                    dst = x1T[:, i % 4] if kind == "a" else x5T[:, i % 2]
                    v.tensor_copy(dst, src[:, 0:2 * S].rearrange("p (c s) -> p c s", c=C)).then_inc(out_free, 1)
                elif stage in ("cx", "sx"):
                    src = full(slot)
                    gain, shift = ("cog", "cobe") if kind == "c" else ("sog", "sobe")
                    for c in range(C):
                        dst = x2T[:, i % 2, c] if kind == "c" else x3T[:, c, i * S:(i + 1) * S]
                        last = v.tensor_scalar(dst, src[:, c * S:(c + 1) * S], col(gain, c), col(shift, c), ALU.mult, ALU.add)
                    last.then_inc(out_free, 1)
                elif stage == "ckv":
                    for m in range(C):
                        src = full(slot + m)
                        v.tensor_scalar(keysT[:, i % 2, m], src[:, 0:KX], col("ckb", m), None, ALU.add).then_inc(out_free, 1)
                    for c in range(KC):
                        src = full(slot + C + c)
                        v.tensor_copy(values[0:KP, i % 2, c, 0:D], src[0:KP, 0:D]).then_inc(out_free, 1)
                elif stage == "cq":
                    for m in range(C):
                        src = full(slot + m)
                        v.tensor_scalar(QTc[:, 0, m], src[:, 0:S], col("cqb", m), None, ALU.add).then_inc(out_free, 1)
                elif stage in ("cqb", "sqb"):
                    u, m = divmod(i, C)
                    dve.wait_ge(out_free, OUT["cq", u] + C if kind == "c" else OUT["sqk", u] + C)
                    if u >= 1:
                        n = NG * (u - 1) + NG // C * (m + 1) - 1
                        dve.wait_ge(score_full, SCORE[kind + "s", n] + (HG if kind == "c" else 1))
                    q, dst = (QTc, qheadsC) if kind == "c" else (QTs, qheadsS)
                    v.tensor_tensor(dst[:, m], q[:, 0, m:m + 1].to_broadcast([128, HB, S]),
                                    qmask[:, :].unsqueeze(2).to_broadcast([128, HB, S]), ALU.mult).then_inc(qheads_ready, 1)
                elif stage == "cs":
                    u, g, m, h = group(i)
                    if g == 0:
                        dve.wait_ge(mask_in[u % 2], 16 * (u // 2 + 1))
                    if i >= 2:
                        dve.wait_ge(pt_full, PT["ct", i - 2] + KC)
                    for j in range(HG):
                        s = SCORE[stage, i] + j
                        dve.wait_ge(score_full, s + 1)
                        v.tensor_tensor_reduce(out=probsC[0:S, (i % 2) * HG + j], in0=score_bank[s % 3][0:S, 0:KX], in1=masks[0:S, u % 2],
                                               scale=-1.0, scalar=3.0e38, op0=ALU.add, op1=ALU.min,
                                               accum_out=negmax["c"][0:S, u, g * HG + j:g * HG + j + 1]).then_inc(scores_masked, 1)
                elif stage == "ss":
                    u, g, m, h = group(i)
                    s = SCORE[stage, i]
                    dve.wait_ge(score_full, s + 1)
                    v.tensor_reduce(negmax["s"][0:S, u, g * HG:(g + 1) * HG],
                                    score_bank[s % 3][0:S, 0:HG * S].rearrange("p (j s) -> p j s", j=HG), AX.X, ALU.max,
                                    negate=True).then_inc(negmax_ready, 1)
                elif stage in ("cpv", "spv"):
                    u, g = divmod(i, NG)
                    src = full(slot)
                    v.tensor_copy((headsTC if kind == "c" else headsTS)[:, u % 2, g], src[:, 0:S]).then_inc(out_free, 1)
                elif stage in ("cob", "sob"):
                    src = full(slot)
                    dve.wait_ge(probs_ready, PROBS[kind + "s", NG * i + NG - 1] + HG)
                    link(v.reciprocal(recips[kind][0:S, i], sums[kind][0:S, i]))
                    linked()
                    v.tensor_tensor((headsC if kind == "c" else headsS)[0:S].rearrange("p (h d) -> p h d", d=HD),
                                    src[0:S, :].rearrange("p (h d) -> p h d", d=2 * HD)[:, :, 0:HD],
                                    recips[kind][0:S, i].unsqueeze(2).to_broadcast([S, H, HD]), ALU.mult).then_inc(out_free, 1)
                elif stage == "zf":
                    kf = OPENED["f2", i]
                    dve.wait_ge(rstd_ready, kf + 1)
                    k = open_norm(stage, i)
                    link(v.scalar_tensor_tensor(ybuf[0:S, kf % NR], ybuf[0:S, kf % NR], meanvar[0:S, kf % NR, 0:1], R["fog"],
                                                ALU.subtract, ALU.mult))
                    linked()
                    dve.wait_ge(x1_biased, KEPT["cq", i] + 1)
                    v.scalar_tensor_tensor(ybuf[0:S, k % NR], ybuf[0:S, kf % NR], rstd[0:S, kf % NR], x1[0:S, i],
                                           ALU.mult, ALU.add).then_inc(norm_done, 1)
                    dve.wait_ge(norm_done, FINISHED[stage, i] + 1)
                    take_stats(k)
                elif stage == "sc":
                    src = full(slot)
                    v.tensor_copy(scores[0:S, i], src[0:S, 0:E]).then_inc(out_free, 1)
            dve.wait_ge(out_free, N_OUT)

            ec = [0]

            def elink(ins):
                ec[0] += 1
                ins.then_inc(e_chain, 1)
                dve.wait_ge(e_chain, ec[0])

            def bc(ap, shape):
                return ap.to_broadcast(shape)

            dve.wait_ge(setup, 12)
            elink(v.tensor_reduce(best[0:S], scores[0:S], AX.X, ALU.max))
            elink(v.tensor_tensor(rt[0:S], scores[0:S], best[0:S].unsqueeze(2).to_broadcast([S, B, E]), ALU.is_equal))
            elink(v.tensor_tensor(rt[0:S], rt[0:S], rev[0:S], ALU.mult))
            elink(v.tensor_reduce(slotf[0:S], rt[0:S], AX.X, ALU.max))
            v.tensor_tensor(onehot[0:S], rt[0:S], slotf[0:S].unsqueeze(2).to_broadcast([S, B, E]), ALU.is_equal).then_inc(picked, 1)
            dve.wait_ge(ranked, 1)
            elink(v.memset(before[:, 0], 0.0))
            tot = bank[5][:, 0:B * E].rearrange("p (b e) -> p b e", b=B)
            for b in range(1, B):
                elink(v.tensor_tensor(before[:, b], before[:, b - 1], tot[:, b - 1], ALU.add))
            elink(v.tensor_tensor(cnt[:, :], before[:, B - 1], tot[:, B - 1], ALU.add))
            elink(v.tensor_tensor(over[:, :, :], cnt[:, :].unsqueeze(2).to_broadcast([128, E, 6]), thr[:, :, :], ALU.is_gt))
            elink(v.reduce_sum(ntile[:, :], over[:, :, :], axis=AX.X))
            elink(v.tensor_scalar(ntile[:, :], ntile[:, :], 1.0, None, ALU.add))
            elink(v.tensor_copy(ends[:, 0:1], ntile[:, 0:1]))
            for e in range(1, E):
                elink(v.tensor_tensor(ends[:, e:e + 1], ends[:, e - 1:e], ntile[:, e:e + 1], ALU.add))
            elink(v.tensor_tensor(base[:, :], ends[:, :], ntile[:, :], ALU.subtract))
            elink(v.tensor_scalar(base[:, :], base[:, :], 128.0, None, ALU.mult))
            elink(v.tensor_tensor(rt[0:S], bank[4][0:S, 0:B * E].rearrange("p (b e) -> p b e", b=B), before[0:S], ALU.add))
            elink(v.tensor_tensor(rt[0:S], rt[0:S], base[0:S].unsqueeze(1).to_broadcast([S, B, E]), ALU.add))
            elink(v.tensor_tensor(rt[0:S], rt[0:S], onehot[0:S], ALU.mult))
            elink(v.reduce_sum(slotf[0:S], rt[0:S], axis=AX.X))
            v.tensor_copy(token_slot[0:S], slotf[0:S]).then_inc(routed, 1)
            dve.wait_ge(routed, 1)
            elink(v.tensor_tensor(tge[:, :, :], tidx[:, :, :], ends[:, 0:E - 1].unsqueeze(1).to_broadcast([128, TILES, E - 1]), ALU.is_ge))
            elink(v.reduce_sum(tilef[:, :], tge[:, :, :], axis=AX.X))
            v.tensor_copy(tile_expert[:, :], tilef[:, :]).then_inc(routed, 1)
            dve.wait_ge(routed, 2)
            dve.wait_ge(exped, 1)
            elink(v.tensor_scalar(ex[0:S], ex[0:S], 1.0, None, ALU.add))
            elink(v.reciprocal(alpha[0:S], ex[0:S]))

            expert = {}

            def load_tile(j):
                dve.wait_ge(tile_in[j % 2], 16 * (j // 2 + 1))
                elink(v.bn_stats(stats[:, j % NR], xs[:, j % 2]))
                v.bn_aggr(meanvar[:, j % NR], stats[:, j % NR]).then_inc(t_stats, 1)
                dve.wait_ge(t_rstd, j + 1)
                v.tensor_scalar(xsn[:, j % 2], xs[:, j % 2], meanvar[:, j % NR, 0:1], rstd[:, j % NR], ALU.subtract, ALU.mult).then_inc(t_normed, 1)

            def gain_tile(j):
                expert[j] = dve.value_load(tile_expert[0:1, j:j + 1], min_val=0, max_val=E - 1)
                dve.wait_ge(t_xT_full, j + 1)
                if j >= 2:
                    dve.wait_ge(t_hid_full, 2 * (j - 1))
                for c in range(C):
                    g = consts[:, bass.ds(expert[j] * C + COLS["gamma"] + c, 1)]
                    b = consts[:, bass.ds(expert[j] * C + COLS["beta"] + c, 1)]
                    last = v.tensor_scalar(xsT[:, j % 2, c], bank[6][:, c * 128:(c + 1) * 128], g, b, ALU.mult, ALU.add)
                last.then_inc(t_xT_ready, 1)

            def relu_tile(j):
                if j >= 2:
                    dve.wait_ge(t_y_full, j - 1)
                for half in range(2):
                    dve.wait_ge(t_hidT_full, 2 * j + half + 1)
                    for f in range(4):
                        b = consts[:, bass.ds(expert[j] * FC + COLS["moeb1"] + half * 4 + f, 1)]
                        last = v.tensor_scalar(hidT[:, j % 2, half * 4 + f], bank[4 + half][:, f * 128:(f + 1) * 128], b, 0.0,
                                               ALU.add, ALU.max)
                    last.then_inc(t_hidT_ready, 1)

            def bias_tile(j):
                if j == 0:
                    dve.wait_ge(moe_b2_in, 16)
                if j >= 2:
                    dve.wait_ge(y_out[j % 2], 16 * (j // 2))
                dve.wait_ge(t_y_full, j + 1)
                v.tensor_tensor(ys[:, j % 2], bank[7][:, 0:D], b2_sb[:, bass.ds(expert[j], 1)].rearrange("p e d -> p (e d)"), ALU.add)\
                    .then_inc(t_y_ready, 1)

            load_tile(0)
            for t in range(-1, TILES + 2):
                if t + 1 < TILES:
                    gain_tile(t + 1)
                if t + 2 < TILES:
                    load_tile(t + 2)
                if 0 <= t - 1 < TILES:
                    relu_tile(t - 1)
                if 0 <= t - 2 < TILES:
                    bias_tile(t - 2)

            dve.wait_ge(x5_doubled, 1)
            dve.wait_ge(gathered, 16 * B)
            for t in range(B + 1):
                if t < B:
                    elink(v.scalar_tensor_tensor(yg[0:S, t], yg[0:S, t], alpha[0:S, t:t + 1], x5[0:S, t], ALU.mult, ALU.add))
                    elink(v.bn_stats(stats[0:S, t % NR], yg[0:S, t]))
                    v.bn_aggr(meanvar[0:S, t % NR], stats[0:S, t % NR]).then_inc(f_stats, 1)
                if t >= 1:
                    b = t - 1
                    dve.wait_ge(f_rstd, b + 1)
                    v.tensor_scalar(yg[0:S, b], yg[0:S, b], meanvar[0:S, b % NR, 0:1], rstd[0:S, b % NR], ALU.subtract, ALU.mult)\
                        .then_inc(f_done, 1)

        @block.scalar
        def _(act):
            a = nc.scalar
            act.wait_ge(w_first, 16)
            act.dma_start(wC, weights[:, 4:8]).then_inc(w_cross, 16)
            act.dma_start(spread[0:S].rearrange("p r d -> p (r d)"), rows.to_broadcast([S, len(ROWS) * D])).then_inc(rows_in, 16)
            act.dma_start(wS, weights[:, 8:12]).then_inc(w_self, 16)
            act.dma_start(fi_sb, fi).then_inc(w_ffn, 16)
            act.dma_start(fo_sb, fo).then_inc(w_ffn, 16)
            act.wait_ge(consts_in, 16)
            for stage, i in STEPS:
                kind = stage[0]
                if stage == "as":
                    if i >= 2:
                        act.wait_ge(pt_full, PT["at", i - 2] + 1)
                    act.wait_ge(negmax_ready, NEGMAX[stage, i] + 1)
                    a.activation(probsA[0:S, i % 2], score_bank[SCORE[stage, i] % 3][0:S, 0:S], ACT.Exp,
                                 bias=negmax["a"][0:S, i], accum_out=sums["a"][0:S, i]).then_inc(probs_ready, 1)
                elif stage == "at":
                    if i >= 2:
                        act.wait_ge(out_full, OUT["apv", i - 2] + 1)
                    act.wait_ge(pt_full, PT[stage, i] + 1)
                    a.activation(probsTA[0:S, i % 2], pt_bank[PT[stage, i] % 3][0:S, 0:S], ACT.Copy).then_inc(pt_free, 1)
                elif stage in ("cs", "ss"):
                    u, g, m, h = group(i)
                    if stage == "ss":
                        if i >= 2:
                            act.wait_ge(pt_full, PT["st", i - 2] + 1)
                        act.wait_ge(negmax_ready, NEGMAX[stage, i] + 1)
                    for j in range(HG):
                        at = g * HG + j
                        if stage == "cs":
                            act.wait_ge(scores_masked, MASKED[stage, i] + j + 1)
                            src = dst = probsC[0:S, (i % 2) * HG + j]
                        else:
                            src, dst = score_bank[SCORE[stage, i] % 3][0:S, j * S:(j + 1) * S], probsS[0:S, (i % 2) * HG + j]
                        a.activation(dst, src, ACT.Exp, bias=negmax[kind][0:S, u, at:at + 1], scale=-1.0 if kind == "c" else 1.0,
                                     accum_out=sums[kind][0:S, u, at:at + 1]).then_inc(probs_ready, 1)
                elif stage in ("ct", "st"):
                    kc, kp, probsT = (KC, KP, probsTC) if kind == "c" else (1, S, probsTS)
                    if i >= 2:
                        act.wait_ge(out_full, OUT[kind + "pv", i - 2] + 1)
                    for c in range(kc):
                        act.wait_ge(pt_full, PT[stage, i] + c + 1)
                        a.activation(probsT[0:kp, i % 2, c], pt_bank[(PT[stage, i] + c) % 3][0:kp, 0:HG * S], ACT.Copy)\
                            .then_inc(pt_free, 1)
                elif stage == "f1":
                    half, f = divmod(i, FC)
                    if half == 0 and f == 0:
                        act.wait_ge(zero_in, 16 * TILES)
                    elif f == 0:
                        act.wait_ge(out_full, OUT["f2", FU - 1] + 1)
                    act.wait_ge(score_full, SCORE[stage, i] + 1)
                    a.activation(hiddenT[:, f], score_bank[SCORE[stage, i] % 3][:, 0:FN], ACT.Gelu, bias=col("fib", f))\
                        .then_inc(hidden_ready, 1)

            act.wait_ge(picked, 1)
            a.activation(ex[0:S], best[0:S], ACT.Exp, scale=-1.0).then_inc(exped, 1)
            for j in range(TILES):
                if j >= 2:
                    act.wait_ge(t_hidT_full, 2 * (j - 1))
                for half in range(2):
                    act.wait_ge(t_hid_full, 2 * j + half + 1)
                    a.activation(hid[:, j % 2, half * 512:(half + 1) * 512], bank[2 * (j % 2) + half][:, :], ACT.Copy)\
                        .then_inc(t_hid_copied, 1)

        @block.gpsimd
        def _(pool):
            g = nc.gpsimd
            g.memset(ident[:, :], 0.0).then_inc(pool_setup, 1)
            pool.wait_ge(pool_setup, 1)
            g.affine_select(out=ident[:, :], in_=ident[:, :], compare_op=ALU.not_equal, fill=1.0, base=0, pattern=[[-1, 128]],
                            channel_multiplier=1).then_inc(setup, 1)
            g.memset(values[:, 0, :, D:], 0.0).then_inc(setup, 1)
            g.memset(values[:, 1, :, D:], 0.0).then_inc(setup, 1)
            g.memset(vrows[:, :, D:], 0.0).then_inc(setup, 1)
            g.memset(scal[:, 0:1], EPS).then_inc(setup, 1)
            g.memset(scal[:, 1:2], -0.5).then_inc(setup, 1)
            g.memset(zero, 0.0).then_inc(setup, 1)
            g.memset(lower[:, :], 1.0).then_inc(pool_setup, 1)
            g.memset(ones[:, :], 1.0).then_inc(setup, 1)
            pool.wait_ge(pool_setup, 2)
            g.affine_select(out=lower[:, :], in_=lower[:, :], compare_op=ALU.is_gt, fill=0.0, base=0, pattern=[[1, S]],
                            channel_multiplier=-1).then_inc(setup, 1)
            g.iota(rev[:, :, :], pattern=[[0, B], [-1, E]], base=E, channel_multiplier=0,
                   allow_small_or_imprecise_dtypes=True).then_inc(setup, 1)
            g.iota(thr[:, :, :], pattern=[[0, E], [128, 6]], base=128, channel_multiplier=0,
                   allow_small_or_imprecise_dtypes=True).then_inc(setup, 1)
            g.iota(tidx[:, :, :], pattern=[[1, TILES], [0, E - 1]], base=0, channel_multiplier=0,
                   allow_small_or_imprecise_dtypes=True).then_inc(setup, 1)
            pool.wait_ge(setup, 7)
            for t in range(TILES):
                pool.dma_start(x_slots[t * 128:(t + 1) * 128, :], zero).then_inc(zero_in, 16)
            pool.wait_ge(rows_in, 16)
            g.tensor_tensor(R["cobe"], R["cobe"], R["sob"], ALU.add).then_inc(biases_added, 1)
            g.tensor_tensor(R["sobe"], R["sobe"], R["fob"], ALU.add).then_inc(biases_added, 1)
            pool.wait_ge(biases_added, 2)

            vareps_count = [0]

            def inverse_deviation(k, rows, stats_sem, ready_sem, n):
                pool.wait_ge(stats_sem, n + 1)
                g.tensor_tensor(vareps[0:rows, k % NR], meanvar[0:rows, k % NR, 1:2], scal[0:rows, 0:1], ALU.add).then_inc(vareps_ready, 1)
                vareps_count[0] += 1
                pool.wait_ge(vareps_ready, vareps_count[0])
                g.tensor_tensor(rstd[0:rows, k % NR], vareps[0:rows, k % NR], scal[0:rows, 1:2], ALU.pow).then_inc(ready_sem, 1)

            pool.wait_ge(xrow_in, 16)
            for u in range(B):
                g.tensor_tensor(resid[0:S, u], resid[0:S, u], R["b4"], ALU.add).then_inc(resid_ready, 1)
            chain = 0
            for stage, i in STEPS:
                if stage in FINISHES:
                    inverse_deviation(OPENED[stage, i], S, stats_ready, rstd_ready, OPENED[stage, i])
                elif stage == "ab":
                    pool.wait_ge(norm_done, FINISHED[stage, i] + 1)
                    g.tensor_tensor(resid[0:S, i], x1[0:S, i], R["cob"], ALU.add).then_inc(resid_ready, 1)
                elif stage == "cq":
                    pool.wait_ge(out_full, OUT["ax", i] + 1)
                    pool.wait_ge(resid_ready, B + RESID["ab", i] + 1)
                    g.tensor_tensor(x1[0:S, i], x1[0:S, i], R["fobe"], ALU.add).then_inc(x1_biased, 1)
                elif stage in ("cb", "sb"):
                    k = OPENED[stage[0] + "y", i]
                    gain, shift = ("cog", "cobe") if stage == "cb" else ("sog", "sobe")
                    pool.wait_ge(norm_done, FINISHED[stage, i] + 1)
                    g.tensor_tensor(resid[0:S, i], ybuf[0:S, k % NR], R[gain], ALU.mult).then_inc(pool_chain, 1)
                    chain += 1
                    pool.wait_ge(pool_chain, chain)
                    g.tensor_tensor(resid[0:S, i], resid[0:S, i], R[shift], ALU.add).then_inc(resid_ready, 1)

            pool.wait_ge(zero_in, 16 * TILES)
            pool.wait_ge(routed, 1)
            for b in range(B):
                g.indirect_dma_start(out=x_slots, out_offset=bass.IndirectOffsetOnAxis(ap=token_slot[0:S, b:b + 1], axis=0),
                                     in_=x5[0:S, b], in_offset=None, bounds_check=TILES * 128 - 1).then_inc(scattered, 16)
            for j in range(TILES):
                if j == 4:
                    pool.wait_ge(scattered, 16 * B)
                    g.tensor_tensor(x5[0:S], x5[0:S], x5[0:S], ALU.add).then_inc(x5_doubled, 1)
                inverse_deviation(j, 128, t_stats, t_rstd, j)
            pool.wait_ge(y_out[0], 16 * (TILES // 2))
            pool.wait_ge(y_out[1], 16 * (TILES // 2))
            for b in range(B):
                g.indirect_dma_start(out=yg[0:S, b], out_offset=None, in_=y_slots,
                                     in_offset=bass.IndirectOffsetOnAxis(ap=token_slot[0:S, b:b + 1], axis=0),
                                     bounds_check=TILES * 128 - 1).then_inc(gathered, 16)
            for b in range(B):
                inverse_deviation(b, S, f_stats, f_rstd, b)


def kernel(**inputs):
    import concourse.bacc as bacc
    from concourse.bass_utils import run_bass_kernel_spmd

    a = {n: np.ascontiguousarray(v) for n, v in inputs.items()}
    at, xa, mo = "L0_attn_", "L0_xattn_", "L0_ffn_"

    def chunks(w):
        return w.reshape(-1, 128, w.shape[-1]).transpose(1, 0, 2)

    def columns(v):
        return v.reshape(-1, 128).T

    x = a["x"]
    w = [a[at + n] for n in ("W1", "W2", "W3", "W4")]
    w += [a[xa + n + "_w"] for n in ("cq", "ck", "cv", "co", "sq", "sk", "sv", "so")]
    cols = [a[at + n] for n in ("b1", "b2", "b3")]
    cols += [a[xa + n] for n in ("cq_b", "ck_b", "cv_b", "sq_b", "sk_b", "sv_b", "fi_b", "co_g", "co_be", "so_g", "so_be")]
    cols += [a[mo + n] for n in ("gamma", "beta", "b1")]
    cent = chunks(a[mo + "centroids"].T).reshape(128, -1)
    rows = [a[at + "b4"]] + [a[xa + n] for n in ("co_b", "co_g", "co_be", "so_b", "so_g", "so_be", "fo_b", "fo_g", "fo_be")]
    moe1 = a[mo + "W1"].transpose(0, 2, 1).reshape(E, C, 128, F).transpose(0, 2, 1, 3).reshape(E, 128, C * F)
    moe2 = a[mo + "W2"].transpose(0, 2, 1).reshape(E, FC, 128, D).transpose(0, 2, 1, 3).reshape(E, 128, FC * D)
    arrays = {
        "xT": x.reshape(B, S, C, 128).transpose(3, 0, 2, 1),
        "xrow": x.transpose(1, 0, 2),
        "ctxT": a["ctx_1024"].reshape(B, KX, C, 128).transpose(0, 3, 2, 1),
        "mask": a["mask_Bx1x1xS2_ff0"].reshape(B, KX),
        "weights": np.stack([chunks(m) for m in w], axis=1),
        "fi": chunks(a[xa + "fi_w"]),
        "fo": chunks(a[xa + "fo_w"]),
        "cols": np.concatenate([columns(c) for c in cols] + [cent], axis=1),
        "rows": np.concatenate(rows).reshape(1, -1),
        "b2rows": a[mo + "b2"].reshape(1, E * D),
        "moe": np.concatenate([moe1, moe2], axis=2),
    }
    arrays = {n: np.ascontiguousarray(v) for n, v in arrays.items()}
    nc = bacc.Bacc("TRN2", target_bir_lowering=False, num_devices=1)
    ap = {n: nc.dram_tensor(n, v.shape, mybir.dt.from_np(v.dtype), kind="ExternalInput").ap() for n, v in arrays.items()}
    x_slots = nc.dram_tensor("x_slots", (TILES * 128, D), F32, kind="Internal").ap()
    y_slots = nc.dram_tensor("y_slots", (TILES * 128, D), F32, kind="Internal").ap()
    out = nc.dram_tensor("out", (B, S, D), F32, kind="ExternalOutput").ap()
    decoder_layer(nc, **ap, x_slots=x_slots, y_slots=y_slots, out=out)
    r = run_bass_kernel_spmd(nc, [arrays], core_ids=[0])
    return r.results[0]["out"]
```

```python
import numpy as np
import concourse.bass as bass
from concourse import mybir
from contextlib import ExitStack, nullcontext

F32 = mybir.dt.float32
I32 = mybir.dt.int32
U32 = mybir.dt.uint32
ALU = mybir.AluOpType
ACT = mybir.ActivationFunctionType
AX = mybir.AxisListType

B, S, D, KX = 8, 112, 256, 375
H, HD = 16, 16
F, E = 1024, 8
C = D // 128
FC = F // 128
FEED = [((0, 1), 34.09), ((2, 3), 39.15), ((4, 5), 45.43), ((6,), 49.62), ((7,), 52.39)]
FN = max(len(batches) for batches, _ in FEED) * S
KP, KC = 125, 3
HG = 4
NG = H // HG
GROUPS = B * NG
HB = 128 // HD
VW = D + HD
EXTRA = (B * S - 1) // 128
TILES = E + EXTRA
XW = D + 4
ALPHA, TOKEN, MEAN, RSTD = range(D, XW)
NR = 6
RS, RP, RO = 3, 2, 3
EPS = 1e-5
FAR = 4096.0

COLS = dict(b1=0, b2=2, b3=4, cqb=6, ckb=8, cvb=10, sqb=12, skb=14, svb=16, fib=18, cog=26, cobe=28,
            sog=30, sobe=32, gamma=34, beta=50, moeb1=66, cent=130)
NCOLS = 146
ROWS = ["b4", "cob", "cog", "cobe", "sob", "sog", "sobe", "fob", "fog", "fobe"]
WEIGHTS = ["W1", "W2", "W3", "W4", "cq", "ck", "cv", "co", "sq", "sk", "sv", "so"]


FIRST_START = (0.04, 0.04, 2, 2.72, 7.08, 8.99, 14.85, 18.96)
FIRST = {"aqk": -9.03, "av": -7.45, "as": -7.93, "at": -6.87, "apv": -5.86, "ay": -4.85, "ab": -3.9, "ax": -2.83}
CONTEXT_START = (-1.96, 4.6, 8.05, 13.28, 15.83, 20.93, 23.52, 28.12)
CONTEXT = {"ck": (-1.7, -1.7), "cv": (-1.7, -1.7, -1.7)}
CROSS = {"cq": (-1.54,), "cqb": (-0.99, 0.35), "cob": (6.16,), "cot": (6.59,), "cy": (8.39,), "cb": (9.26,),
         "cx": (10.77,)}
CROSS_GROUP = {"ct": (1.0, 1.0, 1.03), "cpv": (2.02,)}
HEADS = (-0.18, -0.04, 0.0, 0.0)
SELF_START = (11.0, 15.0, 19.0, 23.0, 27.0, 31.0, 35.0, 38.95)
SELF_PACE = (1.0, 1.11, 1.0, 1.0, 1.0, 1.0, 1.0, 0.94)
SELF = {"sqk": (0.28,), "sv": (3.48,), "sqb": (0.67, 2.42), "sob": (8.36,), "sot": (9.79,), "sy": (10.8,),
        "sb": (11.46,), "sx": (12.47,)}
SELF_GROUP = {"ss": 2.01, "st": 3.08, "spv": 4.02}
FEED_STAGES = {"f1": 0.48, "f2": 1.7, "zf": 2.59, "zb": 3.99, "zn": 4.65, "zx": 4.74, "sc": 5.75, "rk": 6.76}
SEND = (40.92, 41.81, 45.97, 47.66, 55.71, 55.45, 56.62, 58.26)


def steps():
    due = []
    for u in range(B):
        due += [(FIRST_START[u] + lag, stage, u) for stage, lag in FIRST.items()]
        due += [(CONTEXT_START[u] + lag, stage, len(lags) * u + n) for stage, lags in CONTEXT.items() for n, lag in enumerate(lags)]
        due += [(NG * u + lag, stage, len(lags) * u + n) for stage, lags in CROSS.items() for n, lag in enumerate(lags)]
        due += [(SELF_START[u] + lag - (lag > NG and NG * (1 - SELF_PACE[u])), stage, len(lags) * u + n)
                for stage, lags in SELF.items() for n, lag in enumerate(lags)]
        due += [(SELF_START[u] + g * SELF_PACE[u] + lag, stage, u * NG + g) for stage, lag in SELF_GROUP.items() for g in range(NG)]
    for n in range(GROUPS):
        due += [(n + lag, "cs", n * HG + j) for j, lag in enumerate(HEADS)]
        due += [(n + lag, stage, len(lags) * n + k) for stage, lags in CROSS_GROUP.items() for k, lag in enumerate(lags)]
    for q, (batches, start) in enumerate(FEED):
        due += [(start + FEED_STAGES["f1"], "f1", q * FC + f) for f in range(FC)]
        due += [(start + j + lag, stage, u) for j, u in enumerate(batches) for stage, lag in FEED_STAGES.items() if stage != "f1"]
    due += [(start, "al", u) for u, start in enumerate(SEND)]
    return [(stage, i) for _, stage, i in sorted(due, key=lambda d: d[0])]


STEPS = steps()


def number(increments):
    count, before = 0, {}
    for stage in STEPS:
        if stage[0] in increments:
            before[stage] = count
            count += increments[stage[0]]
    return before, count


OUT, N_OUT = number(dict(aqk=2 * C, av=1, apv=1, ay=1, ax=1, ck=1, cv=1, cq=C, cpv=1, cob=1, cot=1, cy=1, cx=1,
                         sqk=2 * C, sv=1, spv=1, sob=1, sot=1, sy=1, sx=1, f2=1, zx=1, sc=1, rk=1))
SCORE, N_SCORE = number({"as": 1, "cs": 1, "ss": 1, "f1": 1})
PT, N_PT = number({"at": 1, "ct": 1, "st": 1})
OPENED, N_NORM = number(dict(ay=1, cy=1, sy=1, f2=1, zf=1))
FINISHED, _ = number(dict(ab=1, cb=1, sb=1, zf=1, zb=1))
FINISHES = dict(ay="ab", cy="cb", sy="sb", f2="zf", zf="zb")
PROBS, _ = number({"as": 1, "cs": 1, "ss": HG})
MASKED, _ = number({"cs": 1})
NEGMAX, _ = number({"as": 1, "ss": 1})
NORMED, _ = number({"at": 1})
SPREAD, _ = number({"cqb": 1, "sqb": 1})
RESID, _ = number(dict(ab=1, cb=1, sb=1))
HIDDEN, _ = number({"f1": 1})
KEPT, _ = number({"cq": 1})


def decoder_layer(nc, xT, xrow, ctxT, mask, weights, fi, fo, cols, rows, b2rows, moe, x_slots, x_more, out):
    ctx = ExitStack()
    with ctx:
        def sb(name, shape, dt=F32):
            return ctx.enter_context(nc.sbuf_tensor(name, shape, dt))

        def sem(name):
            return ctx.enter_context(nc.semaphore(name))

        MOE_WORDS = E * 2 * C * F
        ARENA = 48834
        arena = sb("arena", [128, ARENA])
        top = [0]

        def take(words):
            top[0] += words
            assert top[0] <= ARENA, top
            return arena[:, top[0] - words:top[0]]

        def ring(words, shape, n=2):
            names, sizes = shape
            return take(n * words).rearrange(f"p (r {' '.join(names)}) -> p r {' '.join(names)}", r=n, **dict(zip(names, sizes)))

        rows_T = (("c", "s"), (C, S))
        wA = take(4 * C * D).rearrange("p (w c n) -> p w c n", w=4, c=C)
        xT_sb = take(B * C * S).rearrange("p (b c s) -> p b c s", b=B, c=C)
        QTa, KTa, OTa = ring(C * S, rows_T), ring(C * S, rows_T), ring(C * S, rows_T)
        va = take(4 * D).rearrange("p (u v) -> p u v", u=4)
        probsA = take(2 * S).rearrange("p (r s) -> p r s", r=2)
        probsTA = take(2 * S).rearrange("p (r s) -> p r s", r=2)
        first_end = top[0]
        wC = take(4 * C * D).rearrange("p (w c n) -> p w c n", w=4, c=C)
        x1T = ring(C * S, rows_T, 4)
        QTc, OTc = ring(C * S, rows_T, 1), ring(C * S, rows_T, 1)
        keysT = take(2 * C * KX).rearrange("p (r c k) -> p r c k", r=2, c=C)
        context = take(2 * C * KX).rearrange("p (r c k) -> p r c k", r=2, c=C)
        values = take(2 * KC * VW).rearrange("p (r k v) -> p r k v", r=2, k=KC)
        masks = take(2 * KX).rearrange("p (r k) -> p r k", r=2)
        qheadsC = take(C * HB * S).rearrange("p (c h s) -> p c h s", c=C, h=HB)
        probsC = take(2 * HG * KX).rearrange("p (r k) -> p r k", r=2 * HG)
        probsTC = take(2 * KC * HG * S).rearrange("p (r k n) -> p r k n", r=2, k=KC)
        headsTC = take(2 * NG * S).rearrange("p (r g s) -> p r g s", r=2, g=NG)
        headsC = take(D)
        cross_end = top[0]
        wS = take(4 * C * D).rearrange("p (w c n) -> p w c n", w=4, c=C)
        x2T = ring(C * S, rows_T)
        QTs, KTs, OTs = ring(C * S, rows_T, 1), ring(C * S, rows_T), ring(C * S, rows_T, 1)
        vrows = take(2 * VW).rearrange("p (u v) -> p u v", u=2)
        qheadsS = take(C * HB * S).rearrange("p (c h s) -> p c h s", c=C, h=HB)
        probsS = take(2 * HG * S).rearrange("p (r k) -> p r k", r=2 * HG)
        probsTS = take(2 * HG * S).rearrange("p (r k n) -> p r k n", r=2, k=1)
        headsTS = take(2 * NG * S).rearrange("p (r g s) -> p r g s", r=2, g=NG)
        headsS = take(D)
        take(max(0, MOE_WORDS - top[0]))
        self_end = top[0]
        fi_sb = take(C * F).rearrange("p (c f) -> p c f", c=C)
        resid = take(B * D).rearrange("p (u d) -> p u d", u=B)
        ybuf = take(NR * D).rearrange("p (r d) -> p r d", r=NR)
        x3T = take(C * B * S).rearrange("p (c n) -> p c n", c=C)
        x5T = ring(C * S, rows_T)
        hiddenT = take(2 * FC * FN).rearrange("p (r f n) -> p r f n", r=2, f=FC)
        zero = arena[:, top[0] - 2 * XW:top[0]].rearrange("p (r w) -> p r w", r=2)
        fo_sb = take(FC * D).rearrange("p (f d) -> p f d", f=FC)
        spread = take(len(ROWS) * D).rearrange("p (r d) -> p r d", r=len(ROWS))
        R = {name: spread[0:S, i] for i, name in enumerate(ROWS)}
        W = {name: (wA, wC, wS)[i // 4][:, i % 4] for i, name in enumerate(WEIGHTS)}

        moe_w = arena[:, 0:MOE_WORDS].rearrange("p (e w) -> p e w", e=E)
        words = MOE_WORDS // E
        assert first_end >= words and cross_end >= 5 * words and self_end >= MOE_WORDS and E * D <= C * F, (first_end, cross_end, self_end)
        late = [MOE_WORDS]

        def take_late(words):
            late[0] += words
            assert late[0] <= ARENA
            return arena[:, late[0] - words:late[0]]

        b2_sb = take_late(E * D).rearrange("p (e d) -> p e d", e=E)
        xs = take_late(4 * XW).rearrange("p (r d) -> p r d", r=4)
        xsn = take_late(2 * D).rearrange("p (r d) -> p r d", r=2)
        xsT = take_late(2 * C * 128).rearrange("p (r c s) -> p r c s", r=2, c=C)
        w1_moved = take_late(2 * C * F).rearrange("p (r c f) -> p r c f", r=2, c=C)
        hidT = take_late(2 * F).rearrange("p (r f s) -> p r f s", r=2, f=FC)
        yrow = take_late(2 * D).rearrange("p (r d) -> p r d", r=2)
        ys = take_late(2 * D).rearrange("p (r d) -> p r d", r=2)

        xrows = sb("xrows", [128, B, XW])
        x1 = xrows[:, :, 0:D]
        consts = sb("consts", [128, NCOLS])
        ident = sb("ident", [128, 128])
        qmask = sb("qmask", [128, HB])
        negmax = {k: sb("negmax" + k, [128, B, h]) for k, h in (("a", 1), ("c", H), ("s", H))}
        sums = {k: sb("sums" + k, [128, B, h]) for k, h in (("a", 1), ("c", H), ("s", H))}
        recips = {k: sb("recips" + k, [128, B, h]) for k, h in (("a", 1), ("c", H), ("s", H))}
        stats = sb("stats", [128, NR, 6])
        stats5 = sb("stats5", [128, 6])
        meanvar = sb("meanvar", [128, NR, 2])
        vareps = sb("vareps", [128, NR, 1])
        rstd = sb("rstd", [128, NR, 1])
        scal = sb("scal", [128, 3])
        lower = sb("lower", [S, S])
        ones = sb("ones", [S, 128])
        rev = sb("rev", [128, E])
        token = sb("token", [128, B])
        first = sb("first", [128, B])
        best = sb("best", [128, B])
        ex = sb("ex", [128, B])
        marked = sb("marked", [128, E])
        onehot = sb("onehot", [128, B, E])
        chosen = sb("chosen", [128, B, E])
        ranked_for = sb("ranked_for", [128, E])
        rank = sb("rank", [128, B])
        ebase = sb("ebase", [128, B])
        spare = sb("spare", [128, 2, B])
        past = sb("past", [128, B])
        slotf = sb("slotf", [128, B])
        token_slot = sb("token_slot", [128, B], U32)
        token_slot2 = sb("token_slot2", [128, B], U32)
        thr = sb("thr", [128, E, EXTRA])
        over = sb("over", [128, E, EXTRA])
        nmore = sb("nmore", [128, E])
        ends = sb("ends", [128, E])
        base = sb("base", [128, E])
        rt = sb("rt", [128, B, E])
        tidx = sb("tidx", [128, EXTRA, E - 1])
        tge = sb("tge", [128, EXTRA, E - 1])
        tilef = sb("tilef", [128, EXTRA])
        tile_expert = sb("tile_expert", [128, EXTRA + 1], I32)
        tile_token = sb("tile_token", [128, TILES], U32)

        bank = [ctx.enter_context(nc.psum_tensor(f"bank{i}", [128, 512], F32)) for i in range(8)]
        score_bank, pt_bank, out_bank = bank[0:RS], bank[RS:RS + RP], bank[RS + RP:]

        def col(name, i=0, p=128):
            return consts[0:p, COLS[name] + i:COLS[name] + i + 1]

        w_first, w_second, w_third, w_cross, w_self, w_ffn = [sem(n) for n in "w_first w_second w_third w_cross w_self w_ffn".split()]
        consts_in, b4_in, rows_in, x_first_in, x_early_in, x_late_in, xrow_in, zero_in, moe_b2_in = [sem(n) for n in (
            "consts_in", "b4_in", "rows_in", "x_first_in", "x_early_in", "x_late_in", "xrow_in", "zero_in", "moe_b2_in")]
        ctx_in, mask_in = (sem("ctx_in0"), sem("ctx_in1")), (sem("mask_in0"), sem("mask_in1"))
        setup, setup_dve, pool_setup, biases_added = sem("setup"), sem("setup_dve"), sem("pool_setup"), sem("biases_added")
        (out_full, out_free, score_full, pt_full, pt_free, scores_masked, negmax_ready, probs_ready, probs_normed,
         qheads_ready, stats_ready, vareps_ready, rstd_ready, norm_done, resid_ready, x1_biased, hidden_ready,
         dve_chain, pool_chain) = [sem(n) for n in (
            "out_full out_free score_full pt_full pt_free scores_masked negmax_ready probs_ready probs_normed "
            "qheads_ready stats_ready vareps_ready rstd_ready norm_done resid_ready x1_biased hidden_ready "
            "dve_chain pool_chain").split()]
        (e_chain, x5_stats, x5_vareps, x5_rstd, best_ready, exped, alphaed, picked, placed, scattered, totals, more_placed,
         more_scattered, moe_in0, t_normed, t_xT_full, t_xT_ready, t_w1_moved, t_hid_full, t_hid_ready,
         t_y_full, t_y_added, t_stats, t_rstd, t_y_ready) = [sem(n) for n in (
            "e_chain x5_stats x5_vareps x5_rstd best_ready exped alphaed picked placed scattered totals more_placed "
            "more_scattered moe_in0 t_normed t_xT_full t_xT_ready t_w1_moved t_hid_full t_hid_ready "
            "t_y_full t_y_added t_stats t_rstd t_y_ready").split()]
        moe_in = [moe_in0] + [sem(f"moe_in{e}") for e in range(1, E)]
        y_sent = (sem("y_sent0"), sem("y_sent1"))
        tile_in = [sem(f"tile_in{i}") for i in range(4)]

        block = ctx.enter_context(nc.Block())

        score_release = []
        for stage in STEPS:
            if stage[0] in ("as", "cs", "ss", "f1"):
                score_release.append({"as": lambda: (probs_ready, PROBS[stage] + 1), "cs": lambda: (scores_masked, MASKED[stage] + 1),
                                      "ss": lambda: (probs_ready, PROBS[stage] + HG), "f1": lambda: (hidden_ready, HIDDEN[stage] + 1)}[stage[0]]())

        def all_probs(kind, n):
            return PROBS["cs", n * HG + HG - 1] + 1 if kind == "c" else PROBS["ss", n] + HG

        def group(n):
            u, g = divmod(n, NG)
            return u, g, g * HG // HB, (g * HG) % HB

        def further_tiles(engine, experts=True):
            engine.wait_ge(more_placed, 3)
            loaded = [engine.value_load(tile_expert[0:1, c:c + 1], min_val=0, max_val=E - 1)
                      for c in (*range(EXTRA if experts else 0), EXTRA)]
            return loaded[-1], loaded[:-1]

        def when_used(engine, used, j):
            return engine.If(used > j - E) if j >= E else nullcontext()

        @block.sync
        def _(sp):
            sp.dma_start(xT_sb[:, 0:1], xT[:, 0:1]).then_inc(x_first_in, 16)
            sp.dma_start(wA[:, 0:1], weights[:, 0:1]).then_inc(w_first, 16)
            sp.dma_start(wA[:, 1:2], weights[:, 1:2]).then_inc(w_second, 16)
            sp.dma_start(consts[:, :], cols).then_inc(consts_in, 16)
            sp.dma_start(xT_sb[:, 1:4], xT[:, 1:4]).then_inc(x_early_in, 16)
            sp.dma_start(wA[:, 2:4], weights[:, 2:4]).then_inc(w_third, 16)
            sp.dma_start(resid[0:S], xrow).then_inc(xrow_in, 16)
            for u in range(B):
                if u >= 2:
                    sp.wait_ge(out_full, 1 + max(OUT["ck", C * (u - 1) - 1], OUT["cv", KC * (u - 1) - 1]))
                sp.dma_start(context[:, u % 2], ctxT[u]).then_inc(ctx_in[u % 2], 16)
                if u >= 2:
                    sp.wait_ge(scores_masked, MASKED["cs", H * (u - 1) - 1] + 1)
                sp.dma_start(masks[0:S, u % 2], mask[u:u + 1].to_broadcast([S, KX])).then_inc(mask_in[u % 2], 16)
                if u == 0:
                    sp.dma_start(xT_sb[:, 4:8], xT[:, 4:8]).then_inc(x_late_in, 16)
                if u == 1:
                    sp.wait_ge(setup, 18)
                    for t in range(TILES):
                        dst = x_slots[t * 128:(t + 1) * 128, :] if t < E else x_more[(t - E) * 128:(t - E + 1) * 128, :]
                        sp.dma_start(dst, zero[:, t % 2]).then_inc(zero_in, 16)
                if u == B - 2:
                    sp.wait_ge(out_free, OUT["ax", B - 1] + 1)
                    sp.dma_start(moe_w[:, 0], moe[0]).then_inc(moe_in[0], 16)
            sp.wait_ge(out_free, OUT["cy", B - 1] + 1)
            for e in range(1, 5):
                sp.dma_start(moe_w[:, e], moe[e]).then_inc(moe_in[e], 16)
            sp.wait_ge(out_free, OUT["sy", B - 1] + 1)
            for e in range(5, E):
                sp.dma_start(moe_w[:, e], moe[e]).then_inc(moe_in[e], 16)
            sp.wait_ge(hidden_ready, FC * len(FEED))
            sp.dma_start(b2_sb.rearrange("p e d -> p (e d)"), b2rows.to_broadcast([128, E * D])).then_inc(moe_b2_in, 16)
            sp.wait_ge(out_free, N_OUT)
            sp.wait_ge(scattered, 16 * B)
            used = None
            for t in range(TILES):
                if t == E:
                    used, _ = further_tiles(sp, experts=False)
                    sp.wait_ge(more_scattered, 16 * B)
                with when_used(sp, used, t):
                    if t >= 4:
                        sp.wait_ge(t_stats, t - 3)
                    src = x_slots[t * 128:(t + 1) * 128, :] if t < E else x_more[(t - E) * 128:(t - E + 1) * 128, :]
                    sp.dma_start(xs[:, t % 4], src).then_inc(tile_in[t % 4], 16)

        @block.tensor
        def _(pe):
            mm = nc.tensor.matmul

            def out_slot(n):
                if n >= RO:
                    pe.wait_ge(out_free, n - RO + 1)
                return out_bank[n % RO]

            def score_slot(n):
                if n >= RS:
                    pe.wait_ge(*score_release[n - RS])
                return score_bank[n % RS]

            def pt_slot(n):
                if n >= RP:
                    pe.wait_ge(pt_free, n - RP + 1)
                return pt_bank[n % RP]

            def project_T(slot, w, m, src, n=S):
                dst = out_slot(slot)
                for k in range(C):
                    last = mm(dst[:, 0:n], w[:, k, m * 128:(m + 1) * 128], src[:, k], start=k == 0, stop=k == C - 1)
                last.then_inc(out_full, 1)

            def project_rows(slot, src, w, rows=S):
                dst = out_slot(slot)
                for k in range(C):
                    last = mm(dst[0:rows, 0:D], src[:, k], w[:, k], start=k == 0, stop=k == C - 1)
                last.then_inc(out_full, 1)

            def transposed_rows(slot, src):
                dst = out_slot(slot)
                for m in range(C):
                    last = nc.tensor.transpose(dst[:, m * S:(m + 1) * S], src[:, m * 128:(m + 1) * 128], ident[0:S, 0:S])
                last.then_inc(out_full, 1)

            pe.wait_ge(setup, 1)
            for stage, i in STEPS:
                kind, slot = stage[0], OUT.get((stage, i))
                if stage == "aqk":
                    if i == 0:
                        pe.wait_ge(w_first, 16)
                    pe.wait_ge(x_first_in if i == 0 else x_early_in if i < 4 else x_late_in, 16)
                    for q, w in enumerate(("W1", "W2")):
                        if i == 0 and q == 1:
                            pe.wait_ge(w_second, 16)
                        for m in range(C):
                            project_T(slot + q * C + m, W[w], m, xT_sb[:, i])
                elif stage == "av":
                    if i == 0:
                        pe.wait_ge(w_third, 16)
                    project_rows(slot, xT_sb[:, i], W["W3"])
                elif stage == "as":
                    pe.wait_ge(out_free, OUT["aqk", i] + 2 * C)
                    dst = score_slot(SCORE[stage, i])
                    for k in range(C):
                        last = mm(dst[0:S, 0:S], QTa[:, i % 2, k], KTa[:, i % 2, k], start=k == 0, stop=k == C - 1)
                    last.then_inc(score_full, 1)
                elif stage == "at":
                    dst = pt_slot(PT[stage, i])
                    pe.wait_ge(probs_normed, NORMED[stage, i] + 1)
                    nc.tensor.transpose(dst[0:S, 0:S], probsA[0:S, i % 2], ident[0:S, 0:S]).then_inc(pt_full, 1)
                elif stage == "apv":
                    dst = out_slot(slot)
                    pe.wait_ge(pt_free, PT["at", i] + 1)
                    pe.wait_ge(out_free, OUT["av", i] + 1)
                    for m in range(C):
                        last = mm(dst[:, m * S:(m + 1) * S], va[0:S, i % 4, m * 128:(m + 1) * 128], probsTA[0:S, i % 2],
                                  start=True, stop=True)
                    last.then_inc(out_full, 1)
                elif stage in ("ay", "cy", "sy"):
                    of, src = {"a": ("apv", OTa), "c": ("cot", OTc), "s": ("sot", OTs)}[kind]
                    pe.wait_ge(out_free, OUT[of, i] + 1)
                    project_rows(slot, src[:, i % 2 if kind == "a" else 0], W[{"a": "W4", "c": "co", "s": "so"}[kind]])
                elif stage in ("ax", "cx", "sx", "zx"):
                    opened = {"a": "ay", "c": "cy", "s": "sy", "z": "zf"}[kind]
                    pe.wait_ge(norm_done, FINISHED[FINISHES[opened], i] + 1)
                    transposed_rows(slot, x1[0:S, i] if kind in "az" else ybuf[0:S, OPENED[opened, i] % NR])
                elif stage == "ck":
                    u, m = divmod(i, C)
                    if i == 0:
                        pe.wait_ge(w_cross, 16)
                    pe.wait_ge(ctx_in[u % 2], 16 * (u // 2 + 1))
                    project_T(slot, W["ck"], m, context[:, u % 2], KX)
                elif stage == "cv":
                    u, c = divmod(i, KC)
                    pe.wait_ge(ctx_in[u % 2], 16 * (u // 2 + 1))
                    project_rows(slot, context[:, u % 2, :, c * KP:(c + 1) * KP], W["cv"], KP)
                elif stage == "cq":
                    pe.wait_ge(out_free, OUT["ax", i] + 1)
                    for m in range(C):
                        project_T(slot + m, W["cq"], m, x1T[:, i % 4])
                elif stage == "sqk":
                    if i == 0:
                        pe.wait_ge(w_self, 16)
                    pe.wait_ge(out_free, OUT["cx", i] + 1)
                    for q, w in enumerate(("sq", "sk")):
                        for m in range(C):
                            project_T(slot + q * C + m, W[w], m, x2T[:, i % 2])
                elif stage == "sv":
                    project_rows(slot, x2T[:, i % 2], W["sv"])
                elif stage == "cs":
                    u, at = divmod(i, H)
                    m, h = divmod(at, HB)
                    if at % HG == 0:
                        pe.wait_ge(qheads_ready, SPREAD["cqb", C * u + m] + 1)
                        pe.wait_ge(out_free, OUT["ck", C * u + C - 1] + 1)
                    dst = score_slot(SCORE[stage, i])
                    mm(dst[0:S, 0:KX], qheadsC[:, m, h], keysT[:, u % 2, m], start=True, stop=True).then_inc(score_full, 1)
                elif stage == "ss":
                    u, g, m, h = group(i)
                    pe.wait_ge(qheads_ready, SPREAD["sqb", C * u + m] + 1)
                    dst = score_slot(SCORE[stage, i])
                    for j in range(HG):
                        last = mm(dst[0:S, j * S:(j + 1) * S], qheadsS[:, m, h + j], KTs[:, u % 2, m], start=True, stop=True)
                    last.then_inc(score_full, 1)
                elif stage in ("ct", "st"):
                    kc, kp, probs = (KC, KP, probsC) if kind == "c" else (1, S, probsS)
                    n, c = divmod(i, kc)
                    dst = pt_slot(PT[stage, i])
                    if c == 0:
                        pe.wait_ge(probs_ready, all_probs(kind, n))
                    for j in range(HG):
                        last = nc.tensor.transpose(dst[0:kp, j * S:(j + 1) * S],
                                                   probs[0:S, (n % 2) * HG + j, c * kp:(c + 1) * kp], ident[0:S, 0:S])
                    last.then_inc(pt_full, 1)
                elif stage in ("cpv", "spv"):
                    u, g = divmod(i, NG)
                    kc, kp, probsT = (KC, KP, probsTC) if kind == "c" else (1, S, probsTS)
                    dst = out_slot(slot)
                    pe.wait_ge(pt_free, PT[kind + "t", kc * i + kc - 1] + 1)
                    pe.wait_ge(out_free, OUT["cv", KC * u + KC - 1] + 1 if kind == "c" else OUT["sv", u] + 1)
                    for c in range(kc):
                        for j in range(HG):
                            v = values[0:kp, u % 2, c] if kind == "c" else vrows[0:kp, u % 2]
                            at = (g * HG + j) * HD
                            last = mm(dst[32 * j:32 * j + 32, 0:S], v[:, at:at + 32], probsT[0:kp, i % 2, c, j * S:(j + 1) * S],
                                      start=c == 0, stop=c == kc - 1)
                    last.then_inc(out_full, 1)
                elif stage in ("cob", "sob"):
                    pe.wait_ge(out_free, OUT[kind + "pv", NG * i + NG - 1] + 1)
                    dst = out_slot(slot)
                    headsT = headsTC if kind == "c" else headsTS
                    for g in range(NG):
                        last = nc.tensor.transpose(dst[0:S, g * 128:(g + 1) * 128], headsT[:, i % 2, g], ident[:, :])
                    last.then_inc(out_full, 1)
                elif stage in ("cot", "sot"):
                    pe.wait_ge(out_free, OUT[kind + "ob", i] + 1)
                    transposed_rows(slot, (headsC if kind == "c" else headsS)[0:S])
                elif stage == "f1":
                    q, f = divmod(i, FC)
                    batches = FEED[q][0]
                    if f == 0:
                        if q == 0:
                            pe.wait_ge(w_ffn, 32)
                        pe.wait_ge(out_free, OUT["sx", batches[-1]] + 1)
                    n = len(batches) * S
                    dst = score_slot(SCORE[stage, i])
                    for k in range(C):
                        last = mm(dst[:, 0:n], fi_sb[:, k, f * 128:(f + 1) * 128], x3T[:, k, batches[0] * S:batches[0] * S + n],
                                  start=k == 0, stop=k == C - 1)
                    last.then_inc(score_full, 1)
                elif stage == "f2":
                    q = next(q for q, (batches, _) in enumerate(FEED) if i in batches)
                    j = i - FEED[q][0][0]
                    pe.wait_ge(hidden_ready, FC * (q + 1))
                    dst = out_slot(slot)
                    for f in range(FC):
                        last = mm(dst[0:S, 0:D], hiddenT[:, q % 2, f, j * S:(j + 1) * S], fo_sb[:, f], start=f == 0, stop=f == FC - 1)
                    last.then_inc(out_full, 1)
                elif stage == "sc":
                    pe.wait_ge(out_free, OUT["zx", i] + 1)
                    dst = out_slot(slot)
                    for k in range(C):
                        last = mm(dst[0:S, 0:E], x5T[:, i % 2, k], consts[:, COLS["cent"] + k * E:COLS["cent"] + (k + 1) * E],
                                  start=k == 0, stop=k == C - 1)
                    last.then_inc(out_full, 1)
                elif stage == "rk":
                    pe.wait_ge(picked, i + 1)
                    dst = out_slot(slot)
                    if i:
                        mm(dst[0:S, 0:E], ones[:, 0:S], chosen[0:S, i - 1], start=True, stop=False)
                    mm(dst[0:S, 0:E], lower[:, :], onehot[0:S, i], start=i == 0, stop=True).then_inc(out_full, 1)

            pe.wait_ge(out_free, N_OUT)
            mm(bank[7][:, 0:E], ones[:, :], chosen[0:S, B - 1], start=True, stop=True).then_inc(totals, 1)

            expert, used = list(range(E)), None
            for t in range(-1, TILES + 1):
                j = t + 1
                if j == E:
                    used, more = further_tiles(pe)
                    expert += more
                if j < TILES:
                    with when_used(pe, used, j):
                        pe.wait_ge(t_normed, j + 1)
                        if j >= 2:
                            pe.wait_ge(t_xT_ready, j - 1)
                        for c in range(C):
                            last = nc.tensor.transpose(bank[4 + j % 2][:, c * 128:(c + 1) * 128],
                                                       xsn[:, j % 2, c * 128:(c + 1) * 128], ident[:, :])
                        last.then_inc(t_xT_full, 1)
                j = t
                if 0 <= j < TILES:
                    with when_used(pe, used, j):
                        if j < E:
                            pe.wait_ge(moe_in[j], 16)
                        pe.wait_ge(t_xT_ready, j + 1)
                        if j >= 2:
                            pe.wait_ge(t_hid_ready, 2 * (j - 1))
                        if j < E:
                            w1 = moe_w[:, j, 0:C * F].rearrange("p (c f) -> p c f", c=C)
                        else:
                            pe.wait_ge(t_w1_moved, j - E + 1)
                            w1 = w1_moved[:, j % 2]
                        for f in range(FC):
                            for c in range(C):
                                last = mm(bank[2 * (j % 2) + f // 4][:, f % 4 * 128:(f % 4 + 1) * 128],
                                          w1[:, c, f * 128:(f + 1) * 128], xsT[:, j % 2, c], start=c == 0, stop=c == C - 1)
                            if f % 4 == 3:
                                last.then_inc(t_hid_full, 1)
                j = t - 1
                if 0 <= j < TILES:
                    with when_used(pe, used, j):
                        pe.wait_ge(t_hid_ready, 2 * (j + 1))
                        if j == 1:
                            pe.wait_ge(more_placed, 1)
                        if j >= 2:
                            pe.wait_ge(t_y_added, j - 1)
                        w2 = moe_w[:, bass.ds(expert[j], 1), C * F:].rearrange("p e (f d) -> p (e f) d", f=FC)
                        for f in range(FC):
                            last = mm(bank[6 + j % 2][:, 0:D], hidT[:, j % 2, f], w2[:, f], start=f == 0, stop=f == FC - 1)
                        last.then_inc(t_y_full, 1)

        @block.vector
        def _(dve):
            v = nc.vector
            chain = [0]

            def link(ins):
                chain[0] += 1
                ins.then_inc(dve_chain, 1)

            def linked():
                dve.wait_ge(dve_chain, chain[0])

            dve.wait_ge(setup, 1)
            v.reduce_sum(qmask[:, :], ident[:, :].rearrange("p (h d) -> p h d", d=HD), axis=AX.X).then_inc(setup_dve, 1)
            dve.wait_ge(setup_dve, 1)
            v.tensor_scalar(qmask[:, :], qmask[:, :], 1.0 / HD ** 0.5, None, ALU.mult).then_inc(setup_dve, 1)
            dve.wait_ge(setup, 6)
            dve.wait_ge(consts_in, 16)

            def full(n):
                dve.wait_ge(out_full, n + 1)
                return out_bank[n % RO]

            def open_norm(stage, i):
                k = OPENED[stage, i]
                if k >= NR:
                    was, wi = next(s for s, n in OPENED.items() if n == k - NR)
                    dve.wait_ge(norm_done, FINISHED[FINISHES[was], wi] + 1)
                    if was in ("cy", "sy"):
                        dve.wait_ge(out_full, OUT[was[0] + "x", wi] + 1)
                        dve.wait_ge(resid_ready, B + RESID[was[0] + "b", wi] + 1)
                return k

            def take_stats(k):
                v.bn_stats(stats[0:S, k % NR], ybuf[0:S, k % NR]).then_inc(dve_chain, 1)
                chain[0] += 1
                linked()
                v.bn_aggr(meanvar[0:S, k % NR], stats[0:S, k % NR]).then_inc(stats_ready, 1)

            for stage, i in STEPS:
                kind, slot = stage[0], OUT.get((stage, i))
                if stage in ("aqk", "sqk"):
                    q, kk, bq, bk = (QTa, KTa, "b1", "b2") if kind == "a" else (QTs, KTs, "sqb", "skb")
                    for n, (dst, bias) in enumerate(((q, bq), (kk, bk))):
                        for m in range(C):
                            src = full(slot + n * C + m)
                            if kind == "a" and n == 0:
                                v.tensor_scalar(dst[:, i % 2, m], src[:, 0:S], col(bias, m), 1.0 / D ** 0.5, ALU.add, ALU.mult)\
                                    .then_inc(out_free, 1)
                            else:
                                v.tensor_scalar(dst[:, i % 2 if dst is not QTs else 0, m], src[:, 0:S], col(bias, m), None, ALU.add).then_inc(out_free, 1)
                elif stage in ("av", "sv"):
                    src = full(slot)
                    dst = va[0:S, i % 4] if kind == "a" else vrows[0:S, i % 2, 0:D]
                    v.tensor_copy(dst, src[0:S, 0:D]).then_inc(out_free, 1)
                elif stage == "as":
                    s = SCORE[stage, i]
                    dve.wait_ge(score_full, s + 1)
                    v.tensor_reduce(negmax["a"][0:S, i], score_bank[s % RS][0:S, 0:S], AX.X, ALU.max, negate=True)\
                        .then_inc(negmax_ready, 1)
                elif stage == "at":
                    dve.wait_ge(probs_ready, PROBS["as", i] + 1)
                    link(v.reciprocal(recips["a"][0:S, i], sums["a"][0:S, i]))
                    linked()
                    v.tensor_scalar(probsA[0:S, i % 2], probsA[0:S, i % 2], recips["a"][0:S, i], None, ALU.mult)\
                        .then_inc(probs_normed, 1)
                elif stage in ("apv", "cot", "sot"):
                    src = full(slot)
                    dst, bias = {"a": (OTa, "b3"), "c": (OTc, "cvb"), "s": (OTs, "svb")}[kind]
                    r = i % 2 if kind == "a" else 0
                    v.tensor_scalar(dst[:, r, 0], src[:, 0:S], col(bias, 0), None, ALU.add)
                    v.tensor_scalar(dst[:, r, 1], src[:, S:2 * S], col(bias, 1), None, ALU.add).then_inc(out_free, 1)
                elif stage in ("ay", "cy", "sy", "f2"):
                    k = open_norm(stage, i)
                    src = full(slot)
                    made = {"ay": lambda: i, "cy": lambda: B + RESID["ab", i], "sy": lambda: B + RESID["cb", i],
                            "f2": lambda: B + RESID["sb", i]}[stage]()
                    dve.wait_ge(resid_ready, made + 1)
                    v.tensor_tensor(ybuf[0:S, k % NR], src[0:S, 0:D], resid[0:S, i], ALU.add).then_inc(out_free, 1)
                    dve.wait_ge(out_free, slot + 1)
                    take_stats(k)
                elif stage in ("ab", "cb", "sb", "zb"):
                    k = OPENED[{"a": "ay", "c": "cy", "s": "sy", "z": "zf"}[kind], i]
                    dve.wait_ge(rstd_ready, k + 1)
                    dst = x1[0:S, i] if kind in "az" else ybuf[0:S, k % NR]
                    v.tensor_scalar(dst, ybuf[0:S, k % NR], meanvar[0:S, k % NR, 0:1], rstd[0:S, k % NR], ALU.subtract, ALU.mult)\
                        .then_inc(norm_done, 1)
                elif stage in ("ax", "zx"):
                    src = full(slot)
                    dst = x1T[:, i % 4] if kind == "a" else x5T[:, i % 2]
                    v.tensor_copy(dst, src[:, 0:2 * S].rearrange("p (c s) -> p c s", c=C)).then_inc(out_free, 1)
                elif stage in ("cx", "sx"):
                    src = full(slot)
                    gain, shift = ("cog", "cobe") if kind == "c" else ("sog", "sobe")
                    for c in range(C):
                        dst = x2T[:, i % 2, c] if kind == "c" else x3T[:, c, i * S:(i + 1) * S]
                        last = v.tensor_scalar(dst, src[:, c * S:(c + 1) * S], col(gain, c), col(shift, c), ALU.mult, ALU.add)
                    last.then_inc(out_free, 1)
                elif stage == "ck":
                    u, m = divmod(i, C)
                    v.tensor_scalar(keysT[:, u % 2, m], full(slot)[:, 0:KX], col("ckb", m), None, ALU.add).then_inc(out_free, 1)
                elif stage == "cv":
                    u, c = divmod(i, KC)
                    v.tensor_copy(values[0:KP, u % 2, c, 0:D], full(slot)[0:KP, 0:D]).then_inc(out_free, 1)
                elif stage == "cq":
                    for m in range(C):
                        src = full(slot + m)
                        v.tensor_scalar(QTc[:, 0, m], src[:, 0:S], col("cqb", m), None, ALU.add).then_inc(out_free, 1)
                elif stage in ("cqb", "sqb"):
                    u, m = divmod(i, C)
                    dve.wait_ge(out_free, OUT["cq", u] + C if kind == "c" else OUT["sqk", u] + C)
                    if u >= 1:
                        n = NG * (u - 1) + NG // C * (m + 1) - 1
                        dve.wait_ge(score_full, (SCORE["cs", n * HG + HG - 1] if kind == "c" else SCORE["ss", n]) + 1)
                    q, dst = (QTc, qheadsC) if kind == "c" else (QTs, qheadsS)
                    v.tensor_tensor(dst[:, m], q[:, 0, m:m + 1].to_broadcast([128, HB, S]),
                                    qmask[:, :].unsqueeze(2).to_broadcast([128, HB, S]), ALU.mult).then_inc(qheads_ready, 1)
                elif stage == "cs":
                    (u, at), n = divmod(i, H), i // HG
                    if at == 0:
                        dve.wait_ge(mask_in[u % 2], 16 * (u // 2 + 1))
                    if n >= 2:
                        dve.wait_ge(pt_full, PT["ct", KC * (n - 1) - 1] + 1)
                    slot = SCORE[stage, i]
                    dve.wait_ge(score_full, slot + 1)
                    v.tensor_tensor_reduce(out=probsC[0:S, i % (2 * HG)], in0=score_bank[slot % RS][0:S, 0:KX], in1=masks[0:S, u % 2],
                                           scale=-1.0, scalar=3.0e38, op0=ALU.add, op1=ALU.min,
                                           accum_out=negmax["c"][0:S, u, at:at + 1]).then_inc(scores_masked, 1)
                elif stage == "ss":
                    u, g, m, h = group(i)
                    s = SCORE[stage, i]
                    dve.wait_ge(score_full, s + 1)
                    v.tensor_reduce(negmax["s"][0:S, u, g * HG:(g + 1) * HG],
                                    score_bank[s % RS][0:S, 0:HG * S].rearrange("p (j s) -> p j s", j=HG), AX.X, ALU.max,
                                    negate=True).then_inc(negmax_ready, 1)
                elif stage in ("cpv", "spv"):
                    u, g = divmod(i, NG)
                    src = full(slot)
                    v.tensor_copy((headsTC if kind == "c" else headsTS)[:, u % 2, g], src[:, 0:S]).then_inc(out_free, 1)
                elif stage in ("cob", "sob"):
                    src = full(slot)
                    dve.wait_ge(probs_ready, all_probs(kind, NG * i + NG - 1))
                    link(v.reciprocal(recips[kind][0:S, i], sums[kind][0:S, i]))
                    linked()
                    v.tensor_tensor((headsC if kind == "c" else headsS)[0:S].rearrange("p (h d) -> p h d", d=HD),
                                    src[0:S, :].rearrange("p (h d) -> p h d", d=2 * HD)[:, :, 0:HD],
                                    recips[kind][0:S, i].unsqueeze(2).to_broadcast([S, H, HD]), ALU.mult).then_inc(out_free, 1)
                elif stage == "zf":
                    kf = OPENED["f2", i]
                    dve.wait_ge(rstd_ready, kf + 1)
                    k = open_norm(stage, i)
                    link(v.scalar_tensor_tensor(ybuf[0:S, kf % NR], ybuf[0:S, kf % NR], meanvar[0:S, kf % NR, 0:1], R["fog"],
                                                ALU.subtract, ALU.mult))
                    linked()
                    dve.wait_ge(x1_biased, KEPT["cq", i] + 1)
                    v.scalar_tensor_tensor(ybuf[0:S, k % NR], ybuf[0:S, kf % NR], rstd[0:S, kf % NR], x1[0:S, i],
                                           ALU.mult, ALU.add).then_inc(norm_done, 1)
                    dve.wait_ge(norm_done, FINISHED[stage, i] + 1)
                    take_stats(k)
                elif stage == "zn":
                    dve.wait_ge(norm_done, FINISHED["zb", i] + 1)
                    if i:
                        dve.wait_ge(x5_stats, i)
                    link(v.bn_stats(stats5[0:S], x1[0:S, i]))
                    linked()
                    v.bn_aggr(xrows[0:S, i, MEAN:MEAN + 2], stats5[0:S]).then_inc(x5_stats, 1)
                elif stage == "sc":
                    src = full(slot)
                    if i == 0:
                        dve.wait_ge(setup, 18)
                    v.tensor_reduce(best[0:S, i:i + 1], src[0:S, 0:E], AX.X, ALU.max).then_inc(best_ready, 1)
                    dve.wait_ge(best_ready, i + 1)
                    v.scalar_tensor_tensor(marked[0:S], src[0:S, 0:E], best[0:S, i:i + 1], rev[0:S], ALU.is_equal, ALU.mult)\
                        .then_inc(out_free, 1)
                    dve.wait_ge(out_free, slot + 1)
                    link(v.tensor_reduce(first[0:S, i:i + 1], marked[0:S], AX.X, ALU.max))
                    linked()
                    link(v.tensor_scalar(onehot[0:S, i], marked[0:S], first[0:S, i:i + 1], None, ALU.is_equal))
                    linked()
                    if i:
                        v.tensor_tensor(chosen[0:S, i], chosen[0:S, i - 1], onehot[0:S, i], ALU.add).then_inc(picked, 1)
                    else:
                        v.tensor_copy(chosen[0:S, i], onehot[0:S, i]).then_inc(picked, 1)
                    link(v.tensor_scalar(ebase[0:S, i:i + 1], first[0:S, i:i + 1], -128.0, 128.0 * E, ALU.mult, ALU.add))
                elif stage == "al":
                    dve.wait_ge(exped, i + 1)
                    link(v.tensor_scalar(ex[0:S, i:i + 1], ex[0:S, i:i + 1], 1.0, 2.0, ALU.add, ALU.mult))
                    linked()
                    v.reciprocal(xrows[0:S, i, ALPHA:ALPHA + 1], ex[0:S, i:i + 1]).then_inc(alphaed, 1)
                elif stage == "rk":
                    src = full(slot)
                    v.tensor_tensor_reduce(out=ranked_for[0:S], in0=src[0:S, 0:E], in1=onehot[0:S, i], scale=1.0, scalar=0.0,
                                           op0=ALU.mult, op1=ALU.add, accum_out=rank[0:S, i:i + 1]).then_inc(out_free, 1)
                    dve.wait_ge(out_free, slot + 1)
                    link(v.tensor_scalar(past[0:S, i:i + 1], rank[0:S, i:i + 1], 127.5, FAR, ALU.is_gt, ALU.mult))
                    linked()
                    link(v.scalar_tensor_tensor(slotf[0:S, i:i + 1], rank[0:S, i:i + 1], ebase[0:S, i:i + 1], past[0:S, i:i + 1],
                                                ALU.add, ALU.max))
                    linked()
                    v.tensor_scalar(token_slot[0:S, i:i + 1], slotf[0:S, i:i + 1], spare[0:S, 0, i:i + 1], None, ALU.min).then_inc(placed, 1)
            dve.wait_ge(out_free, N_OUT)

            def place_rest():
                ec = [0]

                def elink(ins):
                    ec[0] += 1
                    ins.then_inc(e_chain, 1)
                    dve.wait_ge(e_chain, ec[0])

                dve.wait_ge(totals, 1)
                v.tensor_tensor(over[:, :, :], bank[7][:, 0:E].unsqueeze(2).to_broadcast([128, E, EXTRA]), thr[:, :, :], ALU.is_gt)\
                    .then_inc(more_placed, 1)
                dve.wait_ge(more_placed, 1)
                elink(v.reduce_sum(nmore[:, :], over[:, :, :], axis=AX.X))
                elink(v.tensor_copy(ends[:, 0:1], nmore[:, 0:1]))
                for e in range(1, E):
                    elink(v.tensor_tensor(ends[:, e:e + 1], ends[:, e - 1:e], nmore[:, e:e + 1], ALU.add))
                elink(v.tensor_tensor(base[:, :], ends[:, :], nmore[:, :], ALU.subtract))
                elink(v.tensor_scalar(base[:, :], base[:, :], 128.0, -128.0, ALU.mult, ALU.add))
                elink(v.tensor_tensor(rt[0:S], onehot[0:S], base[0:S].unsqueeze(1).to_broadcast([S, B, E]), ALU.mult))
                elink(v.reduce_sum(slotf[0:S], rt[0:S], axis=AX.X))
                elink(v.tensor_tensor(slotf[0:S], slotf[0:S], rank[0:S], ALU.add))
                elink(v.tensor_scalar(past[0:S], rank[0:S], 127.5, FAR, ALU.is_lt, ALU.mult))
                elink(v.tensor_tensor(slotf[0:S], slotf[0:S], past[0:S], ALU.max))
                v.tensor_tensor(token_slot2[0:S], slotf[0:S], spare[0:S, 1], ALU.min).then_inc(more_placed, 1)
                elink(v.tensor_tensor(tge[:, :, :], tidx[:, :, :], ends[:, 0:E - 1].unsqueeze(1).to_broadcast([128, EXTRA, E - 1]),
                                      ALU.is_ge))
                elink(v.reduce_sum(tilef[:, :], tge[:, :, :], axis=AX.X))
                v.tensor_copy(tile_expert[:, EXTRA:], ends[:, E - 1:])
                v.tensor_copy(tile_expert[:, 0:EXTRA], tilef[:, :]).then_inc(more_placed, 1)

            expert = list(range(E))

            def normalise_tile(j):
                dve.wait_ge(tile_in[j % 4], 16 * (j // 4 + 1))
                x = xs[:, j % 4]
                if j >= 2:
                    dve.wait_ge(t_xT_full, j - 1)
                v.tensor_scalar(xsn[:, j % 2], x[:, 0:D], x[:, MEAN:MEAN + 1], x[:, RSTD:RSTD + 1], ALU.subtract, ALU.mult)\
                    .then_inc(t_normed, 1)
                v.tensor_copy(tile_token[:, j:j + 1], x[:, TOKEN:TOKEN + 1])

            def gain_tile(j):
                dve.wait_ge(t_xT_full, j + 1)
                if j >= 2:
                    dve.wait_ge(t_hid_full, 2 * (j - 1))
                for c in range(C):
                    g = consts[:, bass.ds(expert[j] * C + COLS["gamma"] + c, 1)]
                    b = consts[:, bass.ds(expert[j] * C + COLS["beta"] + c, 1)]
                    last = v.tensor_scalar(xsT[:, j % 2, c], bank[4 + j % 2][:, c * 128:(c + 1) * 128], g, b, ALU.mult, ALU.add)
                last.then_inc(t_xT_ready, 1)
                if j >= E:
                    if j == E:
                        dve.wait_ge(moe_in[E - 1], 16)
                    v.tensor_copy(w1_moved[:, j % 2].rearrange("p c f -> p (c f)"),
                                  moe_w[:, bass.ds(expert[j], 1), 0:C * F].rearrange("p e w -> p (e w)")).then_inc(t_w1_moved, 1)

            def add_tile(j):
                if j == 0:
                    dve.wait_ge(moe_b2_in, 16)
                if j >= 2:
                    dve.wait_ge(t_y_ready, j - 1)
                dve.wait_ge(t_y_full, j + 1)
                v.tensor_tensor(yrow[:, j % 2], bank[6 + j % 2][:, 0:D],
                                b2_sb[:, bass.ds(expert[j], 1)].rearrange("p e d -> p (e d)"), ALU.add).then_inc(t_y_added, 1)
                dve.wait_ge(t_y_added, j + 1)
                link(v.scalar_tensor_tensor(yrow[:, j % 2], yrow[:, j % 2], xs[:, j % 4, ALPHA:ALPHA + 1], xs[:, j % 4, 0:D],
                                            ALU.mult, ALU.add))
                linked()
                link(v.bn_stats(stats[:, j % NR], yrow[:, j % 2]))
                linked()
                v.bn_aggr(meanvar[:, j % NR], stats[:, j % NR]).then_inc(t_stats, 1)

            def finish_tile(j):
                dve.wait_ge(t_rstd, j + 1)
                if j >= 2:
                    dve.wait_ge(y_sent[j % 2], 16 * (j // 2))
                v.tensor_scalar(ys[:, j % 2], yrow[:, j % 2], meanvar[:, j % NR, 0:1], rstd[:, j % NR], ALU.subtract, ALU.mult)\
                    .then_inc(t_y_ready, 1)

            normalise_tile(0)
            normalise_tile(1)
            used = None
            for t in range(-1, TILES + 2):
                for j, step in ((t + 1, gain_tile), (t + 2 if t >= 0 else -1, normalise_tile), (t - 2, finish_tile), (t - 1, add_tile)):
                    if 0 <= j < TILES:
                        with when_used(dve, used, j):
                            step(j)
                if t == 0:
                    place_rest()
                    used, more = further_tiles(dve)
                    expert += more

        @block.scalar
        def _(act):
            a = nc.scalar
            act.wait_ge(w_first, 16)
            act.dma_start(R["b4"], rows[:, 0:D].to_broadcast([S, D])).then_inc(b4_in, 16)
            act.dma_start(wC, weights[:, 4:8]).then_inc(w_cross, 16)
            act.dma_start(spread[0:S, 1:].rearrange("p r d -> p (r d)"), rows[:, D:].to_broadcast([S, (len(ROWS) - 1) * D]))\
                .then_inc(rows_in, 16)
            act.dma_start(wS, weights[:, 8:12]).then_inc(w_self, 16)
            act.dma_start(fi_sb, fi).then_inc(w_ffn, 16)
            act.dma_start(fo_sb, fo).then_inc(w_ffn, 16)
            act.wait_ge(consts_in, 16)
            for stage, i in STEPS:
                kind = stage[0]
                if stage == "as":
                    if i >= 2:
                        act.wait_ge(pt_full, PT["at", i - 2] + 1)
                    act.wait_ge(negmax_ready, NEGMAX[stage, i] + 1)
                    a.activation(probsA[0:S, i % 2], score_bank[SCORE[stage, i] % RS][0:S, 0:S], ACT.Exp,
                                 bias=negmax["a"][0:S, i], accum_out=sums["a"][0:S, i]).then_inc(probs_ready, 1)
                elif stage == "at":
                    if i >= 2:
                        act.wait_ge(out_full, OUT["apv", i - 2] + 1)
                    act.wait_ge(pt_full, PT[stage, i] + 1)
                    a.activation(probsTA[0:S, i % 2], pt_bank[PT[stage, i] % RP][0:S, 0:S], ACT.Copy).then_inc(pt_free, 1)
                elif stage == "cs":
                    u, at = divmod(i, H)
                    act.wait_ge(scores_masked, MASKED[stage, i] + 1)
                    a.activation(probsC[0:S, i % (2 * HG)], probsC[0:S, i % (2 * HG)], ACT.Exp, bias=negmax["c"][0:S, u, at:at + 1],
                                 scale=-1.0, accum_out=sums["c"][0:S, u, at:at + 1]).then_inc(probs_ready, 1)
                elif stage == "ss":
                    u, g, m, h = group(i)
                    if i >= 2:
                        act.wait_ge(pt_full, PT["st", i - 2] + 1)
                    act.wait_ge(negmax_ready, NEGMAX[stage, i] + 1)
                    for j in range(HG):
                        at = g * HG + j
                        a.activation(probsS[0:S, (i % 2) * HG + j], score_bank[SCORE[stage, i] % RS][0:S, j * S:(j + 1) * S], ACT.Exp,
                                     bias=negmax["s"][0:S, u, at:at + 1], accum_out=sums["s"][0:S, u, at:at + 1])\
                            .then_inc(probs_ready, 1)
                elif stage in ("ct", "st"):
                    kc, kp, probsT = (KC, KP, probsTC) if kind == "c" else (1, S, probsTS)
                    n, c = divmod(i, kc)
                    if n >= 2 and c == 0:
                        act.wait_ge(out_full, OUT[kind + "pv", n - 2] + 1)
                    act.wait_ge(pt_full, PT[stage, i] + 1)
                    a.activation(probsT[0:kp, n % 2, c], pt_bank[PT[stage, i] % RP][0:kp, 0:HG * S], ACT.Copy).then_inc(pt_free, 1)
                elif stage == "f1":
                    q, f = divmod(i, FC)
                    if f == 0 and q == 0:
                        act.wait_ge(zero_in, 16 * TILES)
                    elif f == 0 and q >= 2:
                        act.wait_ge(out_full, OUT["f2", FEED[q - 2][0][-1]] + 1)
                    n = len(FEED[q][0]) * S
                    act.wait_ge(score_full, SCORE[stage, i] + 1)
                    a.activation(hiddenT[:, q % 2, f, 0:n], score_bank[SCORE[stage, i] % RS][:, 0:n], ACT.Gelu, bias=col("fib", f))\
                        .then_inc(hidden_ready, 1)
                elif stage == "al":
                    act.wait_ge(best_ready, i + 1)
                    a.activation(ex[0:S, i:i + 1], best[0:S, i:i + 1], ACT.Exp, scale=-1.0).then_inc(exped, 1)

            expert, used = list(range(E)), None
            for j in range(TILES):
                if j == E:
                    used, more = further_tiles(act)
                    expert += more
                with when_used(act, used, j):
                    if j >= 2:
                        act.wait_ge(t_y_full, j - 1)
                    for half in range(2):
                        act.wait_ge(t_hid_full, 2 * j + half + 1)
                        for f in range(4):
                            b = consts[:, bass.ds(expert[j] * FC + COLS["moeb1"] + half * 4 + f, 1)]
                            last = a.activation(hidT[:, j % 2, half * 4 + f], bank[2 * (j % 2) + half][:, f * 128:(f + 1) * 128],
                                                ACT.Relu, bias=b)
                        last.then_inc(t_hid_ready, 1)

        @block.gpsimd
        def _(pool):
            g = nc.gpsimd
            g.memset(ident[:, :], 0.0).then_inc(pool_setup, 1)
            pool.wait_ge(pool_setup, 1)
            g.affine_select(out=ident[:, :], in_=ident[:, :], compare_op=ALU.not_equal, fill=1.0, base=0, pattern=[[-1, 128]],
                            channel_multiplier=1).then_inc(setup, 1)
            g.memset(values[:, 0, :, D:], 0.0).then_inc(setup, 1)
            g.memset(values[:, 1, :, D:], 0.0).then_inc(setup, 1)
            g.memset(vrows[:, :, D:], 0.0).then_inc(setup, 1)
            g.memset(scal[:, 0:1], EPS).then_inc(setup, 1)
            g.memset(scal[:, 1:2], -0.5).then_inc(setup, 1)
            g.memset(zero, 0.0).then_inc(setup, 1)
            g.memset(scal[:, 2:3], EPS / 4).then_inc(setup, 1)
            g.memset(lower[:, :], 1.0).then_inc(pool_setup, 1)
            g.memset(ones[:, :], 1.0).then_inc(setup, 1)
            pool.wait_ge(pool_setup, 2)
            g.affine_select(out=lower[:, :], in_=lower[:, :], compare_op=ALU.is_gt, fill=0.0, base=0, pattern=[[1, S]],
                            channel_multiplier=-1).then_inc(setup, 1)
            g.iota(rev[:, :], pattern=[[-1, E]], base=E, channel_multiplier=0,
                   allow_small_or_imprecise_dtypes=True).then_inc(setup, 1)
            g.iota(thr[:, :, :], pattern=[[0, E], [128, EXTRA]], base=128, channel_multiplier=0,
                   allow_small_or_imprecise_dtypes=True).then_inc(setup, 1)
            g.iota(tidx[:, :, :], pattern=[[1, EXTRA], [0, E - 1]], base=0, channel_multiplier=0,
                   allow_small_or_imprecise_dtypes=True).then_inc(setup, 1)
            for c, tiles in enumerate((E, EXTRA)):
                g.iota(spare[:, c], pattern=[[128, B]], base=tiles * 128, channel_multiplier=1,
                       allow_small_or_imprecise_dtypes=True).then_inc(setup, 1)
            g.iota(token[:, :], pattern=[[S, B]], base=0, channel_multiplier=1,
                   allow_small_or_imprecise_dtypes=True).then_inc(setup, 1)
            pool.wait_ge(setup, 16)
            g.tensor_copy(xrows[:, :, TOKEN], token[:, :]).then_inc(setup, 1)
            g.iota(zero[:, :, TOKEN], pattern=[[128, 2]], base=B * S, channel_multiplier=1,
                   allow_small_or_imprecise_dtypes=True).then_inc(setup, 1)
            vareps_count = [0]

            def inverse_deviation(k, rows, stats_sem, ready_sem, n, eps=0):
                pool.wait_ge(stats_sem, n + 1)
                g.tensor_tensor(vareps[0:rows, k % NR], meanvar[0:rows, k % NR, 1:2], scal[0:rows, eps:eps + 1], ALU.add).then_inc(vareps_ready, 1)
                vareps_count[0] += 1
                pool.wait_ge(vareps_ready, vareps_count[0])
                g.tensor_tensor(rstd[0:rows, k % NR], vareps[0:rows, k % NR], scal[0:rows, 1:2], ALU.pow).then_inc(ready_sem, 1)

            pool.wait_ge(xrow_in, 16)
            pool.wait_ge(b4_in, 16)
            for u in range(B):
                g.tensor_tensor(resid[0:S, u], resid[0:S, u], R["b4"], ALU.add).then_inc(resid_ready, 1)
            pool.wait_ge(rows_in, 16)
            g.tensor_tensor(R["cobe"], R["cobe"], R["sob"], ALU.add).then_inc(biases_added, 1)
            g.tensor_tensor(R["sobe"], R["sobe"], R["fob"], ALU.add).then_inc(biases_added, 1)
            pool.wait_ge(biases_added, 2)
            chain = 0
            for stage, i in STEPS:
                if stage in FINISHES:
                    inverse_deviation(OPENED[stage, i], S, stats_ready, rstd_ready, OPENED[stage, i])
                elif stage == "ab":
                    pool.wait_ge(norm_done, FINISHED[stage, i] + 1)
                    g.tensor_tensor(resid[0:S, i], x1[0:S, i], R["cob"], ALU.add).then_inc(resid_ready, 1)
                elif stage == "cq":
                    pool.wait_ge(out_full, OUT["ax", i] + 1)
                    pool.wait_ge(resid_ready, B + RESID["ab", i] + 1)
                    g.tensor_tensor(x1[0:S, i], x1[0:S, i], R["fobe"], ALU.add).then_inc(x1_biased, 1)
                elif stage == "zn":
                    pool.wait_ge(x5_stats, i + 1)
                    g.tensor_tensor(xrows[0:S, i, RSTD:RSTD + 1], xrows[0:S, i, RSTD:RSTD + 1], scal[0:S, 0:1], ALU.add)\
                        .then_inc(x5_vareps, 1)
                    pool.wait_ge(x5_vareps, i + 1)
                    g.tensor_tensor(xrows[0:S, i, RSTD:RSTD + 1], xrows[0:S, i, RSTD:RSTD + 1], scal[0:S, 1:2], ALU.pow)\
                        .then_inc(x5_rstd, 1)
                elif stage == "al":
                    if i == 0:
                        pool.wait_ge(zero_in, 16 * TILES)
                    pool.wait_ge(x5_rstd, i + 1)
                    pool.wait_ge(alphaed, i + 1)
                    pool.wait_ge(placed, i + 1)
                    g.indirect_dma_start(out=x_slots, out_offset=bass.IndirectOffsetOnAxis(ap=token_slot[0:S, i:i + 1], axis=0),
                                         in_=xrows[0:S, i], in_offset=None, bounds_check=(E + B) * 128 - 1).then_inc(scattered, 16)
                elif stage in ("cb", "sb"):
                    k = OPENED[stage[0] + "y", i]
                    gain, shift = ("cog", "cobe") if stage == "cb" else ("sog", "sobe")
                    pool.wait_ge(norm_done, FINISHED[stage, i] + 1)
                    g.tensor_tensor(resid[0:S, i], ybuf[0:S, k % NR], R[gain], ALU.mult).then_inc(pool_chain, 1)
                    chain += 1
                    pool.wait_ge(pool_chain, chain)
                    g.tensor_tensor(resid[0:S, i], resid[0:S, i], R[shift], ALU.add).then_inc(resid_ready, 1)

            pool.wait_ge(more_placed, 2)
            for b in range(B):
                g.indirect_dma_start(out=x_more, out_offset=bass.IndirectOffsetOnAxis(ap=token_slot2[0:S, b:b + 1], axis=0),
                                     in_=xrows[0:S, b], in_offset=None, bounds_check=(EXTRA + B) * 128 - 1).then_inc(more_scattered, 16)
            used, _ = further_tiles(pool, experts=False)
            for t in range(TILES + 1):
                if t < TILES:
                    with when_used(pool, used, t):
                        inverse_deviation(t, 128, t_stats, t_rstd, t, eps=2)
                j = t - 1
                if j >= 0:
                    with when_used(pool, used, j):
                        pool.wait_ge(t_y_ready, j + 1)
                        if j >= 2:
                            pool.wait_ge(y_sent[j % 2], 16 * (j // 2))
                        g.indirect_dma_start(out=out, out_offset=bass.IndirectOffsetOnAxis(ap=tile_token[:, j:j + 1], axis=0),
                                             in_=ys[:, j % 2], in_offset=None, bounds_check=B * S + 255).then_inc(y_sent[j % 2], 16)
            for j in range(E - 2, TILES):
                with when_used(pool, used, j):
                    pool.wait_ge(y_sent[j % 2], 16 * (j // 2 + 1))


def kernel(**inputs):
    import concourse.bacc as bacc
    from concourse.bass_utils import run_bass_kernel_spmd

    a = {n: np.ascontiguousarray(v) for n, v in inputs.items()}
    at, xa, mo = "L0_attn_", "L0_xattn_", "L0_ffn_"

    def chunks(w):
        return w.reshape(-1, 128, w.shape[-1]).transpose(1, 0, 2)

    def columns(v):
        return v.reshape(-1, 128).T

    x = a["x"]
    w = [a[at + n] for n in ("W1", "W2", "W3", "W4")]
    w += [a[xa + n + "_w"] for n in ("cq", "ck", "cv", "co", "sq", "sk", "sv", "so")]
    cols = [a[at + n] for n in ("b1", "b2", "b3")]
    cols += [a[xa + n] for n in ("cq_b", "ck_b", "cv_b", "sq_b", "sk_b", "sv_b", "fi_b", "co_g", "co_be", "so_g", "so_be")]
    cols += [a[mo + n] for n in ("gamma", "beta", "b1")]
    cent = chunks(a[mo + "centroids"].T).reshape(128, -1)
    rows = [a[at + "b4"]] + [a[xa + n] for n in ("co_b", "co_g", "co_be", "so_b", "so_g", "so_be", "fo_b", "fo_g", "fo_be")]
    moe1 = a[mo + "W1"].transpose(0, 2, 1).reshape(E, C, 128, F).transpose(0, 2, 1, 3).reshape(E, 128, C * F)
    moe2 = a[mo + "W2"].transpose(0, 2, 1).reshape(E, FC, 128, D).transpose(0, 2, 1, 3).reshape(E, 128, FC * D)
    arrays = {
        "xT": x.reshape(B, S, C, 128).transpose(3, 0, 2, 1),
        "xrow": x.transpose(1, 0, 2),
        "ctxT": a["ctx_1024"].reshape(B, KX, C, 128).transpose(0, 3, 2, 1),
        "mask": a["mask_Bx1x1xS2_ff0"].reshape(B, KX),
        "weights": np.stack([chunks(m) for m in w], axis=1),
        "fi": chunks(a[xa + "fi_w"]),
        "fo": chunks(a[xa + "fo_w"]),
        "cols": np.concatenate([columns(c) for c in cols] + [cent], axis=1),
        "rows": np.concatenate(rows).reshape(1, -1),
        "b2rows": a[mo + "b2"].reshape(1, E * D),
        "moe": np.concatenate([moe1, moe2], axis=2),
    }
    arrays = {n: np.ascontiguousarray(v) for n, v in arrays.items()}
    nc = bacc.Bacc("TRN2", target_bir_lowering=False, num_devices=1)
    ap = {n: nc.dram_tensor(n, v.shape, mybir.dt.from_np(v.dtype), kind="ExternalInput").ap() for n, v in arrays.items()}
    x_slots = nc.dram_tensor("x_slots", ((E + B) * 128, XW), F32, kind="Internal").ap()
    x_more = nc.dram_tensor("x_more", ((EXTRA + B) * 128, XW), F32, kind="Internal").ap()
    out = nc.dram_tensor("out", (B * S + 256, D), F32, kind="ExternalOutput").ap()
    decoder_layer(nc, **ap, x_slots=x_slots, x_more=x_more, out=out)
    r = run_bass_kernel_spmd(nc, [arrays], core_ids=[0])
    return r.results[0]["out"][0:B * S].reshape(B, S, D)
```
